# Optimizing a Trainium2 kernel written in Bass

```python
import numpy as np
import jax
import jax.numpy as jnp

def _softmax(x, axis=-1):
    return jax.nn.softmax(x, axis=axis)

def _gelu(x):
    return jax.nn.gelu(x, approximate=True)

def _silu(x):
    return jax.nn.silu(x)

def _sigmoid(x):
    return jax.nn.sigmoid(x)

def _layernorm(x, axis=-1, eps=1e-05):
    m = jnp.mean(x, axis=axis, keepdims=True)
    v = jnp.var(x, axis=axis, keepdims=True)
    return (x - m) / jnp.sqrt(v + eps)

def _scatter_add(tgt, idx, src, axis=0):
    return tgt.at[idx].add(src)

def _segment_sum(src, seg, n):
    return jax.ops.segment_sum(src, seg, n)
kernel_name = 'mk_gnn_resnorm_d4_gnn_r64_9af2a5'

def setup_inputs(seed: int=0):
    np.random.seed(seed)
    _w = jnp.asarray

    def _rec_inputs():
        import jax
        import jax.numpy as jnp
        _gk = jax.random.key(seed)
        x = -6.415e-05 + 1 * jax.random.normal(jax.random.fold_in(_gk, 1), (10000, 512), jnp.float32)
        src = jax.random.randint(jax.random.fold_in(_gk, 2), (2500,), 0, 10000, jnp.int32)
        dst = jax.random.randint(jax.random.fold_in(_gk, 3), (2500,), 0, 10000, jnp.int32)
        _o = jnp.argsort(dst, stable=True)
        src = src[_o]
        dst = dst[_o]
        edge_attr_20 = 0.000389844 + 1.00025 * jax.random.normal(jax.random.fold_in(_gk, 13), (2500, 20), jnp.float32)
        edge_attr_4 = -0.00185629 + 0.998788 * jax.random.normal(jax.random.fold_in(_gk, 14), (2500, 4), jnp.float32)
        edge_attr_64 = 0.000279952 + 1.00013 * jax.random.normal(jax.random.fold_in(_gk, 15), (2500, 64), jnp.float32)
        edge_weight = jax.random.uniform(jax.random.fold_in(_gk, 17), (2500,), jnp.float32, 0.0, 0.999993)
        return (x, src, dst, edge_attr_20, edge_attr_4, edge_attr_64, edge_weight)
    x, src, dst, edge_attr_20, edge_attr_4, edge_attr_64, edge_weight = _rec_inputs()

    def _L0_gnn_setup():
        import jax, jax.numpy as jnp
        import numpy as np
        N_NODES = 20000
        N_EDGES = 5000
        HIDDEN = 512
        EDGE_DIM = 64
        LN_EPS = 1e-05

        def mish(x):
            return x * jnp.tanh(jax.nn.softplus(x))
        key = jax.random.key(seed)
        ks = jax.random.split(key, 8)
        s = lambda fan_in: 1.0 / np.sqrt(fan_in)
        return {'x': jax.random.normal(ks[0], (N_NODES, HIDDEN), dtype=jnp.float32), 'edge_index': jax.random.randint(ks[1], (2, N_EDGES), 0, N_NODES, dtype=jnp.int64), 'edge_attr': jax.random.normal(ks[2], (N_EDGES, EDGE_DIM), dtype=jnp.float32), 'W1': jax.random.normal(ks[3], (2 * HIDDEN + EDGE_DIM, HIDDEN), dtype=jnp.float32) * s(2 * HIDDEN + EDGE_DIM), 'b1': jnp.zeros((HIDDEN,), dtype=jnp.float32), 'W2': jax.random.normal(ks[4], (HIDDEN, HIDDEN), dtype=jnp.float32) * s(HIDDEN), 'b2': jnp.zeros((HIDDEN,), dtype=jnp.float32), 'W3': jax.random.normal(ks[5], (2 * HIDDEN, HIDDEN), dtype=jnp.float32) * s(2 * HIDDEN), 'b3': jnp.zeros((HIDDEN,), dtype=jnp.float32), 'W4': jax.random.normal(ks[6], (HIDDEN, HIDDEN), dtype=jnp.float32) * s(HIDDEN), 'b4': jnp.zeros((HIDDEN,), dtype=jnp.float32), 'gamma': jnp.ones((HIDDEN,), dtype=jnp.float32), 'beta': jnp.zeros((HIDDEN,), dtype=jnp.float32)}
    _L0_gnn_all = _L0_gnn_setup()
    _L0_gnn_in = {k: v for k, v in _L0_gnn_all.items() if k in ('W1', 'b1', 'W2', 'b2', 'W3', 'b3', 'W4', 'b4', 'gamma', 'beta')}
    del _L0_gnn_all

    def _L1_gnn_setup():
        import jax, jax.numpy as jnp
        import numpy as np
        N, D, E = (50000, 512, 6250)
        EPS = 1e-05
        SLOPE = 0.01
        key = jax.random.key(seed)
        k1, k2, k3, k4 = jax.random.split(key, 4)
        x = jax.random.normal(k1, (N, D), dtype=jnp.float32)
        edge_index = jax.random.randint(k2, (2, E), 0, N, dtype=jnp.int64)
        s = 1.0 / np.sqrt(D)
        W_l = jax.random.normal(k3, (D, D), dtype=jnp.float32) * s
        b_l = jnp.zeros((D,), dtype=jnp.float32)
        W_r = jax.random.normal(k4, (D, D), dtype=jnp.float32) * s
        gamma = jnp.ones((D,), dtype=jnp.float32)
        beta = jnp.zeros((D,), dtype=jnp.float32)
        return {'x': x, 'edge_index': edge_index, 'W_l': W_l, 'b_l': b_l, 'W_r': W_r, 'gamma': gamma, 'beta': beta}
    _L1_gnn_all = _L1_gnn_setup()
    _L1_gnn_in = {k: v for k, v in _L1_gnn_all.items() if k in ('W_l', 'b_l', 'W_r', 'gamma', 'beta')}
    del _L1_gnn_all

    def _L2_gnn_setup():
        import jax, jax.numpy as jnp
        import numpy as np
        import math
        B = 128
        F = 32
        R = 20
        N = 256
        E = 4096
        LOG2 = 0.6931471805599453
        IS2 = 1.0 / math.sqrt(2.0)
        IS3 = 1.0 / math.sqrt(3.0)
        IS6 = 1.0 / math.sqrt(6.0)

        def ssp(x):
            return jax.nn.softplus(x) - LOG2
        key = jax.random.key(seed)
        ks = jax.random.split(key, 14)
        return dict(x=jax.random.normal(ks[0], (N, 4 * B), jnp.float32), idx_i=jax.random.randint(ks[1], (E,), 0, N), idx_j=jax.random.randint(ks[2], (E,), 0, N), f_ij=jax.random.normal(ks[3], (E, R), jnp.float32), rcut_ij=jax.random.uniform(ks[4], (E,), jnp.float32), Yr_ij=jax.random.normal(ks[5], (E, 4), jnp.float32), w_in2f_s=jax.random.normal(ks[6], (B, F), jnp.float32), w_in2f_v=jax.random.normal(ks[7], (B, F), jnp.float32), W1=jax.random.normal(ks[8], (R, F), jnp.float32) / math.sqrt(R), b1=jnp.zeros((F,), jnp.float32), W2=jax.random.normal(ks[9], (F, 6 * F), jnp.float32) / math.sqrt(F), b2=jnp.zeros((6 * F,), jnp.float32), w_f2o1_s=jax.random.normal(ks[10], (2 * F, B), jnp.float32), w_f2o1_v=jax.random.normal(ks[11], (2 * F, B), jnp.float32), w_f2o2_s=jax.random.normal(ks[12], (B, B), jnp.float32), w_f2o2_v=jax.random.normal(ks[13], (B, B), jnp.float32))
    _L2_gnn_all = _L2_gnn_setup()
    _L2_gnn_in = {k: v for k, v in _L2_gnn_all.items() if k in ('w_in2f_s', 'w_in2f_v', 'W1', 'b1', 'W2', 'b2', 'w_f2o1_s', 'w_f2o1_v', 'w_f2o2_s', 'w_f2o2_v')}
    del _L2_gnn_all

    def _L3_gnn_setup():
        import jax, jax.numpy as jnp
        import numpy as np
        N = 20000
        E = 250000
        B = 128
        Fin = 512
        Fqk = 512
        Fv = 512
        H = 8
        key = jax.random.key(seed)
        k1, k2, k3, k4 = jax.random.split(key, 4)
        x = jax.random.normal(k1, (N, Fin), dtype=jnp.float32)
        batch = jnp.sort(jax.random.randint(k2, (N,), 0, B)).astype(jnp.int32)
        ei = jax.random.randint(k3, (2, E), 0, N).astype(jnp.int32)
        W = jax.random.normal(k4, (Fin, 2 * Fqk + Fv), dtype=jnp.float32) / np.sqrt(Fin).astype(np.float32)
        return {'x': x, 'batch': batch, 'ei': ei, 'W': W}
    _L3_gnn_all = _L3_gnn_setup()
    _L3_gnn_in = {k: v for k, v in _L3_gnn_all.items() if k in ('W',)}
    del _L3_gnn_all
    return {'x': x, 'src': src, 'dst': dst, 'edge_attr_20': edge_attr_20, 'edge_attr_4': edge_attr_4, 'edge_attr_64': edge_attr_64, 'edge_weight': edge_weight, 'L0_gnn_W1': _L0_gnn_in['W1'], 'L0_gnn_b1': _L0_gnn_in['b1'], 'L0_gnn_W2': _L0_gnn_in['W2'], 'L0_gnn_b2': _L0_gnn_in['b2'], 'L0_gnn_W3': _L0_gnn_in['W3'], 'L0_gnn_b3': _L0_gnn_in['b3'], 'L0_gnn_W4': _L0_gnn_in['W4'], 'L0_gnn_b4': _L0_gnn_in['b4'], 'L0_gnn_gamma': _L0_gnn_in['gamma'], 'L0_gnn_beta': _L0_gnn_in['beta'], 'L1_gnn_W_l': _L1_gnn_in['W_l'], 'L1_gnn_b_l': _L1_gnn_in['b_l'], 'L1_gnn_W_r': _L1_gnn_in['W_r'], 'L1_gnn_gamma': _L1_gnn_in['gamma'], 'L1_gnn_beta': _L1_gnn_in['beta'], 'L2_gnn_w_in2f_s': _L2_gnn_in['w_in2f_s'], 'L2_gnn_w_in2f_v': _L2_gnn_in['w_in2f_v'], 'L2_gnn_W1': _L2_gnn_in['W1'], 'L2_gnn_b1': _L2_gnn_in['b1'], 'L2_gnn_W2': _L2_gnn_in['W2'], 'L2_gnn_b2': _L2_gnn_in['b2'], 'L2_gnn_w_f2o1_s': _L2_gnn_in['w_f2o1_s'], 'L2_gnn_w_f2o1_v': _L2_gnn_in['w_f2o1_v'], 'L2_gnn_w_f2o2_s': _L2_gnn_in['w_f2o2_s'], 'L2_gnn_w_f2o2_v': _L2_gnn_in['w_f2o2_v'], 'L3_gnn_W': _L3_gnn_in['W']}

def reference(x, src, dst, edge_attr_20, edge_attr_4, edge_attr_64, edge_weight, L0_gnn_W1, L0_gnn_b1, L0_gnn_W2, L0_gnn_b2, L0_gnn_W3, L0_gnn_b3, L0_gnn_W4, L0_gnn_b4, L0_gnn_gamma, L0_gnn_beta, L1_gnn_W_l, L1_gnn_b_l, L1_gnn_W_r, L1_gnn_gamma, L1_gnn_beta, L2_gnn_w_in2f_s, L2_gnn_w_in2f_v, L2_gnn_W1, L2_gnn_b1, L2_gnn_W2, L2_gnn_b2, L2_gnn_w_f2o1_s, L2_gnn_w_f2o1_v, L2_gnn_w_f2o2_s, L2_gnn_w_f2o2_v, L3_gnn_W):
    import jax
    import jax.numpy as jnp

    def _L0_gnn_ref(x, edge_index, edge_attr, W1, b1, W2, b2, W3, b3, W4, b4, gamma, beta):
        import jax, jax.numpy as jnp
        import numpy as np
        N_NODES = 20000
        N_EDGES = 5000
        HIDDEN = 512
        EDGE_DIM = 64
        LN_EPS = 1e-05

        def mish(x):
            return x * jnp.tanh(jax.nn.softplus(x))
        src, dst = (edge_index[0], edge_index[1])
        edge_feat = jnp.concatenate([x[src], x[dst], edge_attr], axis=-1)
        h = mish(edge_feat @ W1 + b1)
        messages = mish(h @ W2 + b2)
        agg = jax.ops.segment_sum(messages, dst, num_segments=x.shape[0])
        u = mish(jnp.concatenate([x, agg], axis=-1) @ W3 + b3)
        out = u @ W4 + b4
        y = x + out
        mu = jnp.mean(y, axis=-1, keepdims=True)
        var = jnp.mean(jnp.square(y - mu), axis=-1, keepdims=True)
        return (y - mu) * jax.lax.rsqrt(var + LN_EPS) * gamma + beta

    def _L1_gnn_ref(x, edge_index, W_l, b_l, W_r, gamma, beta):
        import jax, jax.numpy as jnp
        import numpy as np
        N, D, E = (50000, 512, 6250)
        EPS = 1e-05
        SLOPE = 0.01
        src, dst = (edge_index[0], edge_index[1])
        n = x.shape[0]
        summed = jax.ops.segment_sum(x[src], dst, num_segments=n)
        deg = jax.ops.segment_sum(jnp.ones((src.shape[0],), x.dtype), dst, num_segments=n)
        agg = summed / jnp.maximum(deg, 1.0)[:, None]
        out = agg @ W_l + b_l + x @ W_r
        mean = out.mean(axis=0)
        var = out.var(axis=0)
        out = (out - mean) * jax.lax.rsqrt(var + EPS) * gamma + beta
        out = jnp.where(out >= 0, out, SLOPE * out)
        out = out + x
        return out

    def _L2_gnn_ref(x, idx_i, idx_j, f_ij, rcut_ij, Yr_ij, w_in2f_s, w_in2f_v, W1, b1, W2, b2, w_f2o1_s, w_f2o1_v, w_f2o2_s, w_f2o2_v):
        import jax, jax.numpy as jnp
        import numpy as np
        import math
        B = 128
        F = 32
        R = 20
        N = 256
        E = 4096
        LOG2 = 0.6931471805599453
        IS2 = 1.0 / math.sqrt(2.0)
        IS3 = 1.0 / math.sqrt(3.0)
        IS6 = 1.0 / math.sqrt(6.0)

        def ssp(x):
            return jax.nn.softplus(x) - LOG2
        n = x.shape[0]
        xs = x[:, :B]
        xv = x[:, B:].reshape(n, B, 3)
        hs = xs @ w_in2f_s / math.sqrt(B)
        hv = jnp.einsum('nbc,bf->nfc', xv, w_in2f_v) / math.sqrt(B)
        s = hs[idx_j]
        v = hv[idx_j]
        ys = Yr_ij[:, 0]
        yv = Yr_ij[:, 1:4]
        t_s1 = s * ys[:, None]
        t_s2 = jnp.einsum('efc,ec->ef', v, yv) * IS3
        t_v1 = s[:, :, None] * yv[:, None, :]
        t_v2 = v * ys[:, None, None]
        t_pv = jnp.cross(v, yv[:, None, :]) * IS2
        ax, ay, az = (v[..., 0], v[..., 1], v[..., 2])
        bx, by, bz = (yv[:, None, 0:1], yv[:, None, 1:2], yv[:, None, 2:3])
        bx, by, bz = (bx[..., 0], by[..., 0], bz[..., 0])
        t_q = jnp.stack([(ax * by + ay * bx) * IS2, (ay * bz + az * by) * IS2, (2.0 * az * bz - ax * bx - ay * by) * IS6, (ax * bz + az * bx) * IS2, (ax * bx - ay * by) * IS2], axis=-1)
        h = ssp(f_ij @ W1 + b1)
        Wij = (h @ W2 + b2) * rcut_ij[:, None]
        Wf = Wij.reshape(-1, F, 6)
        edge = jnp.concatenate([(t_s1 * Wf[..., 0])[..., None], (t_s2 * Wf[..., 1])[..., None], t_v1 * Wf[..., 2:3], t_v2 * Wf[..., 3:4], t_pv * Wf[..., 4:5], t_q * Wf[..., 5:6]], axis=-1)
        agg = jax.ops.segment_sum(edge.reshape(edge.shape[0], -1), idx_i, num_segments=n).reshape(n, F, 16)
        s_in = jnp.concatenate([agg[..., 0], agg[..., 1]], axis=1)
        v_in = jnp.concatenate([agg[..., 2:5], agg[..., 5:8]], axis=1)
        os1 = s_in @ w_f2o1_s / math.sqrt(2 * F)
        ov1 = jnp.einsum('nmc,mb->nbc', v_in, w_f2o1_v) / math.sqrt(2 * F)
        os1 = ssp(os1)
        os2 = os1 @ w_f2o2_s / math.sqrt(B)
        ov2 = jnp.einsum('nbc,bd->ndc', ov1, w_f2o2_v) / math.sqrt(B)
        return jnp.concatenate([os2, ov2.reshape(n, -1)], axis=-1)

    def _L3_gnn_ref(x, batch, ei, W):
        import jax, jax.numpy as jnp
        import numpy as np
        N = 20000
        E = 250000
        B = 128
        Fin = 512
        Fqk = 512
        Fv = 512
        H = 8
        src, dest = (ei[0], ei[1])
        n = x.shape[0]
        Fh = Fqk // H
        Fhv = Fv // H
        scaling = float(Fh) ** (-0.5)
        qkv = x @ W
        q, k, v = jnp.split(qkv, [Fqk, 2 * Fqk], axis=-1)
        q = (q * scaling).reshape(n, H, Fh)
        k = k.reshape(n, H, Fh)
        v = v.reshape(n, H, Fhv)
        qs = q[src]
        ks = k[dest]
        vs = v[dest]
        aw = jnp.einsum('ehf,ehf->eh', qs, ks)
        m = jax.ops.segment_max(aw, src, num_segments=n)
        e = jnp.exp(aw - m[src])
        denom = jax.ops.segment_sum(e, src, num_segments=n)
        alpha = e / denom[src]
        out = jax.ops.segment_sum(alpha[:, :, None] * vs, src, num_segments=n)
        return out.reshape(n, Fv)
    edge_index = jnp.stack([src, dst])
    batch0 = jnp.zeros((10000,), jnp.int32)
    x = _layernorm(x + _L0_gnn_ref(x, edge_index, edge_attr_64, L0_gnn_W1, L0_gnn_b1, L0_gnn_W2, L0_gnn_b2, L0_gnn_W3, L0_gnn_b3, L0_gnn_W4, L0_gnn_b4, L0_gnn_gamma, L0_gnn_beta), axis=-1)
    x = _layernorm(x + _L1_gnn_ref(x, edge_index, L1_gnn_W_l, L1_gnn_b_l, L1_gnn_W_r, L1_gnn_gamma, L1_gnn_beta), axis=-1)
    x = _layernorm(x + _L2_gnn_ref(x, src, dst, edge_attr_20, edge_weight, edge_attr_4, L2_gnn_w_in2f_s, L2_gnn_w_in2f_v, L2_gnn_W1, L2_gnn_b1, L2_gnn_W2, L2_gnn_b2, L2_gnn_w_f2o1_s, L2_gnn_w_f2o1_v, L2_gnn_w_f2o2_s, L2_gnn_w_f2o2_v), axis=-1)
    x = _layernorm(x + _L3_gnn_ref(x, batch0, edge_index, L3_gnn_W), axis=-1)
    return x

_drawn_inputs = setup_inputs


def setup_inputs(seed=0):
    import zlib

    import numpy as np

    out = dict(_drawn_inputs(seed))
    spreads = {'L0_gnn_b1': (0.0, 0.8),
     'L0_gnn_b2': (0.0, 0.793),
     'L0_gnn_b3': (0.0, 0.1),
     'L0_gnn_b4': (0.0, 0.1),
     'L0_gnn_gamma': (1.0, 0.2),
     'L0_gnn_beta': (0.0, 0.1),
     'L1_gnn_b_l': (0.0, 0.8),
     'L1_gnn_gamma': (1.0, 0.2),
     'L1_gnn_beta': (0.0, 0.1),
     'L2_gnn_b1': (0.0, 0.8),
     'L2_gnn_b2': (0.0, 0.442)}
    factors = {'edge_attr_64': 3.776}
    for name, (base, spread) in spreads.items():
        noise = np.random.default_rng([zlib.crc32(name.encode()), seed]).standard_normal(out[name].shape)
        drawn = base * np.exp(spread * noise) if base else spread * noise
        out[name] = jnp.asarray(drawn.astype(out[name].dtype))
    for name, factor in factors.items():
        out[name] = (out[name] * factor).astype(out[name].dtype)
    return out
```

```python
from contextlib import ExitStack, contextmanager

import numpy as np

import concourse.bass as bass
from concourse import mybir

F32 = mybir.dt.float32
I32 = mybir.dt.int32
ALU = mybir.AluOpType
ACT = mybir.ActivationFunctionType
AX_X = mybir.AxisListType.X

P = 128
N = 10000
D = 512
KB = D // P
E = 2500
EDGE_TILES = -(-E // P)
LAST_START = E - P
OVERLAP = (EDGE_TILES - 1) * P - LAST_START
ROWS = 10240
NODE_TILES = ROWS // P
LAST_VALID_TILE = N // P
GROUP = 4
GROUPS = EDGE_TILES // GROUP
EDGE64, EDGE20 = 64, 20
F = 32
B = 128
HEADS = 8
HD = D // HEADS
ATT = D + HEADS
LN_EPS = 1e-5
LOG2 = 0.6931471805599453
BIG = 3.0e38


class Shared:
    pass


def at_rows(index_column):
    return bass.IndirectOffsetOnAxis(ap=index_column, axis=0)


def setup_phase(nc, k):
    with phase(nc, "i_") as (sb, ps, sem), ExitStack() as ctx:

        row_i = sb("row_i", [P, 2, EDGE_TILES * P], I32)
        row_f = sb("row_f", [P, 2, EDGE_TILES * P])
        masked = sb("masked", [P, EDGE_TILES * P])
        col_i = sb("col_i", [P, 2, EDGE_TILES], I32)
        col_f = sb("col_f", [P, 2, EDGE_TILES])
        repeated = sb("repeated", [P, 2, EDGE_TILES])
        unique_f = sb("unique_f", [P, 2, EDGE_TILES])
        degree = sb("degree", [P, EDGE_TILES])
        earlier = sb("earlier", [P, P])
        dummy_i = sb("dummy_i", [P, 1], I32)
        dummy_f = sb("dummy_f", [P, 1])
        zeros = sb("zeros", [P, ATT])
        lowest = sb("lowest", [P, NODE_TILES * HEADS])
        b3_row = sb("b3_row", [P, D])
        f20T = sb("f20T", [EDGE20, EDGE_TILES * P])
        w1e = sb("w1e", [EDGE20, F])
        b1e = sb("b1e", [F, 1])
        w2e = sb("w2e", [F + 1, 6 * F])
        y4 = sb("y4", [P, EDGE_TILES, 4])
        cut = sb("cut", [P, EDGE_TILES])
        mag = sb("mag", [F, D])
        mag2 = sb("mag2", [F, D])
        mag3 = sb("mag3", [F, D])
        pos = sb("pos", [F, D])
        hT = sb("hT", [F + 1, EDGE_TILES * P])
        wf = sb("wf", [P, 4, F])
        p_h = [ps(f"p_h{i}", [F, D]) for i in range(2)]
        p_w = [ps(f"p_w{i}", [P, D]) for i in range(2)]

        rows_in, cols_in, b3_in, filt_in, weights_in = (
            sem("rows_in"), sem("cols_in"), sem("b3_in"), sem("filt_in"), sem("weights_in"))
        const_done, tables_set, v = sem("const_done"), sem("tables_set"), sem("setup_v")
        pre_h, act_h, pos_done, h_done, pre_w = (
            sem("pre_h"), sem("act_h"), sem("pos_done"), sem("h_done"), sem("pre_w"))
        z_src = sem("z_src")

        block = ctx.enter_context(nc.Block())

        @block.sync
        def _(sp):
            sp.dma_start(col_i[:, 0, :], k.src_cols).then_inc(cols_in, 16)
            sp.dma_start(col_i[:, 1, :], k.dst_cols).then_inc(cols_in, 16)
            sp.dma_start(f20T[:, :], k.f20T).then_inc(filt_in, 16)
            sp.dma_start(w1e[:, :], k.L2_W1).then_inc(filt_in, 16)
            sp.dma_start(b1e[:, :], k.L2_b1.rearrange("(f a) -> f a", a=1)).then_inc(filt_in, 16)
            sp.dma_start(w2e[0:F, :], k.L2_W2).then_inc(filt_in, 16)
            sp.dma_start(w2e[F:F + 1, :], k.L2_b2.rearrange("(a f) -> a f", a=1)).then_inc(filt_in, 16)
            sp.dma_start(y4[:, :, :], k.y4).then_inc(filt_in, 16)
            sp.dma_start(cut[:, :], k.cut).then_inc(filt_in, 16)
            sp.dma_start(row_i[:, 0, :], k.src_rows.to_broadcast([P, EDGE_TILES * P])).then_inc(rows_in, 16)
            sp.dma_start(row_i[:, 1, :], k.dst_rows.to_broadcast([P, EDGE_TILES * P])).then_inc(rows_in, 16)
            sp.dma_start(b3_row[:, :], k.L0_b3.rearrange("(a n) -> a n", a=1).to_broadcast([P, D])).then_inc(b3_in, 16)
            sp.wait_ge(b3_in, 16)
            sp.dma_start(k.sum0.rearrange("(p n) d -> p n d", p=P),
                         b3_row[:, :].rearrange("p (a d) -> p a d", a=1).to_broadcast([P, NODE_TILES, D])
                         ).then_inc(tables_set, 16)
            sp.wait_ge(cols_in, 32)
            sp.wait_ge(filt_in, 16 * 7)
            sp.wait_ge(rows_in, 32)
            sp.wait_ge(tables_set, 64)

        @block.gpsimd
        def _(pool):
            pool.memset(k.ones[:, :], 1.0).then_inc(const_done, 1)
            pool.memset(k.ident[:, :], 0.0).then_inc(const_done, 1)
            pool.memset(k.minus_half[:, :], -0.5).then_inc(k.half_set, 1)
            pool.memset(zeros[:, :], 0.0).then_inc(z_src, 1)
            pool.memset(lowest[:, :], -BIG).then_inc(z_src, 1)
            pool.iota(dummy_i[:, :], [[0, 1]], base=N, channel_multiplier=1).then_inc(const_done, 1)
            pool.wait_ge(const_done, 3)
            pool.affine_select(out=k.ident[:, :], in_=k.ident[:, :], compare_op=ALU.not_equal, fill=1.0,
                               base=0, pattern=[[-1, P]], channel_multiplier=1).then_inc(const_done, 1)
            pool.affine_select(out=earlier[:, :], in_=k.ones[:, :], compare_op=ALU.is_gt, fill=0.0,
                               base=0, pattern=[[-1, P]], channel_multiplier=1).then_inc(const_done, 1)

        @block.scalar
        def _(act):
            act.wait_ge(z_src, 2)
            act.dma_start(k.sum2.rearrange("(p n) d -> p n d", p=P),
                          zeros[:, 0:8 * F].rearrange("p (a d) -> p a d", a=1).to_broadcast([P, NODE_TILES, 8 * F])
                          ).then_inc(tables_set, 16)
            act.dma_start(k.sum3.rearrange("(p n) d -> p n d", p=P),
                          zeros[:, :].rearrange("p (a d) -> p a d", a=1).to_broadcast([P, NODE_TILES, ATT])
                          ).then_inc(tables_set, 16)
            act.dma_start(k.max3.rearrange("(p n) d -> p (n d)", p=P), lowest[:, :]).then_inc(tables_set, 16)
            act.wait_ge(filt_in, 16 * 7)
            steps = 0
            for g in range(GROUPS):
                act.wait_ge(pre_h, g + 1)
                if g:
                    act.wait_ge(h_done, g)
                act.wait_ge(pos_done, g + 1)
                for out, in_, func, bias, scale in (
                        (mag, p_h[g % 2], ACT.Abs, b1e[:, 0:1], 1.0),
                        (mag2, mag, ACT.Exp, 0.0, -1.0),
                        (mag3, mag2, ACT.Ln, 1.0, 1.0)):
                    act.activation(out[:, :], in_[:, :], func, bias=bias, scale=scale).then_inc(act_h, 1)
                    steps += 1
                    act.wait_ge(act_h, steps)

        @block.tensor
        def _(pe):
            pe.wait_ge(filt_in, 16 * 7)
            for g in range(GROUPS):
                if g >= 2:
                    pe.wait_ge(act_h, 3 * (g - 2) + 1)
                    pe.wait_ge(pos_done, g - 1)
                pe.matmul(p_h[g % 2][:, :], w1e[:, :], f20T[:, g * D:(g + 1) * D],
                          start=True, stop=True).then_inc(pre_h, 1)
            pe.wait_ge(const_done, 5)
            for t in range(EDGE_TILES):
                pe.wait_ge(v, 1)
                pe.wait_ge(h_done, t // GROUP + 1)
                if t >= 2:
                    pe.wait_ge(k.filters_done, t - 1)
                pe.matmul(p_w[t % 2][:, 0:4 * F].rearrange("p (c f) -> p c f", c=4),
                          hT[:, t * P:(t + 1) * P],
                          w2e[:, :].rearrange("k (f c) -> k c f", c=6)[:, 0:4, :],
                          start=True, stop=True).then_inc(pre_w, 1)

        @block.vector
        def _(dve):
            n = [0]

            def step(ins):
                n[0] += 1
                ins.then_inc(v, 1)
                dve.wait_ge(v, n[0])

            step(nc.vector.memset(hT[F:F + 1, :], 1.0))
            dve.wait_ge(cols_in, 32)
            dve.wait_ge(const_done, 5)
            step(nc.vector.tensor_copy(col_f[:, :, :], col_i[:, :, :]))
            step(nc.vector.tensor_copy(dummy_f[:, :], dummy_i[:, :]))
            for g in range(GROUPS):
                dve.wait_ge(pre_h, g + 1)
                nc.vector.tensor_scalar(pos[:, :], p_h[g % 2][:, :], b1e[:, 0:1], 0.0, ALU.add, ALU.max
                                        ).then_inc(pos_done, 1)
                dve.wait_ge(pos_done, g + 1)
                dve.wait_ge(act_h, 3 * g + 3)
                nc.vector.scalar_tensor_tensor(out=hT[0:F, g * D:(g + 1) * D], in0=mag3[:, :], scalar=-LOG2,
                                               in1=pos[:, :], op0=ALU.add, op1=ALU.add).then_inc(h_done, 1)
                dve.wait_ge(h_done, g + 1)
            dve.wait_ge(rows_in, 32)
            step(nc.vector.tensor_copy(row_f[:, :, :], row_i[:, :, :]))
            for s, same in ((0, k.same_src), (1, k.same_dst)):
                for t in range(EDGE_TILES):
                    last = nc.vector.tensor_scalar(same[:, t, :], row_f[:, s, t * P:(t + 1) * P],
                                                   col_f[:, s, t:t + 1], None, ALU.is_equal)
                step(last)
                m3 = masked[:, :].rearrange("p (t e) -> p t e", t=EDGE_TILES)
                step(nc.vector.tensor_tensor(
                    m3, same[:, :, :],
                    earlier[:, :].rearrange("p (a e) -> p a e", a=1).to_broadcast([P, EDGE_TILES, P]), ALU.mult))
                step(nc.vector.tensor_reduce(repeated[:, s, :], m3, AX_X, ALU.max))
                step(nc.vector.tensor_scalar(unique_f[:, s, :], col_f[:, s, :], dummy_f[:, 0:1], -1.0,
                                             ALU.subtract, ALU.mult))
                step(nc.vector.tensor_tensor(unique_f[:, s, :], unique_f[:, s, :], repeated[:, s, :], ALU.mult))
                step(nc.vector.tensor_tensor(unique_f[:, s, :], unique_f[:, s, :], col_f[:, s, :], ALU.add))
                step(nc.vector.tensor_copy(k.unique[:, s, :], unique_f[:, s, :]))
                step(nc.vector.tensor_copy(k.index[:, s, :], col_i[:, s, :]))
                if s == 0:
                    step(nc.vector.tensor_copy(k.same_src_last[:, :], same[:, EDGE_TILES - 1, :]))
                step(nc.vector.memset(same[0:OVERLAP, EDGE_TILES - 1, :], 0.0))
            step(nc.vector.memset(row_f[:, 1, (EDGE_TILES - 1) * P:(EDGE_TILES - 1) * P + OVERLAP], -1.0))
            for t in range(EDGE_TILES):
                step(nc.vector.tensor_scalar(masked[:, :], row_f[:, 1, :], col_f[:, 1, t:t + 1], None,
                                             ALU.is_equal, ALU.add, accum_out=degree[:, t:t + 1]))
            step(nc.vector.reciprocal(k.inv_degree[:, :], degree[:, :]))
            step(nc.vector.tensor_copy(k.share[:, :], k.inv_degree[:, :]))
            step(nc.vector.memset(k.share[0:OVERLAP, EDGE_TILES - 1:EDGE_TILES], 0.0))
            for t in range(EDGE_TILES):
                dve.wait_ge(pre_w, t + 1)
                step(nc.vector.tensor_scalar(wf[:, :, :], p_w[t % 2][:, 0:4 * F].rearrange("p (c f) -> p c f", c=4),
                                             cut[:, t:t + 1], float(B) ** -0.5, ALU.mult, ALU.mult))
                a = k.filters[:, t, :, :]
                for c in range(4):
                    nc.vector.tensor_scalar(a[:, c, :], wf[:, 0 if c == 0 else 2, :], y4[:, t, c:c + 1], None, ALU.mult)
                for c in range(1, 4):
                    nc.vector.tensor_scalar(a[:, 3 + c, :], wf[:, 1, :], y4[:, t, c:c + 1], 3.0 ** -0.5,
                                            ALU.mult, ALU.mult)
                nc.vector.tensor_scalar(a[:, 7, :], wf[:, 3, :], y4[:, t, 0:1], None, ALU.mult
                                        ).then_inc(k.filters_done, 1)
                dve.wait_ge(k.filters_done, t + 1)


def message_phase(nc, k):
    with phase(nc, "m_") as (sb, ps, sem), ExitStack() as ctx:

        w1 = sb("w1", [P, 2 * KB, D])
        w1a = sb("w1a", [EDGE64, D])
        w2 = sb("w2", [P, KB, D])
        w3b = sb("w3b", [P, KB, D])
        bias = sb("bias", [P, 2, KB])
        attrT = sb("attrT", [EDGE64, EDGE_TILES * P])
        x_in = sb("x_in", [P, 2, 2, D])
        xT = sb("xT", [P, 2, 2, KB, D])
        hidT = [sb("hid1T", [P, 2, KB, D]), sb("hid2T", [P, 2, KB, D])]
        h = sb("h", [P, 2, D])
        den = sb("den", [P, 2, D])
        rec = sb("rec", [P, 2, D])
        msg = sb("msg", [P, 2, D])
        tile_sum = sb("tile_sum", [P, 2, D])
        p_T = [ps(f"p_T{i}", [P, D]) for i in range(2)]
        p_H = [ps(f"p_H{i}", [P, D]) for i in range(4)]
        p_C = ps("p_C", [P, D])
        p_S = ps("p_S", [P, D])

        w_in, w2_in, w3_in, small_in = sem("w1_in"), sem("w2_in"), sem("w3_in"), sem("small_in")
        gathered = [sem(f"gathered{i}") for i in range(2)]
        turned, turned_out = sem("turned"), sem("turned_out")
        pre, h_done, exp_done, den_done, rec_done, step_done, hid_done = (
            sem("pre"), sem("h"), sem("exp"), sem("den"), sem("rec"), sem("step"), sem("hid"))
        c_done, c_out, s_done, s_out, scattered = (
            sem("c_done"), sem("c_out"), sem("s_done"), sem("s_out"), sem("scattered0"))

        slots = []
        for it in range(GROUPS + 2):
            slots += [(0, it, q) for q in range(GROUP) if it < GROUPS]
            slots += [(1, it - 1, q) for q in range(GROUP) if it >= 1]
        chunk = {}
        for layer, g, q in slots:
            if g < GROUPS:
                chunk[layer, g, q] = len(chunk)
        CHUNKS = len(chunk)

        def hid_buf(layer, g):
            return hidT[layer][:, g % hidT[layer].shape[1], :, :]

        block = ctx.enter_context(nc.Block())

        @block.sync
        def _(sp):
            sp.dma_start(attrT[:, :], k.f64T).then_inc(small_in, 16)
            for i, b in enumerate((k.L0_b1, k.L0_b2)):
                for q in range(KB):
                    sp.dma_start(bias[:, i, q:q + 1], b[q * P:(q + 1) * P].rearrange("(p a) -> p a", a=1)
                                 ).then_inc(small_in, 16)
            sp.dma_start(w1[:, :, :], k.L0_W1[0:2 * D, :].rearrange("(c p) n -> p c n", p=P)).then_inc(w_in, 16)
            sp.dma_start(w1a[:, :], k.L0_W1[2 * D:2 * D + EDGE64, :]).then_inc(w_in, 16)
            sp.dma_start(w2[:, :, :], k.L0_W2.rearrange("(c p) n -> p c n", p=P)).then_inc(w2_in, 16)
            sp.dma_start(w3b[:, :, :], k.L0_W3[D:2 * D, :].rearrange("(c p) n -> p c n", p=P)).then_inc(w3_in, 16)
            for out, w in ((k.w3a, k.L0_W3[0:D, :]), (k.w4, k.L0_W4)):
                sp.dma_start(out[:, :, :], w.rearrange("(c p) n -> p c n", p=P)).then_inc(k.dense_weights_in, 16)
            for out, r in ((k.b4_row, k.L0_b4), (k.gamma0_row, k.L0_gamma), (k.beta0_row, k.L0_beta)):
                sp.dma_start(out[:, :], r.rearrange("(a n) -> a n", a=1).to_broadcast([P, D])
                             ).then_inc(k.dense_weights_in, 16)

        @block.gpsimd
        def _(pool):
            def gather(t):
                if t >= 2:
                    pool.wait_ge(turned, 2 * (t - 1))
                for s in range(2):
                    pool.indirect_dma_start(
                        x_in[:, t % 2, s, :], None, k.x[:, :],
                        at_rows(k.index[:, s, t:t + 1])).then_inc(gathered[t % 2], 16)

            def finish_chunk(c, layer, g, q):
                pool.wait_ge(step_done, c + 1)
                if layer == 0 and g >= 2:
                    pool.wait_ge(pre, chunk[1, g - 2, GROUP - 1] + 1)
                if layer == 1 and g >= 2:
                    pool.wait_ge(c_done, GROUP * (g - 1))
                nc.gpsimd.tensor_tensor(hid_buf(layer, g)[:, q, :], rec[:, c % 2, :], h[:, c % 2, :],
                                        ALU.add).then_inc(hid_done, 1)

            def scatter(n):
                pool.wait_ge(s_out, n + 1)
                if n >= 1:
                    pool.wait_ge(scattered, 16 * n)
                pool.indirect_dma_start(
                    k.sum0[:, :], at_rows(k.unique[:, 1, n:n + 1]),
                    tile_sum[:, n % 2, :], None, compute_op=ALU.add).then_inc(scattered, 16)

            for t in range(GROUP + 1):
                gather(t)
            for i, (layer, g, q) in enumerate(slots):
                if i and slots[i - 1] in chunk:
                    finish_chunk(chunk[slots[i - 1]], *slots[i - 1])
                if layer == 0:
                    t = GROUP * (g + 1) + q + 1
                    if t < EDGE_TILES:
                        gather(t)
                elif g >= 1:
                    n = GROUP * (g - 1) + q - 1
                    if n >= 0:
                        scatter(n)
            scatter(EDGE_TILES - 1)
            pool.wait_ge(scattered, 16 * EDGE_TILES)

        @block.tensor
        def _(pe):
            def turn(t):
                pe.wait_ge(gathered[t % 2], 32 * (t // 2 + 1))
                for s in range(2):
                    if 2 * t + s >= 2:
                        pe.wait_ge(turned_out, 2 * t + s - 1)
                    for c in range(KB):
                        last = pe.transpose(p_T[s][:, c * P:(c + 1) * P], x_in[:, t % 2, s, c * P:(c + 1) * P],
                                            k.ident[:, :])
                    last.then_inc(turned, 1)

            def tile_sums(n):
                pe.wait_ge(c_out, n + 1)
                if n >= 1:
                    pe.wait_ge(s_out, n)
                pe.matmul(p_S[:, :], k.same_dst[:, n, :], msg[:, n % 2, :], start=True, stop=True
                          ).then_inc(s_done, 1)

            for t in range(GROUP):
                turn(t)
            pe.wait_ge(w_in, 32)
            pe.wait_ge(small_in, 16 * 9)
            for layer, g, q in slots:
                if g < GROUPS:
                    c = chunk[layer, g, q]
                    if c >= 4:
                        pe.wait_ge(h_done, c - 3)
                    out = p_H[c % 4][:, :]
                    cols = slice(q * P, (q + 1) * P)
                    if layer == 0:
                        pe.wait_ge(turned_out, 2 * GROUP * (g + 1))
                        for s in range(2):
                            for b in range(KB):
                                pe.matmul(out, w1[:, s * KB + b, cols], xT[:, g % 2, s, b, :],
                                          start=(s == 0 and b == 0), stop=False)
                        pe.matmul(out, w1a[:, cols], attrT[:, g * D:(g + 1) * D], start=False, stop=True
                                  ).then_inc(pre, 1)
                        if g + 1 < GROUPS:
                            turn(GROUP * (g + 1) + q)
                    else:
                        pe.wait_ge(w2_in, 16)
                        pe.wait_ge(hid_done, chunk[0, g, GROUP - 1] + 1)
                        for b in range(KB):
                            last = pe.matmul(out, w2[:, b, cols], hid_buf(0, g)[:, b, :],
                                             start=(b == 0), stop=(b == KB - 1))
                        last.then_inc(pre, 1)
                if layer == 1 and g >= 1:
                    n = GROUP * (g - 1) + q
                    pe.wait_ge(w3_in, 16)
                    pe.wait_ge(hid_done, chunk[1, g - 1, GROUP - 1] + 1)
                    if n >= 1:
                        pe.wait_ge(c_out, n)
                    for b in range(KB):
                        last = pe.matmul(p_C[:, :], hid_buf(1, g - 1)[:, b, q * P:(q + 1) * P], w3b[:, b, :],
                                         start=(b == 0), stop=(b == KB - 1))
                    last.then_inc(c_done, 1)
                    if n >= 1:
                        tile_sums(n - 1)
            tile_sums(EDGE_TILES - 1)

        @block.scalar
        def _(act):
            def turn_out(t):
                for s in range(2):
                    g = t // GROUP
                    act.wait_ge(turned, 2 * t + s + 1)
                    if g >= 2:
                        act.wait_ge(pre, chunk[0, g - 2, GROUP - 1] + 1)
                    nc.scalar.activation(xT[:, g % 2, s, :, (t % GROUP) * P:(t % GROUP + 1) * P],
                                         p_T[s][:, :].rearrange("p (c e) -> p c e", c=KB), ACT.Copy
                                         ).then_inc(turned_out, 1)

            def message_out(n):
                act.wait_ge(c_done, n + 1)
                if n >= 2:
                    act.wait_ge(s_done, n - 1)
                nc.scalar.activation(msg[:, n % 2, :], p_C[:, :], ACT.Copy).then_inc(c_out, 1)

            def sum_out(n):
                act.wait_ge(s_done, n + 1)
                if n >= 2:
                    act.wait_ge(scattered, 16 * (n - 1))
                nc.scalar.activation(tile_sum[:, n % 2, :], p_S[:, :], ACT.Copy).then_inc(s_out, 1)

            for t in range(GROUP):
                turn_out(t)
            for layer, g, q in slots:
                if g < GROUPS:
                    c = chunk[layer, g, q]
                    act.wait_ge(h_done, c + 1)
                    if c >= 2:
                        act.wait_ge(rec_done, c - 1)
                    nc.scalar.activation(den[:, c % 2, :], h[:, c % 2, :], ACT.Exp).then_inc(exp_done, 1)
                    act.wait_ge(exp_done, c + 1)
                    nc.scalar.activation(den[:, c % 2, :], den[:, c % 2, :], ACT.Square, bias=1.0
                                         ).then_inc(den_done, 1)
                    act.wait_ge(den_done, 2 * c + 1)
                    nc.scalar.activation(den[:, c % 2, :], den[:, c % 2, :], ACT.Copy, bias=1.0
                                         ).then_inc(den_done, 1)
                if layer == 0 and g + 1 < GROUPS:
                    turn_out(GROUP * (g + 1) + q)
                if layer == 1 and g >= 1:
                    n = GROUP * (g - 1) + q
                    message_out(n)
                    if n >= 1:
                        sum_out(n - 1)
            sum_out(EDGE_TILES - 1)

        @block.vector
        def _(dve):
            def divide(c):
                dve.wait_ge(den_done, 2 * c + 2)
                if c >= 2:
                    dve.wait_ge(hid_done, c - 1)
                nc.vector.reciprocal(rec[:, c % 2, :], den[:, c % 2, :]).then_inc(rec_done, 1)
                dve.wait_ge(rec_done, c + 1)
                nc.vector.scalar_tensor_tensor(out=rec[:, c % 2, :], in0=h[:, c % 2, :], scalar=-2.0,
                                               in1=rec[:, c % 2, :], op0=ALU.mult, op1=ALU.mult
                                               ).then_inc(step_done, 1)

            dve.wait_ge(small_in, 16 * 9)
            for layer, g, q in slots:
                if g < GROUPS:
                    c = chunk[layer, g, q]
                    dve.wait_ge(pre, c + 1)
                    if c >= 2:
                        dve.wait_ge(hid_done, c - 1)
                    nc.vector.tensor_scalar(h[:, c % 2, :], p_H[c % 4][:, :], bias[:, layer, q:q + 1], None,
                                            ALU.add).then_inc(h_done, 1)
                    dve.wait_ge(h_done, c + 1)
                    if c >= 1:
                        divide(c - 1)
                    if c + 1 == CHUNKS:
                        divide(c)


@contextmanager
def phase(nc, prefix):
    sems = []
    with ExitStack() as ctx:
        def sem(name):
            sems.append(nc.alloc_semaphore(prefix + name))
            return sems[-1]
        yield (lambda name, shape, dt=F32: ctx.enter_context(nc.sbuf_tensor(prefix + name, shape, dt)),
               lambda name, shape: ctx.enter_context(nc.psum_tensor(prefix + name, shape, F32)), sem)
    nc.clear_and_free_semaphores(sems)
    nc.all_engine_barrier()


def row_scale(pool, k, var, mean, tmp, rstd, shift, done, base, norms=1):
    factor, add = (1.0, LN_EPS) if norms == 1 else (1.0 + LN_EPS + LN_EPS ** 2, LN_EPS ** 3)
    nc = k.nc
    pool.sem_inc(k.passed_pool, 1)
    nc.gpsimd.tensor_scalar(tmp, var, factor, add, ALU.mult, ALU.add).then_inc(done, 1)
    pool.wait_ge(done, base + 1)
    nc.gpsimd.tensor_tensor(rstd, tmp, k.minus_half[:, 0:1], ALU.pow).then_inc(done, 1)
    pool.wait_ge(done, base + 2)
    pool.sem_inc(k.passed_pool, 1)
    nc.gpsimd.tensor_scalar(shift, mean, rstd, -1.0, ALU.mult, ALU.mult).then_inc(done, 1)


def dense_phase(nc, k):
    with phase(nc, "d_") as (sb, ps, sem), ExitStack() as ctx:
        two = lambda name, shape=(P, D): [sb(f"{name}{i}", list(shape)) for i in range(2)]

        xT, x, z, h, den, rec, u, uT = (two("xT", (P, KB, P)), two("x"), two("z"), two("h"),
                                        two("den"), two("rec"), two("u"), two("uT", (P, KB, P)))
        xb, y, yn, yg, xbeta, zz, x1, x1T, p_row, p_sq = (
            two("xb"), two("y"), two("yn"), two("yg"), two("xbeta"), two("zz"), two("x1"),
            two("x1T", (P, KB, P)), two("p"), two("psq"))
        stats, mv, small = two("stats", (P, 2, 6)), two("mv", (P, 2, 2)), two("small", (P, 2, 4))
        wr = sb("wr", [P, KB, D])
        p_h, p_o, p_p = ([ps(f"p_{n}{i}", [P, D]) for i in range(2)] for n in "hop")
        p_uT, p_xT = ps("p_uT", [P, D]), ps("p_xT", [P, D])

        xT_in, x_in, z_in, x1_out, p_out = ([sem(f"{n}{i}") for i in range(2)]
                                            for n in ("xT_in", "x_in", "z_in", "x1_out", "p_out"))
        h_pre, h_done, exp_done, den_done, rec_done, step_done, u_done, u_turned, uT_done = (
            sem(n) for n in ("h_pre", "h_done", "exp", "den", "rec", "step", "u", "u_turned", "uT"))
        o_done, xb_done, y_done, st_done, mv_done, sc_done, yn_done, xbeta_done, yg_done, zz_done = (
            sem(n) for n in ("o", "xb", "y", "st", "mv", "sc", "yn", "xbeta", "yg", "zz"))
        st2_done, mv2_done, sc2_done, x1_done, x1_turned, x1T_done, p_done, row_done, sq_done, acc_done = (
            sem(n) for n in ("st2", "mv2", "sc2", "x1", "x1_turned", "x1T", "pp", "row", "sq", "acc"))

        wr_in = sem("wr_in")
        DEPTH, PEELED = 5, 8

        def run(eng, stages):
            def turn(i, par):
                for lag, f in stages:
                    if not isinstance(i, int) or 0 <= i - lag < NODE_TILES:
                        f(i - lag, (par - lag) % 2)
            for i in range(PEELED):
                turn(i, i % 2)
            with eng.Fori(PEELED, NODE_TILES - 2, 2) as i:
                turn(i, 0)
                turn(i + 1, 1)
            for i in range(NODE_TILES - 2, NODE_TILES + DEPTH):
                turn(i, i % 2)

        def landed(i, par):
            return 16 * (i // 2 + 1) if isinstance(i, int) else (i + (2 - par)) * 8

        def rows(table, i):
            return table[bass.ds(i * P, P), :]

        block = ctx.enter_context(nc.Block())

        @block.sync
        def _(sp):
            sp.dma_start(wr[:, :, :], k.L1_Wr.rearrange("(c p) n -> p c n", p=P)).then_inc(wr_in, 16)

            def load(i, b):
                if not isinstance(i, int) or i >= 2:
                    sp.wait_ge(h_pre, i - 1)
                sp.dma_start(xT[b][:, :, :], k.xT[bass.ds(i * P, P), :].rearrange("p (c n) -> p c n", c=KB)
                             ).then_inc(xT_in[b], 16)
                if not isinstance(i, int) or i >= 2:
                    sp.wait_ge(h_done, i - 1)
                sp.dma_start(z[b][:, :], rows(k.sum0, i)).then_inc(z_in[b], 16)

            def load_x(i, b):
                if not isinstance(i, int) or i >= 2:
                    sp.wait_ge(xbeta_done, i - 1)
                    sp.wait_ge(xb_done, i - 1)
                sp.dma_start(x[b][:, :], rows(k.x, i)).then_inc(x_in[b], 16)

            def store_x1(i, b):
                sp.wait_ge(x1_done, i + 1)
                sp.dma_start(rows(k.x1, i), x1[b][:, :]).then_inc(x1_out[b], 16)

            def store_p(i, b):
                sp.wait_ge(row_done, i + 1)
                sp.dma_start(rows(k.p, i), p_row[b][:, :]).then_inc(p_out[b], 16)

            run(sp, [(0, load), (1, load_x), (3, store_x1), (5, store_p)])
            for b in range(2):
                sp.wait_ge(x1_out[b], 16 * (NODE_TILES // 2))
                sp.wait_ge(p_out[b], 16 * (NODE_TILES // 2))

        @block.tensor
        def _(pe):
            pe.wait_ge(k.dense_weights_in, 16 * 5)

            def product(out, lhsT, w, done):
                for c in range(KB):
                    last = nc.tensor.matmul(out[:, :], lhsT[:, c, :], w[:, c, :], start=(c == 0), stop=(c == KB - 1))
                last.then_inc(done, 1)

            def transposes(out, row, done):
                for c in range(KB):
                    last = nc.tensor.transpose(out[:, c * P:(c + 1) * P], row[:, c * P:(c + 1) * P], k.ident[:, :])
                last.then_inc(done, 1)

            def first(i):
                return isinstance(i, int) and i < 2

            def turn_x1(i, b):
                pe.wait_ge(x1_done, i + 1)
                if not isinstance(i, int) or i >= 1:
                    pe.wait_ge(x1T_done, i)
                transposes(p_xT, x1[b], x1_turned)

            def hidden(i, b):
                pe.wait_ge(xT_in[b], landed(i, b))
                if not first(i):
                    pe.wait_ge(h_done, i - 1)
                product(p_h[b], xT[b], k.w3a, h_pre)

            def turn_u(i, b):
                pe.wait_ge(u_done, i + 1)
                if not isinstance(i, int) or i >= 1:
                    pe.wait_ge(uT_done, i)
                transposes(p_uT, u[b], u_turned)

            def root(i, b):
                pe.wait_ge(x1T_done, i + 1)
                if isinstance(i, int) and i == 0:
                    pe.wait_ge(wr_in, 16)
                if not first(i):
                    pe.wait_ge(row_done, i - 1)
                    pe.wait_ge(sq_done, i - 1)
                product(p_p[b], x1T[b], wr, p_done)

            def output(i, b):
                pe.wait_ge(uT_done, i + 1)
                if not first(i):
                    pe.wait_ge(y_done, i - 1)
                product(p_o[b], uT[b], k.w4, o_done)

            run(pe, [(0, hidden), (1, turn_u), (3, turn_x1), (4, root), (1, output)])

        @block.scalar
        def _(act):
            first = lambda i: isinstance(i, int) and i < 2

            def x1_turned_out(i, b):
                act.wait_ge(x1_turned, i + 1)
                if not first(i):
                    act.wait_ge(p_done, i - 1)
                nc.scalar.activation(x1T[b][:, :, :], p_xT[:, :].rearrange("p (c n) -> p c n", c=KB), ACT.Copy
                                     ).then_inc(x1T_done, 1)

            def normalise_y(i, b):
                act.wait_ge(sc_done, 3 * i + 3)
                if not first(i):
                    act.wait_ge(yg_done, i - 1)
                nc.scalar.activation(yn[b][:, :], y[b][:, :], ACT.Identity, bias=small[b][:, 0, 2:3],
                                     scale=small[b][:, 0, 1:2]).then_inc(yn_done, 1)

            def u_turned_out(i, b):
                act.wait_ge(u_turned, i + 1)
                if not first(i):
                    act.wait_ge(o_done, i - 1)
                nc.scalar.activation(uT[b][:, :, :], p_uT[:, :].rearrange("p (c n) -> p c n", c=KB), ACT.Copy
                                     ).then_inc(uT_done, 1)

            def denominator(i, b):
                act.wait_ge(h_done, i + 1)
                if not first(i):
                    act.wait_ge(rec_done, i - 1)
                nc.scalar.activation(den[b][:, :], h[b][:, :], ACT.Exp).then_inc(exp_done, 1)
                act.wait_ge(exp_done, i + 1)
                nc.scalar.activation(den[b][:, :], den[b][:, :], ACT.Square, bias=1.0).then_inc(den_done, 1)
                act.wait_ge(den_done, 2 * i + 1)
                nc.scalar.activation(den[b][:, :], den[b][:, :], ACT.Copy, bias=1.0).then_inc(den_done, 1)

            def normalise_x1(i, b):
                act.wait_ge(sc2_done, 3 * i + 3)
                if not first(i):
                    act.wait_ge(x1_turned, i - 1)
                    act.wait_ge(x1_out[b], landed(i - 2, b))
                nc.scalar.activation(x1[b][:, :], zz[b][:, :], ACT.Identity, bias=small[b][:, 1, 2:3],
                                     scale=small[b][:, 1, 1:2]).then_inc(x1_done, 1)

            def root_out(i, b):
                act.wait_ge(p_done, i + 1)
                if not first(i):
                    act.wait_ge(p_out[b], landed(i - 2, b))
                    act.wait_ge(acc_done, 2 * i - 2)
                nc.scalar.activation(p_row[b][:, :], p_p[b][:, :], ACT.Copy).then_inc(row_done, 1)
                nc.scalar.activation(p_sq[b][:, :], p_p[b][:, :], ACT.Square).then_inc(sq_done, 1)

            run(act, [(3, normalise_x1), (2, normalise_y), (1, u_turned_out), (3, x1_turned_out),
                      (0, denominator), (4, root_out)])

        @block.vector
        def _(dve):
            first = lambda i: isinstance(i, int) and i < 2

            def residual(i, b):
                dve.wait_ge(o_done, i + 1)
                dve.wait_ge(xb_done, i + 1)
                if not first(i):
                    dve.wait_ge(yn_done, i - 1)
                nc.vector.tensor_tensor(y[b][:, :], p_o[b][:, :], xb[b][:, :], ALU.add).then_inc(y_done, 1)
                dve.wait_ge(y_done, i + 1)
                nc.vector.bn_stats(stats[b][:, 0, :], y[b][:, :]).then_inc(st_done, 1)
                dve.wait_ge(st_done, i + 1)
                if not first(i):
                    dve.wait_ge(sc_done, 3 * i - 3)
                dve.sem_inc(k.passed_dve, 1)
                nc.vector.bn_aggr(mv[b][:, 0, :], stats[b][:, 0, :]).then_inc(mv_done, 1)

            def accumulate(i, b):
                valid = P
                if isinstance(i, int) and i >= LAST_VALID_TILE:
                    valid = N % P if i == LAST_VALID_TILE else 0
                dve.wait_ge(row_done, i + 1)
                dve.wait_ge(sq_done, i + 1)
                if not isinstance(i, int) or i >= 1:
                    dve.wait_ge(acc_done, 2 * i)
                for s, part in enumerate((p_row, p_sq)):
                    if valid:
                        nc.vector.tensor_tensor(k.column_acc[0:valid, s, :], k.column_acc[0:valid, s, :],
                                                part[b][0:valid, :], ALU.add).then_inc(acc_done, 1)

            def hidden(i, b):
                dve.wait_ge(h_pre, i + 1)
                dve.wait_ge(z_in[b], landed(i, b))
                if not first(i):
                    dve.wait_ge(step_done, i - 1)
                    dve.wait_ge(u_done, i - 1)
                nc.vector.tensor_tensor(h[b][:, :], p_h[b][:, :], z[b][:, :], ALU.add).then_inc(h_done, 1)

            def second_norm(i, b):
                dve.wait_ge(yg_done, i + 1)
                dve.wait_ge(xbeta_done, i + 1)
                if not first(i):
                    dve.wait_ge(x1_done, i - 1)
                nc.vector.tensor_tensor(zz[b][:, :], yg[b][:, :], xbeta[b][:, :], ALU.add).then_inc(zz_done, 1)
                dve.wait_ge(zz_done, i + 1)
                nc.vector.bn_stats(stats[b][:, 1, :], zz[b][:, :]).then_inc(st2_done, 1)
                dve.wait_ge(st2_done, i + 1)
                if not first(i):
                    dve.wait_ge(sc2_done, 3 * i - 3)
                dve.sem_inc(k.passed_dve, 1)
                nc.vector.bn_aggr(mv[b][:, 1, :], stats[b][:, 1, :]).then_inc(mv2_done, 1)

            def divide(i, b):
                dve.wait_ge(den_done, 2 * i + 2)
                if not first(i):
                    dve.wait_ge(u_done, i - 1)
                nc.vector.reciprocal(rec[b][:, :], den[b][:, :]).then_inc(rec_done, 1)
                dve.wait_ge(rec_done, i + 1)
                nc.vector.scalar_tensor_tensor(out=rec[b][:, :], in0=h[b][:, :], scalar=-2.0, in1=rec[b][:, :],
                                               op0=ALU.mult, op1=ALU.mult).then_inc(step_done, 1)

            nc.vector.memset(k.column_acc[:, :, :], 0.0).then_inc(k.acc_zero, 1)
            dve.wait_ge(k.acc_zero, 1)
            run(dve, [(2, residual), (5, accumulate), (0, hidden), (2, second_norm), (0, divide)])

        @block.gpsimd
        def _(pool):
            first = lambda i: isinstance(i, int) and i < 2
            pool.wait_ge(k.dense_weights_in, 16 * 5)

            def finish_u(i, b):
                pool.wait_ge(step_done, i + 1)
                if not first(i):
                    pool.wait_ge(u_turned, i - 1)
                nc.gpsimd.tensor_tensor(u[b][:, :], rec[b][:, :], h[b][:, :], ALU.add).then_inc(u_done, 1)

            def add_beta(i, b):
                pool.wait_ge(x_in[b], landed(i, b))
                if not first(i):
                    pool.wait_ge(zz_done, i - 1)
                nc.gpsimd.tensor_tensor(xbeta[b][:, :], x[b][:, :], k.beta0_row[:, :], ALU.add).then_inc(xbeta_done, 1)

            def scale_y(i, b):
                pool.wait_ge(mv_done, i + 1)
                if not first(i):
                    pool.wait_ge(yn_done, i - 1)
                row_scale(pool, k, mv[b][:, 0, 1:2], mv[b][:, 0, 0:1], small[b][:, 0, 0:1], small[b][:, 0, 1:2],
                          small[b][:, 0, 2:3], sc_done, 3 * i)

            def add_b4(i, b):
                pool.wait_ge(x_in[b], landed(i, b))
                if not first(i):
                    pool.wait_ge(y_done, i - 1)
                nc.gpsimd.tensor_tensor(xb[b][:, :], x[b][:, :], k.b4_row[:, :], ALU.add).then_inc(xb_done, 1)

            def times_gamma(i, b):
                pool.wait_ge(yn_done, i + 1)
                if not first(i):
                    pool.wait_ge(zz_done, i - 1)
                nc.gpsimd.tensor_tensor(yg[b][:, :], yn[b][:, :], k.gamma0_row[:, :], ALU.mult).then_inc(yg_done, 1)

            def scale_x1(i, b):
                pool.wait_ge(mv2_done, i + 1)
                if not first(i):
                    pool.wait_ge(x1_done, i - 1)
                row_scale(pool, k, mv[b][:, 1, 1:2], mv[b][:, 1, 0:1], small[b][:, 1, 0:1], small[b][:, 1, 1:2],
                          small[b][:, 1, 2:3], sc2_done, 3 * i)

            run(pool, [(1, finish_u), (2, scale_y), (2, add_beta), (2, times_gamma), (1, add_b4), (2, scale_x1)])


def aggregate_phase(nc, k):
    with phase(nc, "a_") as (sb, ps, sem), ExitStack() as ctx:

        wl = sb("wl", [P, KB, D])
        old = sb("old", [P, EDGE_TILES, D])
        xT = [sb(f"xT{i}", [P, KB, P]) for i in range(2)]
        msg, tile_sum, both, share = ([sb(f"{n}{i}", [P, w]) for i in range(2)]
                                      for n, w in (("msg", D), ("tile_sum", D), ("both", D), ("share", P)))
        gamma, beta, bl, mean, var, tmp = (sb(n, [P, D]) for n in ("gamma", "beta", "bl", "mean", "var", "tmp"))
        power = msg[0]
        p_T, p_A, p_S = ([ps(f"p_{n}{i}", [P, D]) for i in range(2)] for n in "TAS")
        p_sum, p_sq = ps("p_sum", [P, D]), ps("p_sq", [P, D])

        x_in, new_in = [sem(f"x_in{i}") for i in range(4)], [sem(f"new_in{i}") for i in range(4)]
        old_in, w_in, turned, turned_out, a_done, a_out, s_done, s_out, scattered = (
            sem(n) for n in ("old_in", "w_in", "turned", "turned_out", "done", "out", "s_done", "s_out", "scattered"))
        diff, both_done, share_done, summed, fin, power_done = (
            sem(n) for n in ("diff", "both_done", "share_done", "summed", "fin", "power_done"))

        block = ctx.enter_context(nc.Block())

        @block.sync
        def _(sp):
            sp.dma_start(wl[:, :, :], k.L1_Wl.rearrange("(c p) n -> p c n", p=P)).then_inc(w_in, 16)
            for out, r in ((gamma, k.L1_gamma), (beta, k.L1_beta), (bl, k.L1_bl)):
                sp.dma_start(out[:, :], r.rearrange("(a n) -> a n", a=1).to_broadcast([P, D])).then_inc(w_in, 16)

        @block.gpsimd
        def _(pool):
            for t in range(EDGE_TILES):
                if t >= 4:
                    pool.wait_ge(x_in[t % 4], 16 * (t // 4))
                pool.indirect_dma_start(k.src_rows_sb[:, t, :], None, k.x1[:, :], at_rows(k.index[:, 0, t:t + 1])
                                        ).then_inc(x_in[t % 4], 16)
                pool.indirect_dma_start(old[:, t, :], None, k.p[:, :], at_rows(k.index[:, 1, t:t + 1])
                                        ).then_inc(old_in, 16)
            pool.wait_ge(old_in, 16 * EDGE_TILES)
            for t in range(EDGE_TILES):
                pool.wait_ge(s_out, t + 1)
                if t:
                    pool.wait_ge(scattered, 16 * t)
                pool.indirect_dma_start(k.p[:, :], at_rows(k.unique[:, 1, t:t + 1]), tile_sum[t % 2][:, :], None,
                                        compute_op=ALU.add).then_inc(scattered, 16)
            pool.wait_ge(scattered, 16 * EDGE_TILES)
            for t in range(EDGE_TILES):
                if t >= 4:
                    pool.wait_ge(new_in[t % 4], 16 * (t // 4))
                pool.indirect_dma_start(k.dst_rows_sb[:, t, :], None, k.p[:, :], at_rows(k.index[:, 1, t:t + 1])
                                        ).then_inc(new_in[t % 4], 16)
            nc.gpsimd.memset(power[:, :], -0.5).then_inc(power_done, 1)
            pool.wait_ge(power_done, 1)
            pool.wait_ge(fin, 4)
            nc.gpsimd.tensor_tensor(tmp[:, :], var[:, :], power[:, :], ALU.pow).then_inc(power_done, 1)

        @block.tensor
        def _(pe):
            def turn(t):
                pe.wait_ge(x_in[t % 4], 16 * (t // 4 + 1))
                if t >= 2:
                    pe.wait_ge(turned_out, t - 1)
                for c in range(KB):
                    last = nc.tensor.transpose(p_T[t % 2][:, c * P:(c + 1) * P],
                                               k.src_rows_sb[:, t, c * P:(c + 1) * P], k.ident[:, :])
                last.then_inc(turned, 1)

            def tile_sums(t):
                pe.wait_ge(a_out, t + 1)
                if t >= 2:
                    pe.wait_ge(s_out, t - 1)
                nc.tensor.matmul(p_S[t % 2][:, :], k.same_dst[:, t, :], msg[t % 2][:, :], start=True, stop=True
                                 ).then_inc(s_done, 1)

            turn(0)
            pe.wait_ge(w_in, 64)
            for t in range(EDGE_TILES):
                if t + 1 < EDGE_TILES:
                    turn(t + 1)
                pe.wait_ge(turned_out, t + 1)
                if t >= 2:
                    pe.wait_ge(a_out, t - 1)
                for c in range(KB):
                    last = nc.tensor.matmul(p_A[t % 2][:, :], xT[t % 2][:, c, :], wl[:, c, :],
                                            start=(c == 0), stop=(c == KB - 1))
                last.then_inc(a_done, 1)
                if t:
                    tile_sums(t - 1)
            tile_sums(EDGE_TILES - 1)
            nc.tensor.matmul(p_sum[:, :], k.ones[:, :], k.column_acc[:, 0, :], start=True, stop=False)
            nc.tensor.matmul(p_sq[:, :], k.ones[:, :], k.column_acc[:, 1, :], start=True, stop=False)
            for t in range(EDGE_TILES):
                pe.wait_ge(share_done, t + 1)
                pe.wait_ge(both_done, 2 * t + 2)
                last = t == EDGE_TILES - 1
                nc.tensor.matmul(p_sum[:, :], share[t % 2][:, :], old[:, t, :], start=False, stop=last)
                nc.tensor.matmul(p_sq[:, :], share[t % 2][:, :], both[t % 2][:, :], start=False, stop=last
                                 ).then_inc(summed, 1)

        @block.scalar
        def _(act):
            def turn_out(t):
                act.wait_ge(turned, t + 1)
                if t >= 2:
                    act.wait_ge(a_done, t - 1)
                nc.scalar.activation(xT[t % 2][:, :, :], p_T[t % 2][:, :].rearrange("p (c n) -> p c n", c=KB),
                                     ACT.Copy).then_inc(turned_out, 1)

            def sum_out(t):
                act.wait_ge(s_done, t + 1)
                if t >= 2:
                    act.wait_ge(scattered, 16 * (t - 1))
                nc.scalar.activation(tile_sum[t % 2][:, :], p_S[t % 2][:, :], ACT.Copy).then_inc(s_out, 1)

            turn_out(0)
            for t in range(EDGE_TILES):
                if t + 1 < EDGE_TILES:
                    turn_out(t + 1)
                act.wait_ge(a_done, t + 1)
                if t >= 2:
                    act.wait_ge(s_done, t - 1)
                nc.scalar.activation(msg[t % 2][:, :], p_A[t % 2][:, :], ACT.Copy, scale=k.inv_degree[:, t:t + 1]
                                     ).then_inc(a_out, 1)
                if t:
                    sum_out(t - 1)
            sum_out(EDGE_TILES - 1)

        @block.vector
        def _(dve):
            for t in range(EDGE_TILES):
                dve.wait_ge(new_in[t % 4], 16 * (t // 4 + 1))
                if t == 0:
                    dve.wait_ge(old_in, 16 * EDGE_TILES)
                if t >= 2:
                    dve.wait_ge(summed, t - 1)
                nc.vector.tensor_scalar(share[t % 2][:, :], k.ones[:, :], k.share[:, t:t + 1], None, ALU.mult
                                        ).then_inc(share_done, 1)
                nc.vector.tensor_tensor(both[t % 2][:, :], k.dst_rows_sb[:, t, :], old[:, t, :], ALU.add
                                        ).then_inc(both_done, 1)
                dve.wait_ge(both_done, 2 * t + 1)
                nc.vector.tensor_tensor(old[:, t, :], k.dst_rows_sb[:, t, :], old[:, t, :], ALU.subtract
                                        ).then_inc(diff, 1)
                dve.wait_ge(diff, t + 1)
                nc.vector.tensor_tensor(both[t % 2][:, :], both[t % 2][:, :], old[:, t, :], ALU.mult
                                        ).then_inc(both_done, 1)
            dve.wait_ge(summed, EDGE_TILES)
            dve.wait_ge(w_in, 64)
            n = [0]

            def step(ins):
                n[0] += 1
                ins.then_inc(fin, 1)
                dve.wait_ge(fin, n[0])

            step(nc.vector.tensor_scalar(mean[:, :], p_sum[:, :], 1.0 / N, None, ALU.mult))
            step(nc.vector.tensor_tensor(tmp[:, :], mean[:, :], mean[:, :], ALU.mult))
            step(nc.vector.scalar_tensor_tensor(out=var[:, :], in0=p_sq[:, :], scalar=1.0 / N, in1=tmp[:, :],
                                                op0=ALU.mult, op1=ALU.subtract))
            step(nc.vector.tensor_scalar(var[:, :], var[:, :], 0.0, LN_EPS, ALU.max, ALU.add))
            dve.wait_ge(power_done, 2)
            step(nc.vector.tensor_tensor(k.bn_scale[:, :], tmp[:, :], gamma[:, :], ALU.mult))
            step(nc.vector.tensor_tensor(mean[:, :], mean[:, :], bl[:, :], ALU.add))
            step(nc.vector.tensor_tensor(mean[:, :], bl[:, :], mean[:, :], ALU.subtract))
            step(nc.vector.tensor_tensor(mean[:, :], mean[:, :], k.bn_scale[:, :], ALU.mult))
            step(nc.vector.tensor_tensor(k.bn_shift[:, :], mean[:, :], beta[:, :], ALU.add))


def plain_load(nc, k, sp, i):
    b = i % 2
    if i >= 2:
        sp.wait_ge(k.plain_y, i - 1)
    sp.dma_start(k.plain_p_rows[b][:, :], k.p[i * P:(i + 1) * P, :]).then_inc(k.plain_p_in[b], 16)
    sp.dma_start(k.plain_x1_rows[b][:, :], k.x1[i * P:(i + 1) * P, :]).then_inc(k.plain_x1_in[b], 16)


def plain_store(nc, k, sp, i):
    b = i % 2
    sp.wait_ge(k.plain_out, i + 1)
    sp.dma_start(k.out[i * P:(i + 1) * P, :], k.plain_y_rows[b][:, :]).then_inc(k.plain_gone[b], 16)


def plain_scale(nc, k, pool, i):
    b = i % 2
    pool.wait_ge(k.plain_p_in[b], 16 * (i // 2 + 1))
    nc.gpsimd.tensor_tensor(k.plain_p_rows[b][:, :], k.plain_p_rows[b][:, :], k.bn_scale[:, :], ALU.mult
                            ).then_inc(k.plain_scaled, 1)


def plain_norm(nc, k, dve, i):
    b = i % 2
    a, y = k.plain_p_rows[b], k.plain_y_rows[b]
    dve.wait_ge(k.plain_scaled, i + 1)
    nc.vector.tensor_tensor(a[:, :], a[:, :], k.bn_shift[:, :], ALU.add).then_inc(k.plain_shifted, 1)
    dve.wait_ge(k.plain_shifted, i + 1)
    nc.vector.scalar_tensor_tensor(out=a[:, :], in0=a[:, :], scalar=0.01, in1=a[:, :], op0=ALU.mult, op1=ALU.max
                                   ).then_inc(k.plain_leaky, 1)
    dve.wait_ge(k.plain_leaky, i + 1)
    dve.wait_ge(k.plain_x1_in[b], 16 * (i // 2 + 1))
    if i >= 2:
        dve.wait_ge(k.plain_gone[b], 16 * (i // 2))
    nc.vector.scalar_tensor_tensor(out=y[:, :], in0=k.plain_x1_rows[b][:, :], scalar=2.0, in1=a[:, :],
                                   op0=ALU.mult, op1=ALU.add).then_inc(k.plain_y, 1)
    dve.wait_ge(k.plain_y, i + 1)
    nc.vector.bn_stats(k.plain_stats[b][:, :], y[:, :]).then_inc(k.plain_st, 1)
    dve.wait_ge(k.plain_st, i + 1)
    if i >= 2:
        dve.wait_ge(k.plain_sc, 3 * i - 3)
    nc.vector.bn_aggr(k.plain_mv[b][:, :], k.plain_stats[b][:, :]).then_inc(k.plain_mv_done, 1)


def plain_row_scale(nc, k, pool, i):
    b = i % 2
    mv, small = k.plain_mv[b], k.plain_small[b]
    pool.wait_ge(k.plain_mv_done, i + 1)
    if i >= 2:
        pool.wait_ge(k.plain_out, i - 1)
    row_scale(pool, k, mv[:, 1:2], mv[:, 0:1], small[:, 0:1], small[:, 1:2], small[:, 2:3], k.plain_sc, 3 * i,
              norms=3)


def plain_row(nc, k, act, i):
    b = i % 2
    y, small = k.plain_y_rows[b], k.plain_small[b]
    act.wait_ge(k.plain_sc, 3 * i + 3)
    nc.scalar.activation(y[:, :], y[:, :], ACT.Identity, bias=small[:, 2:3], scale=small[:, 1:2]
                         ).then_inc(k.plain_out, 1)


def edge_rows_phase(nc, k):
    with phase(nc, "e_") as (sb, ps, sem), ExitStack() as ctx:
        T = EDGE_TILES
        ws, wv = sb("ws", [P, F]), sb("wv", [P, F])
        other = [sb(f"other{i}", [P, D]) for i in range(4)]
        a, y, featT = ([sb(f"{n}{i}", [P, D]) for i in range(2)] for n in ("a", "y", "featT"))
        stats, mv, small = ([sb(f"{n}{i}", [P, w]) for i in range(2)] for n, w in (("stats", 6), ("mv", 2), ("small", 4)))
        edge, part, tile_sum = ([sb(f"{n}{i}", [P, w]) for i in range(2)]
                                for n, w in (("edge", 8 * F), ("part", 3 * F), ("tile_sum", 8 * F)))
        p_T, p_F, p_S = ([ps(f"p_{n}{i}", [P, D]) for i in range(2)] for n in "TFS")

        w_in = sem("w_in")
        other_in = [sem(f"other_in{i}") for i in range(4)]
        scaled, shifted, leaky, y_done, st, mv_done, sc, x2_done = (
            sem(n) for n in ("scaled", "shifted", "leaky", "y", "st", "mv", "sc", "x2"))
        turned, turned_out, feat, s_part, v_part, dot, edge_done, s_done, s_out, scattered = (
            sem(n) for n in ("turned", "turned_out", "feat", "s_part", "v_part", "dot", "edge", "s_done", "s_out", "scat"))

        def p_of(u):
            return k.dst_rows_sb[:, u, :] if u < T else other[u % 4][:, :]

        def x1_of(u):
            return other[u % 4][:, :] if u < T else k.src_rows_sb[:, u - T, :]

        def x2_of(u):
            return k.dst_rows_sb[:, u, :] if u < T else k.src_rows_sb[:, u - T, :]

        block = ctx.enter_context(nc.Block())

        @block.sync
        def _(sp):
            sp.dma_start(ws[:, :], k.L2_ws).then_inc(w_in, 16)
            sp.dma_start(wv[:, :], k.L2_wv).then_inc(w_in, 16)

        @block.gpsimd
        def _(pool):
            def gather(u):
                if u >= 4:
                    pool.wait_ge(y_done if u - 4 < T else scaled, u - 3)
                table, side = (k.x1, 1) if u < T else (k.p, 0)
                pool.indirect_dma_start(other[u % 4][:, :], None, table[:, :],
                                        at_rows(k.index[:, side, u % T:u % T + 1])).then_inc(other_in[u % 4], 16)

            def scale(u):
                if u >= T:
                    pool.wait_ge(other_in[u % 4], 16 * (u // 4 + 1))
                if u >= 2:
                    pool.wait_ge(y_done, u - 1)
                nc.gpsimd.tensor_tensor(a[u % 2][:, :], p_of(u), k.bn_scale[:, :], ALU.mult).then_inc(scaled, 1)

            def row(u):
                b = u % 2
                pool.wait_ge(mv_done, u + 1)
                if u >= 2:
                    pool.wait_ge(x2_done, u - 1)
                row_scale(pool, k, mv[b][:, 1:2], mv[b][:, 0:1], small[b][:, 0:1], small[b][:, 1:2],
                          small[b][:, 2:3], sc, 3 * u)

            def scatter(t):
                pool.wait_ge(s_out, t + 1)
                if t:
                    pool.wait_ge(scattered, 16 * t)
                pool.indirect_dma_start(k.sum2[:, :], at_rows(k.unique[:, 0, t:t + 1]), tile_sum[t % 2][:, :], None,
                                        compute_op=ALU.add).then_inc(scattered, 16)

            for u in range(3):
                gather(u)
            for u in range(2 * T + 6):
                if u < 2 * T:
                    scale(u)
                if u + 3 < 2 * T:
                    gather(u + 3)
                if 1 <= u <= 2 * T:
                    row(u - 1)
                if 0 <= u - 5 < T:
                    scatter(u - 5)
            pool.wait_ge(scattered, 16 * T)

        @block.vector
        def _(dve):
            def norm(u):
                b = u % 2
                dve.wait_ge(scaled, u + 1)
                nc.vector.tensor_tensor(a[b][:, :], a[b][:, :], k.bn_shift[:, :], ALU.add).then_inc(shifted, 1)
                dve.wait_ge(shifted, u + 1)
                nc.vector.scalar_tensor_tensor(out=a[b][:, :], in0=a[b][:, :], scalar=0.01, in1=a[b][:, :],
                                               op0=ALU.mult, op1=ALU.max).then_inc(leaky, 1)
                dve.wait_ge(leaky, u + 1)
                if u < T:
                    dve.wait_ge(other_in[u % 4], 16 * (u // 4 + 1))
                if u >= 2:
                    dve.wait_ge(x2_done, u - 1)
                nc.vector.scalar_tensor_tensor(out=y[b][:, :], in0=x1_of(u), scalar=2.0, in1=a[b][:, :],
                                               op0=ALU.mult, op1=ALU.add).then_inc(y_done, 1)
                dve.wait_ge(y_done, u + 1)
                nc.vector.bn_stats(stats[b][:, :], y[b][:, :]).then_inc(st, 1)
                dve.wait_ge(st, u + 1)
                if u >= 2:
                    dve.wait_ge(sc, 3 * u - 3)
                nc.vector.bn_aggr(mv[b][:, :], stats[b][:, :]).then_inc(mv_done, 1)

            def message(t):
                b = t % 2
                e4 = edge[b][:, :].rearrange("p (c h f) -> p c h f", c=4, h=2)
                a4 = k.filters[:, t, :, :]
                dve.wait_ge(feat, t + 1)
                if t >= 2:
                    dve.wait_ge(s_done, t - 1)
                s = p_F[b][:, 0:F].rearrange("p (a f) -> p a f", a=1)
                v = p_F[b][:, F:4 * F].rearrange("p (c f) -> p c f", c=3)
                nc.vector.tensor_tensor(e4[:, :, 0, :], s.to_broadcast([P, 4, F]), a4[:, 0:4, :], ALU.mult
                                        ).then_inc(s_part, 1)
                nc.vector.tensor_tensor(e4[:, 1:4, 1, :], v, a4[:, 7:8, :].to_broadcast([P, 3, F]), ALU.mult
                                        ).then_inc(v_part, 1)
                if t >= 2:
                    dve.wait_ge(edge_done, t - 1)
                nc.vector.tensor_tensor(part[b][:, :].rearrange("p (c f) -> p c f", c=3), v, a4[:, 4:7, :], ALU.mult
                                        ).then_inc(dot, 1)
                dve.wait_ge(dot, t + 1)
                nc.vector.tensor_reduce(e4[:, 0, 1, :], part[b][:, :].rearrange("p (c f) -> p f c", c=3), AX_X,
                                        ALU.add).then_inc(edge_done, 1)

            for u in range(2 * T + 4):
                if u < 2 * T:
                    norm(u)
                if 0 <= u - 3 < T:
                    message(u - 3)

        @block.scalar
        def _(act):
            def x2_row(u):
                b = u % 2
                act.wait_ge(sc, 3 * u + 3)
                nc.scalar.activation(x2_of(u), y[b][:, :], ACT.Identity, bias=small[b][:, 2:3],
                                     scale=small[b][:, 1:2]).then_inc(x2_done, 1)

            def turn_out(t):
                act.wait_ge(turned, t + 1)
                if t >= 2:
                    act.wait_ge(feat, t - 1)
                nc.scalar.activation(featT[t % 2][:, :], p_T[t % 2][:, :], ACT.Copy).then_inc(turned_out, 1)

            def sum_out(t):
                act.wait_ge(s_done, t + 1)
                if t >= 2:
                    act.wait_ge(scattered, 16 * (t - 1))
                nc.scalar.activation(tile_sum[t % 2][:, :], p_S[t % 2][:, 0:8 * F], ACT.Copy).then_inc(s_out, 1)

            for u in range(2 * T + 5):
                if 1 <= u <= 2 * T:
                    x2_row(u - 1)
                if 0 <= u - 2 < T:
                    turn_out(u - 2)
                if 0 <= u - 4 < T:
                    sum_out(u - 4)

        @block.tensor
        def _(pe):
            def turn(t):
                pe.wait_ge(x2_done, t + 1)
                if t >= 2:
                    pe.wait_ge(turned_out, t - 1)
                x2 = k.dst_rows_sb[:, t, :]
                vector = x2[:, B:].rearrange("p (b c) -> p c b", c=3)
                for c in range(4):
                    last = nc.tensor.transpose(p_T[t % 2][:, c * P:(c + 1) * P],
                                               x2[:, 0:B] if c == 0 else vector[:, c - 1, :], k.ident[:, :])
                last.then_inc(turned, 1)

            def features(t):
                pe.wait_ge(turned_out, t + 1)
                if t >= 2:
                    pe.wait_ge(edge_done, t - 1)
                for c in range(4):
                    last = nc.tensor.matmul(p_F[t % 2][:, c * F:(c + 1) * F], featT[t % 2][:, c * P:(c + 1) * P],
                                            (ws if c == 0 else wv)[:, :], start=True, stop=True)
                last.then_inc(feat, 1)

            def tile_sums(t):
                pe.wait_ge(s_part, t + 1)
                pe.wait_ge(v_part, t + 1)
                pe.wait_ge(edge_done, t + 1)
                if t >= 2:
                    pe.wait_ge(s_out, t - 1)
                nc.tensor.matmul(p_S[t % 2][:, 0:8 * F], k.same_src[:, t, :], edge[t % 2][:, :], start=True, stop=True
                                 ).then_inc(s_done, 1)

            pe.wait_ge(w_in, 32)
            for u in range(T + 3):
                if u < T:
                    turn(u)
                if 1 <= u <= T:
                    features(u - 1)
                if 0 <= u - 2 < T:
                    tile_sums(u - 2)


def equivariant_phase(nc, k):
    with phase(nc, "q_") as (sb, ps, sem), ExitStack() as ctx:
        U, BATCH, AHEAD = 2 * EDGE_TILES, 4, 8
        NB = U // BATCH
        LAG = 2 * BATCH
        w1s, w1v, w2s, w2v = sb("w1s", [2 * F, B]), sb("w1v", [2 * F, B]), sb("w2s", [B, B]), sb("w2v", [B, B])
        sums = [sb(f"sums{i}", [P, 8 * F]) for i in range(AHEAD)]
        sumT = [sb(f"sumT{i}", [2 * F, 4, P]) for i in range(2)]
        outT = [sb(f"outT{i}", [P, BATCH, D]) for i in range(3)]
        mag, low, logs, pos = (sb(n, [P, BATCH, B]) for n in ("mag", "low", "logs", "pos"))
        y = [sb(f"y{i}", [P, D]) for i in range(2)]
        stats, mv, small = ([sb(f"{n}{i}", [P, w]) for i in range(2)] for n, w in (("stats", 6), ("mv", 2), ("small", 4)))
        p_T = [ps(f"p_T{i}", [2 * F, 4, P]) for i in range(2)]
        p_O, p_R = ([ps(f"p_{n}{i}", [P, D]) for i in range(2)] for n in "OR")
        w_in = sem("w_in")
        sums_in = [sem(f"sums_in{i}") for i in range(AHEAD)]
        turned, turned_out, first_done, first_out, act_steps, pos_done, ssp_done, second_done = (
            sem(n) for n in ("turned", "turned_out", "first", "first_out", "act", "pos", "ssp", "second"))
        y_s, y_done, st, mv_done, sc, x3_done = (sem(n) for n in ("y_s", "y", "st", "mv", "sc", "x3"))

        def rows_of(u):
            return (k.src_rows_sb, k.dst_rows_sb)[u % 2][:, u // 2, :]

        block = ctx.enter_context(nc.Block())

        @block.sync
        def _(sp):
            for out, w in ((w1s, k.L2_o1s), (w1v, k.L2_o1v), (w2s, k.L2_o2s), (w2v, k.L2_o2v)):
                sp.dma_start(out[:, :], w).then_inc(w_in, 16)
            for u in range(U):
                plain_load(nc, k, sp, u)
                if u >= 2:
                    plain_store(nc, k, sp, u - 2)

        @block.gpsimd
        def _(pool):
            def gather(u):
                if u >= AHEAD:
                    pool.wait_ge(turned, u - AHEAD + 1)
                pool.indirect_dma_start(sums[u % AHEAD][:, :], None, k.sum2[:, :],
                                        at_rows(k.index[:, u % 2, u // 2:u // 2 + 1])).then_inc(sums_in[u % AHEAD], 16)

            def row(u):
                b = u % 2
                pool.wait_ge(mv_done, u + 1)
                if u >= 2:
                    pool.wait_ge(x3_done, u - 1)
                row_scale(pool, k, mv[b][:, 1:2], mv[b][:, 0:1], small[b][:, 0:1], small[b][:, 1:2],
                          small[b][:, 2:3], sc, 3 * u)

            for u in range(AHEAD):
                gather(u)
            for u in range(U + LAG):
                if u < U:
                    plain_scale(nc, k, pool, u)
                if u >= LAG:
                    row(u - LAG)
                if u + AHEAD < U:
                    gather(u + AHEAD)
                if 1 <= u <= U:
                    plain_row_scale(nc, k, pool, u - 1)

        @block.tensor
        def _(pe):
            pe.wait_ge(w_in, 64)

            def turn(u):
                pe.wait_ge(sums_in[u % AHEAD], 16 * (u // AHEAD + 1))
                if u >= 2:
                    pe.wait_ge(turned_out, u - 1)
                for c in range(4):
                    last = nc.tensor.transpose(p_T[u % 2][:, c, :], sums[u % AHEAD][:, c * 2 * F:(c + 1) * 2 * F],
                                               k.ident[:, :])
                last.then_inc(turned, 1)

            def first(u):
                pe.wait_ge(turned_out, u + 1)
                if u >= 2:
                    pe.wait_ge(first_out, u - 1)
                nc.tensor.matmul(p_O[u % 2][:, 0:P], w1s[:, :], sumT[u % 2][:, 0, :], start=True, stop=True)
                nc.tensor.matmul(p_O[u % 2][:, P:D], w1v[:, :], sumT[u % 2][:, 1:4, :].rearrange("k c n -> k (c n)"),
                                 start=True, stop=True).then_inc(first_done, 1)

            def second(u):
                n = u // BATCH
                pe.wait_ge(ssp_done, n + 1)
                if u >= 2:
                    pe.wait_ge(y_done, u - 1)
                for c in range(4):
                    last = nc.tensor.matmul(p_R[u % 2][:, c * P:(c + 1) * P],
                                            outT[n % 3][:, u % BATCH, c * P:(c + 1) * P],
                                            (w2s if c == 0 else w2v)[:, :], start=True, stop=True)
                last.then_inc(second_done, 1)

            turn(0)
            for u in range(U + LAG):
                if u + 1 < U:
                    turn(u + 1)
                if u < U:
                    first(u)
                if u >= LAG:
                    second(u - LAG)

        @block.scalar
        def _(act):
            def turn_out(u):
                act.wait_ge(turned, u + 1)
                if u >= 2:
                    act.wait_ge(first_done, u - 1)
                nc.scalar.activation(sumT[u % 2][:, :, :], p_T[u % 2][:, :, :], ACT.Copy).then_inc(turned_out, 1)

            def first_product_out(u):
                n = u // BATCH
                act.wait_ge(first_done, u + 1)
                if n >= 3:
                    act.wait_ge(second_done, BATCH * (n - 2))
                nc.scalar.activation(outT[n % 3][:, u % BATCH, :], p_O[u % 2][:, :], ACT.Copy,
                                     scale=(2 * F) ** -0.5).then_inc(first_out, 1)

            def logarithms(n):
                act.wait_ge(first_out, BATCH * (n + 1))
                if n:
                    act.wait_ge(ssp_done, n)
                for step, (out, in_, func, bias, scale) in enumerate((
                        (mag[:, :, :], outT[n % 3][:, :, 0:B], ACT.Abs, 0.0, 1.0),
                        (low[:, :, :], mag[:, :, :], ACT.Exp, 0.0, -1.0),
                        (logs[:, :, :], low[:, :, :], ACT.Ln, 1.0, 1.0))):
                    nc.scalar.activation(out, in_, func, bias=bias, scale=scale).then_inc(act_steps, 1)
                    act.wait_ge(act_steps, 3 * n + step + 1)

            def x3_row(u):
                b = u % 2
                act.wait_ge(sc, 3 * u + 3)
                nc.scalar.activation(rows_of(u), y[b][:, :], ACT.Identity, bias=small[b][:, 2:3],
                                     scale=small[b][:, 1:2]).then_inc(x3_done, 1)

            turn_out(0)
            for u in range(U + LAG):
                if u + 1 < U:
                    turn_out(u + 1)
                if u < U:
                    first_product_out(u)
                if u >= LAG:
                    x3_row(u - LAG)
                if 1 <= u <= U:
                    plain_row(nc, k, act, u - 1)
                if u < U and u % BATCH == BATCH - 1:
                    logarithms(u // BATCH)

        @block.vector
        def _(dve):
            def softplus(n):
                nc.vector.tensor_scalar(pos[:, :, :], outT[n % 3][:, :, 0:B], 0.0, None, ALU.max
                                        ).then_inc(pos_done, 1)
                dve.wait_ge(pos_done, n + 1)
                nc.vector.scalar_tensor_tensor(out=outT[n % 3][:, :, 0:B], in0=logs[:, :, :], scalar=-LOG2,
                                               in1=pos[:, :, :], op0=ALU.add, op1=ALU.add).then_inc(ssp_done, 1)
                dve.wait_ge(ssp_done, n + 1)

            def norm(u):
                b = u % 2
                x2, inv = rows_of(u), float(B) ** -0.5
                dve.wait_ge(second_done, u + 1)
                if u >= 2:
                    dve.wait_ge(x3_done, u - 1)
                nc.vector.scalar_tensor_tensor(out=y[b][:, 0:B], in0=p_R[b][:, 0:B], scalar=inv,
                                               in1=x2[:, 0:B], op0=ALU.mult, op1=ALU.add).then_inc(y_s, 1)
                nc.vector.scalar_tensor_tensor(
                    out=y[b][:, B:D].rearrange("p (d c) -> p c d", c=3),
                    in0=p_R[b][:, B:D].rearrange("p (c d) -> p c d", c=3), scalar=inv,
                    in1=x2[:, B:D].rearrange("p (d c) -> p c d", c=3), op0=ALU.mult, op1=ALU.add
                    ).then_inc(y_done, 1)
                dve.wait_ge(y_s, u + 1)
                dve.wait_ge(y_done, u + 1)
                nc.vector.bn_stats(stats[b][:, :], y[b][:, :]).then_inc(st, 1)
                dve.wait_ge(st, u + 1)
                if u >= 2:
                    dve.wait_ge(sc, 3 * u - 3)
                nc.vector.bn_aggr(mv[b][:, :], stats[b][:, :]).then_inc(mv_done, 1)

            for u in range(U + LAG):
                if u % BATCH == 1 and 1 <= u // BATCH <= NB:
                    n = u // BATCH - 1
                    dve.wait_ge(act_steps, 3 * n + 3)
                    softplus(n)
                if u >= LAG:
                    norm(u - LAG)
                if u < U:
                    plain_norm(nc, k, dve, u)


def scores_phase(nc, k):
    with phase(nc, "s_") as (sb, ps, sem), ExitStack() as ctx:
        T = EDGE_TILES
        PLAIN = 2 * T
        wqk = sb("wqk", [P, KB, 2 * D])
        srcT = [sb(f"srcT{i}", [P, KB, P]) for i in range(2)]
        q = [sb(f"q{i}", [P, D]) for i in range(2)]
        prod = sb("prod", [P, D])
        diag = sb("diag", [HEADS, HEADS, P])
        away = [sb(f"away{i}", [P, P]) for i in range(2)]
        cand = sb("cand", [P, HEADS, P])
        tile_max, known = ([sb(f"{n}{i}", [P, HEADS]) for i in range(2)] for n in ("tile_max", "known"))
        p_T = [ps(f"p_T{i}", [P, D]) for i in range(2)]
        p_q, p_k, p_w = ps("p_q", [P, D]), ps("p_k", [P, D]), ps("p_w", [HEADS, P])
        p_all = ps("p_all", [P, HEADS, P])
        w_in, known_in, max_gone = sem("w_in"), sem("known_in"), sem("max_gone")
        turned, turned_out, q_done, k_done, q_out, prod_done, aw_done, aw_turned, diag_done, spread = (
            sem(n) for n in ("turned", "turned_out", "q_done", "k_done", "q_out", "prod", "aw", "aw_turned", "diag", "spread"))
        away_done, cand_done, tile_max_done, merged = (sem(n) for n in ("away", "cand", "tile_max", "merged"))

        block = ctx.enter_context(nc.Block())

        @block.sync
        def _(sp):
            sp.dma_start(wqk[:, :, :], k.L3_W[:, 0:2 * D].rearrange("(c p) n -> p c n", p=P)).then_inc(w_in, 16)
            sp.dma_start(k.wv[:, :, :], k.L3_W[:, 2 * D:3 * D].rearrange("(c p) n -> p c n", p=P)).then_inc(w_in, 16)
            for i in range(PLAIN, PLAIN + T):
                plain_load(nc, k, sp, i)
                plain_store(nc, k, sp, i - 2)
            sp.wait_ge(w_in, 32)

        @block.tensor
        def _(pe):
            def turn(t):
                for s, rows in enumerate((k.src_rows_sb, k.dst_rows_sb)):
                    if t >= 1:
                        pe.wait_ge(turned_out, 2 * t - 1 + s)
                    for c in range(KB):
                        last = nc.tensor.transpose(p_T[s][:, c * P:(c + 1) * P], rows[:, t, c * P:(c + 1) * P],
                                                   k.ident[:, :])
                    last.then_inc(turned, 1)

            def scores(t):
                pe.wait_ge(aw_done, t + 1)
                if t:
                    pe.wait_ge(diag_done, t)
                nc.tensor.transpose(p_w[:, :], k.scores[:, t, :], k.ident[:, :]).then_inc(aw_turned, 1)

            def spread_scores(t):
                pe.wait_ge(diag_done, t + 1)
                if t:
                    pe.wait_ge(cand_done, t)
                for half in range(2):
                    hs = slice(half * HEADS // 2, (half + 1) * HEADS // 2)
                    last = nc.tensor.matmul(p_all[:, hs, :], k.ones[0:HEADS, :], diag[:, hs, :], start=True, stop=True)
                last.then_inc(spread, 1)

            turn(0)
            pe.wait_ge(w_in, 32)
            for t in range(T + 1):
                if t < T:
                    pe.wait_ge(turned_out, 2 * t + 2)
                    if t:
                        pe.wait_ge(q_out, t)
                    for c in range(KB):
                        last = nc.tensor.matmul(p_q[:, :], srcT[t % 2][:, c, :], wqk[:, c, 0:D],
                                                start=(c == 0), stop=(c == KB - 1))
                    last.then_inc(q_done, 1)
                if t:
                    scores(t - 1)
                if t < T:
                    if t + 1 < T:
                        turn(t + 1)
                    if t:
                        pe.wait_ge(prod_done, t)
                    for c in range(KB):
                        last = nc.tensor.matmul(p_k[:, :], k.dst_rows_sb[:, t, c * P:(c + 1) * P], wqk[:, c, D:2 * D],
                                                start=(c == 0), stop=(c == KB - 1))
                    last.then_inc(k_done, 1)
                if t:
                    spread_scores(t - 1)

        @block.scalar
        def _(act):
            def turn_out(t):
                act.wait_ge(turned, 2 * t + 1)
                if t >= 2:
                    act.wait_ge(q_done, t - 1)
                nc.scalar.activation(srcT[t % 2][:, :, :], p_T[0][:, :].rearrange("p (c n) -> p c n", c=KB), ACT.Copy
                                     ).then_inc(turned_out, 1)
                act.wait_ge(turned, 2 * t + 2)
                nc.scalar.activation(k.dst_rows_sb[:, t, :], p_T[1][:, :], ACT.Copy).then_inc(turned_out, 1)

            turn_out(0)
            for t in range(T):
                if t >= 2:
                    act.wait_ge(cand_done, t - 1)
                same = k.same_src[:, t, :] if t < T - 1 else k.same_src_last[:, :]
                nc.scalar.activation(away[t % 2][:, :], same, ACT.Copy, bias=-BIG, scale=BIG).then_inc(away_done, 1)
                act.wait_ge(q_done, t + 1)
                if t >= 2:
                    act.wait_ge(prod_done, t - 1)
                nc.scalar.activation(q[t % 2][:, :], p_q[:, :], ACT.Copy, scale=float(HD) ** -0.5).then_inc(q_out, 1)
                if t + 1 < T:
                    turn_out(t + 1)
                if t:
                    plain_row(nc, k, act, PLAIN + t - 1)

        @block.vector
        def _(dve):
            def merge(t):
                dve.wait_ge(known_in, 16 * (t + 1))
                nc.vector.tensor_tensor(known[t % 2][:, :], known[t % 2][:, :], tile_max[t % 2][:, :], ALU.max
                                        ).then_inc(merged, 1)

            def tile_maximum(t):
                dve.wait_ge(spread, t + 1)
                dve.wait_ge(away_done, t + 1)
                if t:
                    dve.wait_ge(tile_max_done, t)
                nc.vector.tensor_tensor(cand[:, :, :], p_all[:, :, :],
                                        away[t % 2][:, :].rearrange("p (a e) -> p a e", a=1)
                                        .to_broadcast([P, HEADS, P]), ALU.add).then_inc(cand_done, 1)
                dve.wait_ge(cand_done, t + 1)
                if t >= 2:
                    dve.wait_ge(merged, t - 1)
                nc.vector.tensor_reduce(tile_max[t % 2][:, :], cand[:, :, :], AX_X, ALU.max).then_inc(tile_max_done, 1)
                dve.wait_ge(tile_max_done, t + 1)

            for t in range(T + 1):
                if t < T:
                    dve.wait_ge(k_done, t + 1)
                    dve.wait_ge(q_out, t + 1)
                    if t:
                        dve.wait_ge(aw_done, t)
                    nc.vector.tensor_tensor(prod[:, :], p_k[:, :], q[t % 2][:, :], ALU.mult).then_inc(prod_done, 1)
                    dve.wait_ge(prod_done, t + 1)
                    nc.vector.tensor_reduce(k.scores[:, t, :], prod[:, :].rearrange("p (h f) -> p h f", h=HEADS), AX_X,
                                            ALU.add).then_inc(aw_done, 1)
                if t:
                    tile_maximum(t - 1)
                    merge(t - 1)
                if t < T:
                    dve.wait_ge(aw_turned, t + 1)
                    if t:
                        dve.wait_ge(spread, t)
                    nc.vector.tensor_tensor(
                        diag[:, :, :], p_w[:, :].rearrange("h (a e) -> h a e", a=1).to_broadcast([HEADS, HEADS, P]),
                        k.ident[0:HEADS, 0:HEADS].rearrange("h (g a) -> h g a", a=1).to_broadcast([HEADS, HEADS, P]),
                        ALU.mult).then_inc(diag_done, 1)
                    plain_norm(nc, k, dve, PLAIN + t)

        @block.gpsimd
        def _(pool):
            plain_scale(nc, k, pool, PLAIN)
            for t in range(T):
                if t:
                    pool.wait_ge(max_gone, 16 * t)
                pool.indirect_dma_start(known[t % 2][:, :], None, k.max3[:, :], at_rows(k.index[:, 0, t:t + 1])
                                        ).then_inc(known_in, 16)
                if t:
                    plain_row_scale(nc, k, pool, PLAIN + t - 1)
                if t + 1 < T:
                    plain_scale(nc, k, pool, PLAIN + t + 1)
                pool.wait_ge(merged, t + 1)
                pool.indirect_dma_start(k.max3[:, :], at_rows(k.unique[:, 0, t:t + 1]), known[t % 2][:, :], None
                                        ).then_inc(max_gone, 16)
            pool.wait_ge(max_gone, 16 * T)


def values_phase(nc, k):
    with phase(nc, "v_") as (sb, ps, sem), ExitStack() as ctx:
        T = EDGE_TILES
        top = sb("top", [P, T, HEADS])
        weight = sb("weight", [P, T, HEADS])
        both = [sb(f"both{i}", [P, ATT]) for i in range(2)]
        tile_sum = [sb(f"tile_sum{i}", [P, ATT]) for i in range(2)]
        PLAIN = 3 * T
        p_v, p_S, p_W = ([ps(f"p_{n}{i}", [P, D]) for i in range(2)] for n in "vSW")
        top_in = [sem(f"top_in{i}") for i in range(4)]
        v_done, less, weighed, weights_in, both_done, s_done, s_out, scattered = (
            sem(n) for n in ("done", "less", "weighed", "weights_in", "both", "s_done", "s_out", "scattered"))
        block = ctx.enter_context(nc.Block())

        @block.sync
        def _(sp):
            for i in range(PLAIN, PLAIN + T):
                plain_load(nc, k, sp, i)
                plain_store(nc, k, sp, i - 2)
            for i in range(PLAIN + T - 2, PLAIN + T):
                plain_store(nc, k, sp, i)
            for b in range(2):
                sp.wait_ge(k.plain_gone[b], 16 * (NODE_TILES // 2))

        @block.gpsimd
        def _(pool):
            for t in range(T):
                if t >= 4:
                    pool.wait_ge(top_in[t % 4], 16 * (t // 4))
                pool.indirect_dma_start(top[:, t, :], None, k.max3[:, :], at_rows(k.index[:, 0, t:t + 1])
                                        ).then_inc(top_in[t % 4], 16)
            for t in range(T):
                plain_scale(nc, k, pool, PLAIN + t)
                plain_row_scale(nc, k, pool, PLAIN + t - 1)
                pool.wait_ge(s_out, 2 * t + 2)
                if t:
                    pool.wait_ge(scattered, 16 * t)
                pool.indirect_dma_start(k.sum3[:, :], at_rows(k.unique[:, 0, t:t + 1]), tile_sum[t % 2][:, :], None,
                                        compute_op=ALU.add).then_inc(scattered, 16)
            plain_row_scale(nc, k, pool, PLAIN + T - 1)
            pool.wait_ge(scattered, 16 * T)

        @block.tensor
        def _(pe):
            def tile_sums(t):
                pe.wait_ge(both_done, t + 1)
                pe.wait_ge(weights_in, t + 1)
                if t >= 2:
                    pe.wait_ge(s_out, 2 * t - 2)
                nc.tensor.matmul(p_S[t % 2][:, :], k.same_src[:, t, :], both[t % 2][:, 0:D], start=True, stop=True)
                nc.tensor.matmul(p_W[t % 2][:, 0:HEADS], k.same_src[:, t, :], both[t % 2][:, D:ATT], start=True,
                                 stop=True).then_inc(s_done, 1)

            for t in range(T):
                if t >= 2:
                    pe.wait_ge(both_done, t - 1)
                for c in range(KB):
                    last = nc.tensor.matmul(p_v[t % 2][:, :], k.dst_rows_sb[:, t, c * P:(c + 1) * P], k.wv[:, c, :],
                                            start=(c == 0), stop=(c == KB - 1))
                last.then_inc(v_done, 1)
                if t:
                    tile_sums(t - 1)
            tile_sums(T - 1)

        @block.vector
        def _(dve):
            for t in range(T):
                dve.wait_ge(top_in[t % 4], 16 * (t // 4 + 1))
                nc.vector.tensor_tensor(top[:, t, :], k.scores[:, t, :], top[:, t, :], ALU.subtract).then_inc(less, 1)
            for t in range(T):
                dve.wait_ge(v_done, t + 1)
                dve.wait_ge(weighed, t + 1)
                if t >= 2:
                    dve.wait_ge(s_done, t - 1)
                nc.vector.tensor_copy(both[t % 2][:, D:ATT], weight[:, t, :]).then_inc(weights_in, 1)
                nc.vector.tensor_tensor(
                    both[t % 2][:, 0:D].rearrange("p (h f) -> p h f", h=HEADS),
                    p_v[t % 2][:, :].rearrange("p (h f) -> p h f", h=HEADS),
                    weight[:, t, :].rearrange("p (h a) -> p h a", a=1).to_broadcast([P, HEADS, HD]), ALU.mult
                    ).then_inc(both_done, 1)
                plain_norm(nc, k, dve, PLAIN + t)

        @block.scalar
        def _(act):
            for t in range(T):
                act.wait_ge(less, t + 1)
                nc.scalar.activation(weight[:, t, :], top[:, t, :], ACT.Exp).then_inc(weighed, 1)
            for t in range(T):
                act.wait_ge(s_done, t + 1)
                if t >= 2:
                    act.wait_ge(scattered, 16 * (t - 1))
                nc.scalar.activation(tile_sum[t % 2][:, 0:D], p_S[t % 2][:, :], ACT.Copy).then_inc(s_out, 1)
                nc.scalar.activation(tile_sum[t % 2][:, D:ATT], p_W[t % 2][:, 0:HEADS], ACT.Copy).then_inc(s_out, 1)
                plain_row(nc, k, act, PLAIN + t - 1)
            plain_row(nc, k, act, PLAIN + T - 1)


def attended_rows_phase(nc, k):
    with phase(nc, "o_") as (sb, ps, sem), ExitStack() as ctx:
        T = EDGE_TILES
        sums = [sb(f"sums{i}", [P, ATT]) for i in range(4)]
        inv = [sb(f"inv{i}", [P, HEADS]) for i in range(2)]
        y, out = ([sb(f"{n}{i}", [P, D]) for i in range(2)] for n in ("y", "out"))
        stats, mv, small = ([sb(f"{n}{i}", [P, w]) for i in range(2)] for n, w in (("stats", 6), ("mv", 2), ("small", 4)))
        sums_in = [sem(f"sums_in{i}") for i in range(4)]
        inv_done, att, y_done, st, mv_done, sc, out_done, gone = (
            sem(n) for n in ("inv", "att", "y", "st", "mv", "sc", "out", "gone"))
        block = ctx.enter_context(nc.Block())

        @block.gpsimd
        def _(pool):
            def gather(t):
                if t >= 4:
                    pool.wait_ge(att, t - 3)
                pool.indirect_dma_start(sums[t % 4][:, :], None, k.sum3[:, :], at_rows(k.index[:, 0, t:t + 1])
                                        ).then_inc(sums_in[t % 4], 16)

            for t in range(3):
                gather(t)
            for t in range(T + 2):
                if t + 3 < T:
                    gather(t + 3)
                if t < T:
                    b = t % 2
                    pool.wait_ge(mv_done, t + 1)
                    if t >= 2:
                        pool.wait_ge(out_done, t - 1)
                    row_scale(pool, k, mv[b][:, 1:2], mv[b][:, 0:1], small[b][:, 0:1], small[b][:, 1:2],
                              small[b][:, 2:3], sc, 3 * t)
                if 0 <= t - 1 < T:
                    pool.wait_ge(out_done, t)
                    if t >= 2:
                        pool.wait_ge(gone, 16 * (t - 1))
                    pool.indirect_dma_start(k.out[:, :], at_rows(k.unique[:, 0, t - 1:t]), out[(t - 1) % 2][:, :], None
                                            ).then_inc(gone, 16)
            pool.wait_ge(gone, 16 * T)

        @block.vector
        def _(dve):
            for t in range(T):
                b = t % 2
                dve.wait_ge(sums_in[t % 4], 16 * (t // 4 + 1))
                if t >= 2:
                    dve.wait_ge(att, t - 1)
                nc.vector.reciprocal(inv[b][:, :], sums[t % 4][:, D:ATT]).then_inc(inv_done, 1)
                dve.wait_ge(inv_done, t + 1)
                if t >= 2:
                    dve.wait_ge(out_done, t - 1)
                nc.vector.tensor_tensor(
                    y[b][:, :].rearrange("p (h f) -> p h f", h=HEADS),
                    sums[t % 4][:, 0:D].rearrange("p (h f) -> p h f", h=HEADS),
                    inv[b][:, :].rearrange("p (h a) -> p h a", a=1).to_broadcast([P, HEADS, HD]), ALU.mult
                    ).then_inc(att, 1)
                dve.wait_ge(att, t + 1)
                nc.vector.tensor_tensor(y[b][:, :], y[b][:, :], k.src_rows_sb[:, t, :], ALU.add).then_inc(y_done, 1)
                dve.wait_ge(y_done, t + 1)
                nc.vector.bn_stats(stats[b][:, :], y[b][:, :]).then_inc(st, 1)
                dve.wait_ge(st, t + 1)
                if t >= 2:
                    dve.wait_ge(sc, 3 * t - 3)
                nc.vector.bn_aggr(mv[b][:, :], stats[b][:, :]).then_inc(mv_done, 1)

        @block.scalar
        def _(act):
            for t in range(T):
                b = t % 2
                act.wait_ge(sc, 3 * t + 3)
                if t >= 2:
                    act.wait_ge(gone, 16 * (t - 1))
                nc.scalar.activation(out[b][:, :], y[b][:, :], ACT.Identity, bias=small[b][:, 2:3],
                                     scale=small[b][:, 1:2]).then_inc(out_done, 1)


TABLES = [("sum0", D), ("x1", D), ("p", D), ("sum2", 8 * F), ("sum3", ATT), ("max3", HEADS)]
PASSED = ["L0_gnn_W1", "L0_gnn_b1", "L0_gnn_W2", "L0_gnn_b2", "L0_gnn_W3", "L0_gnn_b3", "L0_gnn_W4", "L0_gnn_b4",
          "L0_gnn_gamma", "L0_gnn_beta", "L1_gnn_W_l", "L1_gnn_b_l", "L1_gnn_W_r", "L1_gnn_gamma", "L1_gnn_beta",
          "L2_gnn_w_in2f_s", "L2_gnn_w_in2f_v", "L2_gnn_W1", "L2_gnn_b1", "L2_gnn_W2", "L2_gnn_b2",
          "L2_gnn_w_f2o1_s", "L2_gnn_w_f2o1_v", "L2_gnn_w_f2o2_s", "L2_gnn_w_f2o2_v", "L3_gnn_W"]
DEBUG = 0


def build(nc, args, out, debug=None):
    k = Shared()
    k.nc, k.out = nc, out
    k.x = args["x"]
    k.xT = args["xT"]
    k.src_cols = args["src_cols"]
    k.dst_cols = args["dst_cols"]
    k.src_rows = args["src_rows"]
    k.dst_rows = args["dst_rows"]
    k.f64T = args["edge_attr_64T"]
    k.f20T = args["edge_attr_20T"]
    k.y4 = args["edge_attr_4t"]
    k.cut = args["edge_weight_t"]
    k.L0_W1 = args["L0_gnn_W1"]
    k.L0_b1 = args["L0_gnn_b1"]
    k.L0_W2 = args["L0_gnn_W2"]
    k.L0_b2 = args["L0_gnn_b2"]
    k.L0_W3 = args["L0_gnn_W3"]
    k.L0_b3 = args["L0_gnn_b3"]
    k.L0_W4 = args["L0_gnn_W4"]
    k.L0_b4 = args["L0_gnn_b4"]
    k.L0_gamma = args["L0_gnn_gamma"]
    k.L0_beta = args["L0_gnn_beta"]
    k.L1_Wl = args["L1_gnn_W_l"]
    k.L1_bl = args["L1_gnn_b_l"]
    k.L1_Wr = args["L1_gnn_W_r"]
    k.L1_gamma = args["L1_gnn_gamma"]
    k.L1_beta = args["L1_gnn_beta"]
    k.L2_ws = args["L2_gnn_w_in2f_s"]
    k.L2_wv = args["L2_gnn_w_in2f_v"]
    k.L2_W1 = args["L2_gnn_W1"]
    k.L2_b1 = args["L2_gnn_b1"]
    k.L2_W2 = args["L2_gnn_W2"]
    k.L2_b2 = args["L2_gnn_b2"]
    k.L2_o1s = args["L2_gnn_w_f2o1_s"]
    k.L2_o1v = args["L2_gnn_w_f2o1_v"]
    k.L2_o2s = args["L2_gnn_w_f2o2_s"]
    k.L2_o2v = args["L2_gnn_w_f2o2_v"]
    k.L3_W = args["L3_gnn_W"]
    kinds = debug or {}
    k.sum0, k.x1, k.p, k.sum2, k.sum3, k.max3 = (
        kinds.get(name) if name in kinds else nc.dram_tensor(name, [ROWS, width], F32).ap() for name, width in TABLES)
    with ExitStack() as ctx:
        ctx.enter_context(nc.allow_non_contiguous_dma(reason="bias columns and strided weights"))
        sb = lambda name, shape, dt=F32: ctx.enter_context(nc.sbuf_tensor(name, shape, dt))
        sem = lambda name: ctx.enter_context(nc.semaphore(name))
        k.ident, k.ones, k.minus_half = sb("ident", [P, P]), sb("ones", [P, P]), sb("minus_half", [P, 4])
        k.index, k.unique = sb("index", [P, 2, EDGE_TILES], I32), sb("unique", [P, 2, EDGE_TILES], I32)
        k.inv_degree, k.share = sb("inv_degree", [P, EDGE_TILES]), sb("share", [P, EDGE_TILES])
        k.same_src, k.same_dst = sb("same_src", [P, EDGE_TILES, P]), sb("same_dst", [P, EDGE_TILES, P])
        k.same_src_last = sb("same_src_last", [P, P])
        k.filters = sb("filters", [P, EDGE_TILES, 8, F])
        k.filters_done, k.dense_weights_in, k.acc_zero, k.half_set, k.passed_dve, k.passed_pool = sem("filters_done"), sem("dense_weights_in"), sem("acc_zero"), sem("half_set"), sem("passed_dve"), sem("passed_pool")
        setup_phase(nc, k)
        k.column_acc = sb("column_acc", [P, 2, D])
        with ExitStack() as dense:
            sbd = lambda name, shape: dense.enter_context(nc.sbuf_tensor(name, shape, F32))
            k.w3a, k.w4 = sbd("w3a", [P, KB, D]), sbd("w4", [P, KB, D])
            k.b4_row, k.gamma0_row, k.beta0_row = sbd("b4_row", [P, D]), sbd("gamma0_row", [P, D]), sbd("beta0_row", [P, D])
            message_phase(nc, k)
            dense_phase(nc, k)
        k.bn_scale, k.bn_shift = sb("bn_scale", [P, D]), sb("bn_shift", [P, D])
        k.src_rows_sb, k.dst_rows_sb = sb("src_rows_sb", [P, EDGE_TILES, D]), sb("dst_rows_sb", [P, EDGE_TILES, D])
        k.scores = sb("scores", [P, EDGE_TILES, HEADS])
        aggregate_phase(nc, k)
        edge_rows_phase(nc, k)
        k.plain_p_rows, k.plain_x1_rows, k.plain_y_rows = (
            [sb(f"plain_{n}{i}", [P, D]) for i in range(2)] for n in ("p", "x1", "y"))
        k.plain_stats, k.plain_mv, k.plain_small = (
            [sb(f"plain_{n}{i}", [P, w]) for i in range(2)] for n, w in (("stats", 6), ("mv", 2), ("small", 4)))
        k.plain_p_in, k.plain_x1_in, k.plain_gone = (
            [sem(f"plain_{n}{i}") for i in range(2)] for n in ("p_in", "x1_in", "gone"))
        k.plain_scaled, k.plain_shifted, k.plain_leaky, k.plain_y, k.plain_st, k.plain_mv_done, k.plain_sc, k.plain_out = (
            sem("plain_" + n) for n in ("scaled", "shifted", "leaky", "y_done", "st", "mv_done", "sc", "out"))
        equivariant_phase(nc, k)
        k.wv = sb("wv", [P, KB, D])
        scores_phase(nc, k)
        values_phase(nc, k)
        attended_rows_phase(nc, k)


def kernel(**inputs):
    import concourse.bacc as _bacc
    from concourse.bass_utils import run_bass_kernel_spmd as _run

    a = {n: np.asarray(v) for n, v in inputs.items()}

    def edges(v):
        return np.concatenate([v[:(EDGE_TILES - 1) * P], v[LAST_START:]])

    x = np.zeros((ROWS, D), a["x"].dtype)
    x[:N] = a["x"]
    arrays = {
        "x": x,
        "xT": np.ascontiguousarray(x.reshape(NODE_TILES, P, KB, P).transpose(0, 3, 2, 1)).reshape(ROWS, D),
        "edge_attr_64T": np.ascontiguousarray(edges(a["edge_attr_64"]).T),
        "edge_attr_20T": np.ascontiguousarray(edges(a["edge_attr_20"]).T),
        "edge_attr_4t": np.ascontiguousarray(edges(a["edge_attr_4"]).reshape(EDGE_TILES, P, 4).transpose(1, 0, 2)),
        "edge_weight_t": np.ascontiguousarray(edges(a["edge_weight"]).reshape(EDGE_TILES, P).T),
    }
    for n in ("src", "dst"):
        arrays[f"{n}_rows"] = edges(a[n]).reshape(1, -1)
        arrays[f"{n}_cols"] = np.ascontiguousarray(edges(a[n]).reshape(EDGE_TILES, P).T)
    for n in PASSED:
        arrays[n] = np.ascontiguousarray(a[n])

    nc = _bacc.Bacc("TRN2", target_bir_lowering=False, num_devices=1)
    args = {n: nc.dram_tensor(f"in_{n}", v.shape, mybir.dt.from_np(v.dtype), kind="ExternalInput").ap()
            for n, v in arrays.items()}
    out = nc.dram_tensor("out_rows", [ROWS, D], F32, kind="ExternalOutput").ap()
    debug = {n: nc.dram_tensor(n, [ROWS, w], F32, kind="ExternalOutput").ap() for n, w in TABLES} if DEBUG else None
    build(nc, args, out, debug)
    r = _run(nc, [{f"in_{n}": v for n, v in arrays.items()}], core_ids=[0])
    return r.results[0]["out_rows"][:N]
```

```python
from contextlib import ExitStack, contextmanager

import numpy as np

import concourse.bass as bass
from concourse import mybir

F32 = mybir.dt.float32
I32 = mybir.dt.int32
ALU = mybir.AluOpType
ACT = mybir.ActivationFunctionType
AX_X = mybir.AxisListType.X

P = 128
N = 10000
D = 512
KB = D // P
E = 2500
EDGE_TILES = -(-E // P)
LAST_START = E - P
OVERLAP = (EDGE_TILES - 1) * P - LAST_START
ROWS = 10240
NODE_TILES = ROWS // P
LAST_VALID_TILE = N // P
GROUP = 4
GROUPS = EDGE_TILES // GROUP
EDGE64, EDGE20 = 64, 20
F = 32
B = 128
HEADS = 8
HD = D // HEADS
ATT = D + HEADS
LN_EPS = 1e-5
LOG2 = 0.6931471805599453
BIG = 3.0e38


class Shared:
    pass


def at_rows(index_column):
    return bass.IndirectOffsetOnAxis(ap=index_column, axis=0)


def message_phase(nc, k):
    with phase(nc, "m_") as (sb, ps, sem), ExitStack() as ctx:

        w1 = sb("w1", [P, 2 * KB, D])
        w1a = sb("w1a", [EDGE64, D])
        w2 = sb("w2", [P, KB, D])
        w3b = sb("w3b", [P, KB, D])
        bias = sb("bias", [P, 2, KB])
        attrT = [sb(f"attrT{i}", [EDGE64, D]) for i in range(2)]
        x_in = sb("x_in", [P, 2, 2, D])
        xT = sb("xT", [P, 2, 2, KB, D])
        hidT = [sb("hid1T", [P, 2, KB, D]), sb("hid2T", [P, 2, KB, D])]
        h = sb("h", [P, 2, D])
        den = sb("den", [P, 2, D])
        rec = sb("rec", [P, 2, D])
        msg = sb("msg", [P, 2, D])
        tile_sum = sb("tile_sum", [P, 2, D])
        p_T = [ps(f"p_T{i}", [P, D]) for i in range(2)]
        p_H = [ps(f"p_H{i}", [P, D]) for i in range(3)]
        p_F = ps("p_F", [P, D])
        p_C = ps("p_C", [P, D])
        p_S = ps("p_S", [P, D])

        PARTS, FILLS = 4, 10
        row_i = sb("row_i", [P, E], I32)
        col_f = sb("col_f", [P, 2, EDGE_TILES])
        repeated, unique_f = sb("repeated", [P, 2, EDGE_TILES]), sb("unique_f", [P, 2, EDGE_TILES])
        counted = sb("counted", [P, E // PARTS])
        masked = counted[:, 0:GROUP * P].rearrange("p (t e) -> p t e", t=GROUP)
        degree = sb("degree", [P, PARTS, EDGE_TILES])
        earlier = sb("earlier", [P, P])
        dummy_i, dummy_f = sb("dummy_i", [P, 1], I32), sb("dummy_f", [P, 1])
        b3_row = tile_sum[:, 0, :]
        f20T = [sb(f"f20T{i}", [EDGE20, D]) for i in range(2)]
        w1e, b1e, w2e = sb("w1e", [EDGE20, F]), sb("b1e", [F, 1]), sb("w2e", [F + 1, 6 * F])
        y4, cut = sb("y4", [P, EDGE_TILES, 4]), sb("cut", [P, EDGE_TILES])
        mag = sb("mag", [F, D])
        hT = sb("hT", [F + 1, D])
        wf = sb("wf", [P, 4, F])

        rows_in, cols_in, b3_in, filt_in, sum0_set = (
            sem("rows_in"), sem("cols_in"), sem("b3_in"), sem("filt_in"), sem("sum0_set"))
        attr_in, f20_in = [sem(f"attr_in{i}") for i in range(2)], [sem(f"f20_in{i}") for i in range(2)]
        const_done, v, src_rows_used, unique_done = sem("const"), sem("setup_v"), sem("src_rows_used"), sem("unique")
        pre_h, act_h, pos_done, h20_done, pre_w = sem("pre_h"), sem("act_h"), sem("pos"), sem("h20"), sem("pre_w")
        w_in, w2_in, w3_in, small_in = sem("w1_in"), sem("w2_in"), sem("w3_in"), sem("small_in")
        gathered = [sem(f"gathered{i}") for i in range(2)]
        turned, turned_out = sem("turned"), sem("turned_out")
        pre, h_done, exp_done, den_done, rec_done, step_done, hid_done = (
            sem("pre"), sem("h"), sem("exp"), sem("den"), sem("rec"), sem("step"), sem("hid"))
        c_done, c_out, s_done, s_out, scattered = (
            sem("c_done"), sem("c_out"), sem("s_done"), sem("s_out"), sem("scattered0"))

        slots = []
        for it in range(GROUPS + 2):
            slots += [(0, it, q) for q in range(GROUP) if it < GROUPS]
            slots += [(1, it - 1, q) for q in range(GROUP) if it >= 1]
        chunk = {}
        for layer, g, q in slots:
            if g < GROUPS:
                chunk[layer, g, q] = len(chunk)
        CHUNKS = len(chunk)
        STEPS = CHUNKS // GROUPS
        EARLY = 5

        def hid_buf(layer, g):
            return hidT[layer][:, g % hidT[layer].shape[1], :, :]

        block = ctx.enter_context(nc.Block())

        @block.sync
        def _(sp):
            sp.dma_start(k.index[:, 0, :], k.src_cols).then_inc(cols_in, 16)
            sp.dma_start(k.index[:, 1, :], k.dst_cols).then_inc(cols_in, 16)
            sp.dma_start(w1[:, :, :], k.L0_W1[0:2 * D, :].rearrange("(c p) n -> p c n", p=P)).then_inc(w_in, 16)
            sp.dma_start(w1a[:, :], k.L0_W1[2 * D:2 * D + EDGE64, :]).then_inc(w_in, 16)

            def load_group(g):
                if g >= 2:
                    sp.wait_ge(pre, chunk[0, g - 2, GROUP - 1] + 1)
                sp.dma_start(attrT[g % 2][:, :], k.f64T[:, g * D:(g + 1) * D]).then_inc(attr_in[g % 2], 16)
                if g >= 2:
                    sp.wait_ge(pre_h, g - 1)
                sp.dma_start(f20T[g % 2][:, :], k.f20T[:, g * D:(g + 1) * D]).then_inc(f20_in[g % 2], 16)

            load_group(0)
            load_group(1)
            sp.dma_start(w2[:, :, :], k.L0_W2.rearrange("(c p) n -> p c n", p=P)).then_inc(w2_in, 16)
            sp.dma_start(w3b[:, :, :], k.L0_W3[D:2 * D, :].rearrange("(c p) n -> p c n", p=P)).then_inc(w3_in, 16)
            sp.wait_ge(b3_in, 16)
            some = NODE_TILES // FILLS
            for part in range(FILLS):
                sp.wait_ge(pre, part + 1)
                sp.dma_start(k.sum0.rearrange("(p n) d -> p n d", p=P)[:, part * some:(part + 1) * some, :],
                             b3_row.rearrange("p (a d) -> p a d", a=1).to_broadcast([P, some, D])
                             ).then_inc(sum0_set, 16)
            for g in range(2, GROUPS):
                load_group(g)
            sp.dma_start(k.w3a[:, :, :], k.L0_W3[0:D, :].rearrange("(c p) n -> p c n", p=P)).then_inc(k.w3a_in, 16)

        @block.gpsimd
        def _(pool):
            pool.memset(k.ones[:, :], 1.0).then_inc(const_done, 1)
            pool.memset(k.ident[:, :], 0.0).then_inc(const_done, 1)
            pool.memset(k.minus_half[:, :], -0.5).then_inc(k.half_set, 1)
            pool.iota(dummy_i[:, :], [[0, 1]], base=N, channel_multiplier=1).then_inc(const_done, 1)
            pool.wait_ge(const_done, 3)
            pool.affine_select(out=k.ident[:, :], in_=k.ident[:, :], compare_op=ALU.not_equal, fill=1.0,
                               base=0, pattern=[[-1, P]], channel_multiplier=1).then_inc(const_done, 1)
            pool.affine_select(out=earlier[:, :], in_=k.ones[:, :], compare_op=ALU.is_gt, fill=0.0,
                               base=0, pattern=[[-1, P]], channel_multiplier=1).then_inc(const_done, 1)

            def gather(t):
                if t >= 2:
                    pool.wait_ge(turned, 2 * (t - 1))
                for s in range(2):
                    pool.indirect_dma_start(
                        x_in[:, t % 2, s, :], None, k.x[:, :],
                        at_rows(k.index[:, s, t:t + 1])).then_inc(gathered[t % 2], 16)

            def finish_chunk(c, layer, g, q):
                pool.wait_ge(step_done, c + 1)
                if layer == 0 and g >= 2:
                    pool.wait_ge(pre, chunk[1, g - 2, GROUP - 1] + 1)
                if layer == 1 and g >= 2:
                    pool.wait_ge(c_done, GROUP * (g - 1))
                nc.gpsimd.tensor_tensor(hid_buf(layer, g)[:, q, :], rec[:, c % 2, :], h[:, c % 2, :],
                                        ALU.add).then_inc(hid_done, 1)

            def scatter(n):
                pool.wait_ge(s_out, n + 1)
                if n >= 1:
                    pool.wait_ge(scattered, 16 * n)
                else:
                    pool.wait_ge(sum0_set, 16 * FILLS)
                    pool.wait_ge(unique_done, 1)
                pool.indirect_dma_start(
                    k.sum0[:, :], at_rows(k.unique[:, 1, n:n + 1]),
                    tile_sum[:, n % 2, :], None, compute_op=ALU.add).then_inc(scattered, 16)

            pool.wait_ge(cols_in, 32)
            for t in range(GROUP + 1):
                gather(t)
            for i, (layer, g, q) in enumerate(slots):
                if i and slots[i - 1] in chunk:
                    finish_chunk(chunk[slots[i - 1]], *slots[i - 1])
                if layer == 0:
                    t = GROUP * (g + 1) + q + 1
                    if t < EDGE_TILES:
                        gather(t)
                elif g >= 1:
                    n = GROUP * (g - 1) + q - 1
                    if n >= 0:
                        scatter(n)
            scatter(EDGE_TILES - 1)
            pool.wait_ge(scattered, 16 * EDGE_TILES)

        @block.tensor
        def _(pe):
            def turn(t):
                pe.wait_ge(gathered[t % 2], 32 * (t // 2 + 1))
                for s in range(2):
                    if 2 * t + s >= 2:
                        pe.wait_ge(turned_out, 2 * t + s - 1)
                    for c in range(KB):
                        last = pe.transpose(p_T[s][:, c * P:(c + 1) * P], x_in[:, t % 2, s, c * P:(c + 1) * P],
                                            k.ident[:, :])
                    last.then_inc(turned, 1)

            def tile_sums(n):
                pe.wait_ge(c_out, n + 1)
                if n >= 1:
                    pe.wait_ge(s_out, n)
                pe.matmul(p_S[:, :], k.same_dst[:, n, :], msg[:, n % 2, :], start=True, stop=True
                          ).then_inc(s_done, 1)

            def filter_hidden(g):
                pe.wait_ge(f20_in[g % 2], 16 * (g // 2 + 1))
                if g:
                    pe.wait_ge(k.filters_done, GROUP * g)
                else:
                    pe.wait_ge(filt_in, 16 * 6)
                pe.matmul(p_F[0:F, :], w1e[:, :], f20T[g % 2][:, :], start=True, stop=True).then_inc(pre_h, 1)

            def filter_output(g):
                pe.wait_ge(act_h, 3 * g + 1)
                pe.wait_ge(h20_done, g + 1)
                pe.wait_ge(v, 1)
                for j in range(GROUP):
                    last = pe.matmul(p_F[:, j * P:(j + 1) * P].rearrange("p (c f) -> p c f", c=4),
                                     hT[:, j * P:(j + 1) * P],
                                     w2e[:, :].rearrange("k (f c) -> k c f", c=6)[:, 0:4, :], start=True, stop=True)
                last.then_inc(pre_w, 1)

            pe.wait_ge(const_done, 5)
            for t in range(GROUP):
                turn(t)
            pe.wait_ge(w_in, 32)
            for layer, g, q in slots:
                if g < GROUPS:
                    c = chunk[layer, g, q]
                    if c >= 3:
                        pe.wait_ge(h_done, c - 2)
                    out = p_H[c % 3][:, :]
                    cols = slice(q * P, (q + 1) * P)
                    if layer == 0:
                        pe.wait_ge(turned_out, 2 * GROUP * (g + 1))
                        for s in range(2):
                            for b in range(KB):
                                pe.matmul(out, w1[:, s * KB + b, cols], xT[:, g % 2, s, b, :],
                                          start=(s == 0 and b == 0), stop=False)
                        pe.wait_ge(attr_in[g % 2], 16 * (g // 2 + 1))
                        pe.matmul(out, w1a[:, cols], attrT[g % 2][:, :], start=False, stop=True).then_inc(pre, 1)
                        if g + 1 < GROUPS:
                            turn(GROUP * (g + 1) + q)
                    else:
                        pe.wait_ge(w2_in, 16)
                        pe.wait_ge(hid_done, chunk[0, g, GROUP - 1] + 1)
                        for b in range(KB):
                            last = pe.matmul(out, w2[:, b, cols], hid_buf(0, g)[:, b, :],
                                             start=(b == 0), stop=(b == KB - 1))
                        last.then_inc(pre, 1)
                    if c % STEPS == 1:
                        filter_hidden(c // STEPS)
                    if c % STEPS == 5:
                        filter_output(c // STEPS)
                if layer == 1 and g >= 1:
                    n = GROUP * (g - 1) + q
                    if n == 0:
                        pe.wait_ge(unique_done, 1)
                    pe.wait_ge(w3_in, 16)
                    pe.wait_ge(hid_done, chunk[1, g - 1, GROUP - 1] + 1)
                    if n >= 1:
                        pe.wait_ge(c_out, n)
                    for b in range(KB):
                        last = pe.matmul(p_C[:, :], hid_buf(1, g - 1)[:, b, q * P:(q + 1) * P], w3b[:, b, :],
                                         start=(b == 0), stop=(b == KB - 1))
                    last.then_inc(c_done, 1)
                    if n >= 1:
                        tile_sums(n - 1)
            tile_sums(EDGE_TILES - 1)

        @block.scalar
        def _(act):
            def turn_out(t):
                for s in range(2):
                    g = t // GROUP
                    act.wait_ge(turned, 2 * t + s + 1)
                    if g >= 2:
                        act.wait_ge(pre, chunk[0, g - 2, GROUP - 1] + 1)
                    nc.scalar.activation(xT[:, g % 2, s, :, (t % GROUP) * P:(t % GROUP + 1) * P],
                                         p_T[s][:, :].rearrange("p (c e) -> p c e", c=KB), ACT.Copy
                                         ).then_inc(turned_out, 1)

            def message_out(n):
                act.wait_ge(c_done, n + 1)
                if n >= 2:
                    act.wait_ge(s_done, n - 1)
                nc.scalar.activation(msg[:, n % 2, :], p_C[:, :], ACT.Copy).then_inc(c_out, 1)

            def sum_out(n):
                act.wait_ge(s_done, n + 1)
                if n == 0:
                    act.wait_ge(sum0_set, 16 * FILLS)
                if n >= 2:
                    act.wait_ge(scattered, 16 * (n - 1))
                nc.scalar.activation(tile_sum[:, n % 2, :], p_S[:, :], ACT.Copy).then_inc(s_out, 1)

            def filter_logarithms(g):
                act.wait_ge(pos_done, g + 1)
                for i, (out, in_, func, bias, scale) in enumerate((
                        (mag, p_F[0:F, :], ACT.Abs, b1e[:, 0:1], 1.0),
                        (mag, mag[:, :], ACT.Exp, 0.0, -1.0),
                        (mag, mag[:, :], ACT.Ln, 1.0, 1.0))):
                    if i == 0 and g:
                        act.wait_ge(h20_done, g)
                    nc.scalar.activation(out[:, :], in_, func, bias=bias, scale=scale).then_inc(act_h, 1)
                    act.wait_ge(act_h, 3 * g + i + 1)

            act.dma_start(row_i[:, :], k.src_rows.to_broadcast([P, E])).then_inc(rows_in, 16)
            act.dma_start(b3_row, k.L0_b3.rearrange("(a n) -> a n", a=1).to_broadcast([P, D])).then_inc(b3_in, 16)
            for i, b in enumerate((k.L0_b1, k.L0_b2)):
                for q in range(KB):
                    act.dma_start(bias[:, i, q:q + 1], b[q * P:(q + 1) * P].rearrange("(p a) -> p a", a=1)
                                  ).then_inc(small_in, 16)
            act.dma_start(w1e[:, :], k.L2_W1).then_inc(filt_in, 16)
            act.dma_start(b1e[:, :], k.L2_b1.rearrange("(f a) -> f a", a=1)).then_inc(filt_in, 16)
            act.dma_start(w2e[0:F, :], k.L2_W2).then_inc(filt_in, 16)
            act.dma_start(w2e[F:F + 1, :], k.L2_b2.rearrange("(a f) -> a f", a=1)).then_inc(filt_in, 16)
            act.dma_start(y4[:, :, :], k.y4).then_inc(filt_in, 16)
            act.dma_start(cut[:, :], k.cut).then_inc(filt_in, 16)
            act.wait_ge(src_rows_used, 1)
            act.dma_start(row_i[:, :], k.dst_rows.to_broadcast([P, E])).then_inc(rows_in, 16)
            for t in range(GROUP):
                turn_out(t)
            for layer, g, q in slots:
                if g < GROUPS:
                    c = chunk[layer, g, q]
                    act.wait_ge(h_done, c + 1)
                    if c >= 2:
                        act.wait_ge(rec_done, c - 1)
                    nc.scalar.activation(den[:, c % 2, :], h[:, c % 2, :], ACT.Exp).then_inc(exp_done, 1)
                    act.wait_ge(exp_done, c + 1)
                    nc.scalar.activation(den[:, c % 2, :], den[:, c % 2, :], ACT.Square, bias=1.0
                                         ).then_inc(den_done, 1)
                    act.wait_ge(den_done, 2 * c + 1)
                    nc.scalar.activation(den[:, c % 2, :], den[:, c % 2, :], ACT.Copy, bias=1.0
                                         ).then_inc(den_done, 1)
                if layer == 0 and g + 1 < GROUPS:
                    turn_out(GROUP * (g + 1) + q)
                if layer == 1 and g >= 1:
                    n = GROUP * (g - 1) + q
                    message_out(n)
                    if n >= 1:
                        sum_out(n - 1)
                if g < GROUPS and chunk[layer, g, q] % STEPS == 2:
                    filter_logarithms(chunk[layer, g, q] // STEPS)
            sum_out(EDGE_TILES - 1)

        @block.vector
        def _(dve):
            def divide(c):
                dve.wait_ge(den_done, 2 * c + 2)
                if c >= 2:
                    dve.wait_ge(hid_done, c - 1)
                nc.vector.reciprocal(rec[:, c % 2, :], den[:, c % 2, :]).then_inc(rec_done, 1)
                dve.wait_ge(rec_done, c + 1)
                nc.vector.scalar_tensor_tensor(out=rec[:, c % 2, :], in0=h[:, c % 2, :], scalar=-2.0,
                                               in1=rec[:, c % 2, :], op0=ALU.mult, op1=ALU.mult
                                               ).then_inc(step_done, 1)

            n = [0]

            def step(ins):
                n[0] += 1
                ins.then_inc(v, 1)
                dve.wait_ge(v, n[0])

            def compare(s, same):
                for t in range(EDGE_TILES):
                    start = t * P if t < EDGE_TILES - 1 else LAST_START
                    last = nc.vector.tensor_scalar(same[:, t, :], row_i[:, start:start + P],
                                                   col_f[:, s, t:t + 1], None, ALU.is_equal)
                step(last)
                for g in range(GROUPS):
                    tiles = slice(g * GROUP, (g + 1) * GROUP)
                    step(nc.vector.tensor_tensor(
                        masked, same[:, tiles, :],
                        earlier[:, :].rearrange("p (a e) -> p a e", a=1).to_broadcast([P, GROUP, P]), ALU.mult))
                    step(nc.vector.tensor_reduce(repeated[:, s, tiles], masked, AX_X, ALU.max))
                step(nc.vector.tensor_scalar(unique_f[:, s, :], col_f[:, s, :], dummy_f[:, 0:1], -1.0,
                                             ALU.subtract, ALU.mult))
                step(nc.vector.tensor_tensor(unique_f[:, s, :], unique_f[:, s, :], repeated[:, s, :], ALU.mult))
                step(nc.vector.tensor_tensor(unique_f[:, s, :], unique_f[:, s, :], col_f[:, s, :], ALU.add))
                step(nc.vector.tensor_copy(k.unique[:, s, :], unique_f[:, s, :]))
                if s == 0:
                    step(nc.vector.tensor_copy(k.same_src_last[:, :], same[:, EDGE_TILES - 1, :]))
                step(nc.vector.memset(same[0:OVERLAP, EDGE_TILES - 1, :], 0.0))

            def count(n):
                t, part = n // PARTS, n % PARTS
                step(nc.vector.tensor_scalar(counted[:, :], row_i[:, part * (E // PARTS):(part + 1) * (E // PARTS)],
                                             col_f[:, 1, t:t + 1], None, ALU.is_equal, ALU.add,
                                             accum_out=degree[:, part, t:t + 1]))

            def filter_positive(g):
                dve.wait_ge(pre_h, g + 1)
                if g:
                    dve.wait_ge(pre_w, g)
                nc.vector.tensor_scalar(hT[0:F, :], p_F[0:F, :], b1e[:, 0:1], 0.0, ALU.add, ALU.max
                                        ).then_inc(pos_done, 1)

            def filter_softplus(g):
                dve.wait_ge(pos_done, g + 1)
                dve.wait_ge(act_h, 3 * g + 3)
                nc.vector.scalar_tensor_tensor(out=hT[0:F, :], in0=mag[:, :], scalar=-LOG2,
                                               in1=hT[0:F, :], op0=ALU.add, op1=ALU.add).then_inc(h20_done, 1)
                dve.wait_ge(h20_done, g + 1)

            def filter_tile(t):
                j = t % GROUP
                dve.wait_ge(pre_w, t // GROUP + 1)
                step(nc.vector.tensor_scalar(wf[:, :, :], p_F[:, j * P:(j + 1) * P].rearrange("p (c f) -> p c f", c=4),
                                             cut[:, t:t + 1], float(B) ** -0.5, ALU.mult, ALU.mult))
                a = k.filters[:, t, :, :]
                for c in range(4):
                    nc.vector.tensor_scalar(a[:, c, :], wf[:, 0 if c == 0 else 2, :], y4[:, t, c:c + 1], None, ALU.mult)
                for c in range(1, 4):
                    nc.vector.tensor_scalar(a[:, 3 + c, :], wf[:, 1, :], y4[:, t, c:c + 1], 3.0 ** -0.5,
                                            ALU.mult, ALU.mult)
                nc.vector.tensor_scalar(a[:, 7, :], wf[:, 3, :], y4[:, t, 0:1], None, ALU.mult
                                        ).then_inc(k.filters_done, 1)
                dve.wait_ge(k.filters_done, t + 1)

            step(nc.vector.memset(hT[F:F + 1, :], 1.0))
            dve.wait_ge(cols_in, 32)
            dve.wait_ge(const_done, 5)
            step(nc.vector.tensor_copy(col_f[:, :, :], k.index[:, :, :]))
            step(nc.vector.tensor_copy(dummy_f[:, :], dummy_i[:, :]))
            dve.wait_ge(rows_in, 16)
            compare(0, k.same_src)
            dve.sem_inc(src_rows_used, 1)
            dve.wait_ge(rows_in, 32)
            compare(1, k.same_dst)
            dve.sem_inc(unique_done, 1)
            for counts in range(PARTS * EARLY):
                count(counts)
            dve.wait_ge(filt_in, 16 * 6)
            dve.wait_ge(small_in, 16 * 8)
            for layer, g, q in slots:
                if g < GROUPS:
                    c = chunk[layer, g, q]
                    dve.wait_ge(pre, c + 1)
                    if c >= 2:
                        dve.wait_ge(hid_done, c - 1)
                    nc.vector.tensor_scalar(h[:, c % 2, :], p_H[c % 3][:, :], bias[:, layer, q:q + 1], None,
                                            ALU.add).then_inc(h_done, 1)
                    dve.wait_ge(h_done, c + 1)
                    if c >= 1:
                        divide(c - 1)
                    if c + 1 == CHUNKS:
                        divide(c)
                    if c % STEPS < 6:
                        for _ in range(2):
                            counts += 1
                            count(counts)
                    if c % STEPS == 2:
                        filter_positive(c // STEPS)
                    if c % STEPS == 3:
                        filter_softplus(c // STEPS)
                    if c % STEPS >= 6:
                        first = GROUP * (c // STEPS) + 2 * (c % STEPS - 6)
                        filter_tile(first)
                        filter_tile(first + 1)
            for part in range(1, PARTS):
                step(nc.vector.tensor_tensor(degree[:, 0, :], degree[:, 0, :], degree[:, part, :], ALU.add))
            step(nc.vector.reciprocal(k.inv_degree[:, :], degree[:, 0, :]))
            step(nc.vector.tensor_copy(k.share[:, :], k.inv_degree[:, :]))
            step(nc.vector.memset(k.share[0:OVERLAP, EDGE_TILES - 1:EDGE_TILES], 0.0))


@contextmanager
def phase(nc, prefix):
    sems = []
    with ExitStack() as ctx:
        def sem(name):
            sems.append(nc.alloc_semaphore(prefix + name))
            return sems[-1]
        yield (lambda name, shape, dt=F32: ctx.enter_context(nc.sbuf_tensor(prefix + name, shape, dt)),
               lambda name, shape: ctx.enter_context(nc.psum_tensor(prefix + name, shape, F32)), sem)
    nc.clear_and_free_semaphores(sems)
    nc.all_engine_barrier()


def row_scale(pool, k, var, mean, tmp, rstd, shift, done, base, norms=1):
    factor, add = (1.0, LN_EPS) if norms == 1 else (1.0 + LN_EPS + LN_EPS ** 2, LN_EPS ** 3)
    nc = k.nc
    pool.sem_inc(k.passed_pool, 1)
    nc.gpsimd.tensor_scalar(tmp, var, factor, add, ALU.mult, ALU.add).then_inc(done, 1)
    pool.wait_ge(done, base + 1)
    nc.gpsimd.tensor_tensor(rstd, tmp, k.minus_half[:, 0:1], ALU.pow).then_inc(done, 1)
    pool.wait_ge(done, base + 2)
    pool.sem_inc(k.passed_pool, 1)
    nc.gpsimd.tensor_scalar(shift, mean, rstd, -1.0, ALU.mult, ALU.mult).then_inc(done, 1)


def dense_phase(nc, k):
    with phase(nc, "d_") as (sb, ps, sem), ExitStack() as ctx:
        two = lambda name, shape=(P, D): [sb(f"{name}{i}", list(shape)) for i in range(2)]

        xT, x, z, h, den, rec, u, uT = (two("xT", (P, KB, P)), two("x"), two("z"), two("h"),
                                        two("den"), two("rec"), two("u"), two("uT", (P, KB, P)))
        xb, y, yn, yg, xbeta, zz, x1, x1T, p_row, p_sq = (
            two("xb"), two("y"), two("yn"), two("yg"), two("xbeta"), two("zz"), two("x1"),
            two("x1T", (P, KB, P)), two("p"), two("psq"))
        stats, mv, small = two("stats", (P, 2, 6)), two("mv", (P, 2, 2)), two("small", (P, 2, 4))
        wr, w4 = sb("wr", [P, KB, D]), sb("w4", [P, KB, D])
        b4_row, gamma_row, beta_row = sb("b4_row", [P, D]), sb("gamma_row", [P, D]), sb("beta_row", [P, D])
        zeros, lowest = sb("zeros", [P, ATT]), sb("lowest", [P, HEADS])
        p_h, p_o, p_p = ([ps(f"p_{n}{i}", [P, D]) for i in range(2)] for n in "hop")
        p_uT, p_xT = ps("p_uT", [P, D]), ps("p_xT", [P, D])

        xT_in, x_in, z_in, x1_out, p_out = ([sem(f"{n}{i}") for i in range(2)]
                                            for n in ("xT_in", "x_in", "z_in", "x1_out", "p_out"))
        h_pre, h_done, exp_done, den_done, rec_done, step_done, u_done, u_turned, uT_done = (
            sem(n) for n in ("h_pre", "h_done", "exp", "den", "rec", "step", "u", "u_turned", "uT"))
        o_done, xb_done, y_done, st_done, mv_done, sc_done, yn_done, xbeta_done, yg_done, zz_done = (
            sem(n) for n in ("o", "xb", "y", "st", "mv", "sc", "yn", "xbeta", "yg", "zz"))
        st2_done, mv2_done, sc2_done, x1_done, x1_turned, x1T_done, p_done, row_done, sq_done, acc_done = (
            sem(n) for n in ("st2", "mv2", "sc2", "x1", "x1_turned", "x1T", "pp", "row", "sq", "acc"))

        wr_in, w4_in, rows_in, filled, tables_set = (
            sem("wr_in"), sem("w4_in"), sem("rows_in"), sem("filled"), sem("tables_set"))
        DEPTH, PEELED = 5, 8

        def run(eng, stages):
            def turn(i, par):
                for lag, f in stages:
                    if not isinstance(i, int) or 0 <= i - lag < NODE_TILES:
                        f(i - lag, (par - lag) % 2)
            for i in range(PEELED):
                turn(i, i % 2)
            with eng.Fori(PEELED, NODE_TILES - 2, 2) as i:
                turn(i, 0)
                turn(i + 1, 1)
            for i in range(NODE_TILES - 2, NODE_TILES + DEPTH):
                turn(i, i % 2)

        def landed(i, par):
            return 16 * (i // 2 + 1) if isinstance(i, int) else (i + (2 - par)) * 8

        def rows(table, i):
            return table[bass.ds(i * P, P), :]

        block = ctx.enter_context(nc.Block())

        @block.sync
        def _(sp):
            def load(i, b):
                if not isinstance(i, int) or i >= 2:
                    sp.wait_ge(h_pre, i - 1)
                sp.dma_start(xT[b][:, :, :], k.xT[bass.ds(i * P, P), :].rearrange("p (c n) -> p c n", c=KB)
                             ).then_inc(xT_in[b], 16)
                if not isinstance(i, int) or i >= 2:
                    sp.wait_ge(h_done, i - 1)
                sp.dma_start(z[b][:, :], rows(k.sum0, i)).then_inc(z_in[b], 16)

            def load_x(i, b):
                if not isinstance(i, int) or i >= 2:
                    sp.wait_ge(xbeta_done, i - 1)
                    sp.wait_ge(xb_done, i - 1)
                sp.dma_start(x[b][:, :], rows(k.x, i)).then_inc(x_in[b], 16)

            sp.wait_ge(filled, 2)

            def store_x1(i, b):
                sp.wait_ge(x1_done, i + 1)
                sp.dma_start(rows(k.x1, i), x1[b][:, :]).then_inc(x1_out[b], 16)

            def store_p(i, b):
                sp.wait_ge(row_done, i + 1)
                sp.dma_start(rows(k.p, i), p_row[b][:, :]).then_inc(p_out[b], 16)

            def fill(i, b):
                sp.dma_start(rows(k.sum2, i), zeros[:, 0:8 * F]).then_inc(tables_set, 16)
                sp.dma_start(rows(k.sum3, i), zeros[:, :]).then_inc(tables_set, 16)
                sp.dma_start(rows(k.max3, i), lowest[:, :]).then_inc(tables_set, 16)

            run(sp, [(0, load), (1, load_x), (3, store_x1), (5, store_p), (2, fill)])
            sp.wait_ge(tables_set, 16 * 3 * NODE_TILES)
            for b in range(2):
                sp.wait_ge(x1_out[b], 16 * (NODE_TILES // 2))
                sp.wait_ge(p_out[b], 16 * (NODE_TILES // 2))

        @block.tensor
        def _(pe):
            pe.wait_ge(k.w3a_in, 16)

            def product(out, lhsT, w, done):
                for c in range(KB):
                    last = nc.tensor.matmul(out[:, :], lhsT[:, c, :], w[:, c, :], start=(c == 0), stop=(c == KB - 1))
                last.then_inc(done, 1)

            def transposes(out, row, done):
                for c in range(KB):
                    last = nc.tensor.transpose(out[:, c * P:(c + 1) * P], row[:, c * P:(c + 1) * P], k.ident[:, :])
                last.then_inc(done, 1)

            def first(i):
                return isinstance(i, int) and i < 2

            def turn_x1(i, b):
                pe.wait_ge(x1_done, i + 1)
                if not isinstance(i, int) or i >= 1:
                    pe.wait_ge(x1T_done, i)
                transposes(p_xT, x1[b], x1_turned)

            def hidden(i, b):
                pe.wait_ge(xT_in[b], landed(i, b))
                if not first(i):
                    pe.wait_ge(h_done, i - 1)
                product(p_h[b], xT[b], k.w3a, h_pre)

            def turn_u(i, b):
                pe.wait_ge(u_done, i + 1)
                if not isinstance(i, int) or i >= 1:
                    pe.wait_ge(uT_done, i)
                transposes(p_uT, u[b], u_turned)

            def root(i, b):
                pe.wait_ge(x1T_done, i + 1)
                if isinstance(i, int) and i == 0:
                    pe.wait_ge(wr_in, 16)
                if not first(i):
                    pe.wait_ge(row_done, i - 1)
                    pe.wait_ge(sq_done, i - 1)
                product(p_p[b], x1T[b], wr, p_done)

            def output(i, b):
                pe.wait_ge(uT_done, i + 1)
                if isinstance(i, int) and i == 0:
                    pe.wait_ge(w4_in, 16)
                if not first(i):
                    pe.wait_ge(y_done, i - 1)
                product(p_o[b], uT[b], w4, o_done)

            run(pe, [(0, hidden), (1, turn_u), (3, turn_x1), (4, root), (1, output)])

        @block.scalar
        def _(act):
            first = lambda i: isinstance(i, int) and i < 2
            for out, row in ((b4_row, k.L0_b4), (gamma_row, k.L0_gamma), (beta_row, k.L0_beta)):
                act.dma_start(out[:, :], row.rearrange("(a n) -> a n", a=1).to_broadcast([P, D])).then_inc(rows_in, 16)
            act.dma_start(w4[:, :, :], k.L0_W4.rearrange("(c p) n -> p c n", p=P)).then_inc(w4_in, 16)
            act.dma_start(wr[:, :, :], k.L1_Wr.rearrange("(c p) n -> p c n", p=P)).then_inc(wr_in, 16)

            def x1_turned_out(i, b):
                act.wait_ge(x1_turned, i + 1)
                if not first(i):
                    act.wait_ge(p_done, i - 1)
                nc.scalar.activation(x1T[b][:, :, :], p_xT[:, :].rearrange("p (c n) -> p c n", c=KB), ACT.Copy
                                     ).then_inc(x1T_done, 1)

            def normalise_y(i, b):
                act.wait_ge(sc_done, 3 * i + 3)
                if not first(i):
                    act.wait_ge(yg_done, i - 1)
                nc.scalar.activation(yn[b][:, :], y[b][:, :], ACT.Identity, bias=small[b][:, 0, 2:3],
                                     scale=small[b][:, 0, 1:2]).then_inc(yn_done, 1)

            def u_turned_out(i, b):
                act.wait_ge(u_turned, i + 1)
                if not first(i):
                    act.wait_ge(o_done, i - 1)
                nc.scalar.activation(uT[b][:, :, :], p_uT[:, :].rearrange("p (c n) -> p c n", c=KB), ACT.Copy
                                     ).then_inc(uT_done, 1)

            def denominator(i, b):
                act.wait_ge(h_done, i + 1)
                if not first(i):
                    act.wait_ge(rec_done, i - 1)
                nc.scalar.activation(den[b][:, :], h[b][:, :], ACT.Exp).then_inc(exp_done, 1)
                act.wait_ge(exp_done, i + 1)
                nc.scalar.activation(den[b][:, :], den[b][:, :], ACT.Square, bias=1.0).then_inc(den_done, 1)
                act.wait_ge(den_done, 2 * i + 1)
                nc.scalar.activation(den[b][:, :], den[b][:, :], ACT.Copy, bias=1.0).then_inc(den_done, 1)

            def normalise_x1(i, b):
                act.wait_ge(sc2_done, 3 * i + 3)
                if not first(i):
                    act.wait_ge(x1_turned, i - 1)
                    act.wait_ge(x1_out[b], landed(i - 2, b))
                nc.scalar.activation(x1[b][:, :], zz[b][:, :], ACT.Identity, bias=small[b][:, 1, 2:3],
                                     scale=small[b][:, 1, 1:2]).then_inc(x1_done, 1)

            def root_out(i, b):
                act.wait_ge(p_done, i + 1)
                if not first(i):
                    act.wait_ge(p_out[b], landed(i - 2, b))
                    act.wait_ge(acc_done, 2 * i - 2)
                nc.scalar.activation(p_row[b][:, :], p_p[b][:, :], ACT.Copy).then_inc(row_done, 1)
                nc.scalar.activation(p_sq[b][:, :], p_p[b][:, :], ACT.Square).then_inc(sq_done, 1)

            run(act, [(3, normalise_x1), (2, normalise_y), (1, u_turned_out), (3, x1_turned_out),
                      (0, denominator), (4, root_out)])

        @block.vector
        def _(dve):
            first = lambda i: isinstance(i, int) and i < 2

            def residual(i, b):
                dve.wait_ge(o_done, i + 1)
                dve.wait_ge(xb_done, i + 1)
                if not first(i):
                    dve.wait_ge(yn_done, i - 1)
                nc.vector.tensor_tensor(y[b][:, :], p_o[b][:, :], xb[b][:, :], ALU.add).then_inc(y_done, 1)
                dve.wait_ge(y_done, i + 1)
                nc.vector.bn_stats(stats[b][:, 0, :], y[b][:, :]).then_inc(st_done, 1)
                dve.wait_ge(st_done, i + 1)
                if not first(i):
                    dve.wait_ge(sc_done, 3 * i - 3)
                dve.sem_inc(k.passed_dve, 1)
                nc.vector.bn_aggr(mv[b][:, 0, :], stats[b][:, 0, :]).then_inc(mv_done, 1)

            def accumulate(i, b):
                valid = P
                if isinstance(i, int) and i >= LAST_VALID_TILE:
                    valid = N % P if i == LAST_VALID_TILE else 0
                dve.wait_ge(row_done, i + 1)
                dve.wait_ge(sq_done, i + 1)
                if not isinstance(i, int) or i >= 1:
                    dve.wait_ge(acc_done, 2 * i)
                for s, part in enumerate((p_row, p_sq)):
                    if valid:
                        nc.vector.tensor_tensor(k.column_acc[0:valid, s, :], k.column_acc[0:valid, s, :],
                                                part[b][0:valid, :], ALU.add).then_inc(acc_done, 1)

            def hidden(i, b):
                dve.wait_ge(h_pre, i + 1)
                dve.wait_ge(z_in[b], landed(i, b))
                if not first(i):
                    dve.wait_ge(step_done, i - 1)
                    dve.wait_ge(u_done, i - 1)
                nc.vector.tensor_tensor(h[b][:, :], p_h[b][:, :], z[b][:, :], ALU.add).then_inc(h_done, 1)

            def second_norm(i, b):
                dve.wait_ge(yg_done, i + 1)
                dve.wait_ge(xbeta_done, i + 1)
                if not first(i):
                    dve.wait_ge(x1_done, i - 1)
                nc.vector.tensor_tensor(zz[b][:, :], yg[b][:, :], xbeta[b][:, :], ALU.add).then_inc(zz_done, 1)
                dve.wait_ge(zz_done, i + 1)
                nc.vector.bn_stats(stats[b][:, 1, :], zz[b][:, :]).then_inc(st2_done, 1)
                dve.wait_ge(st2_done, i + 1)
                if not first(i):
                    dve.wait_ge(sc2_done, 3 * i - 3)
                dve.sem_inc(k.passed_dve, 1)
                nc.vector.bn_aggr(mv[b][:, 1, :], stats[b][:, 1, :]).then_inc(mv2_done, 1)

            def divide(i, b):
                dve.wait_ge(den_done, 2 * i + 2)
                if not first(i):
                    dve.wait_ge(u_done, i - 1)
                nc.vector.reciprocal(rec[b][:, :], den[b][:, :]).then_inc(rec_done, 1)
                dve.wait_ge(rec_done, i + 1)
                nc.vector.scalar_tensor_tensor(out=rec[b][:, :], in0=h[b][:, :], scalar=-2.0, in1=rec[b][:, :],
                                               op0=ALU.mult, op1=ALU.mult).then_inc(step_done, 1)

            nc.vector.memset(k.column_acc[:, :, :], 0.0).then_inc(k.acc_zero, 1)
            dve.wait_ge(k.acc_zero, 1)
            run(dve, [(2, residual), (5, accumulate), (0, hidden), (2, second_norm), (0, divide)])

        @block.gpsimd
        def _(pool):
            first = lambda i: isinstance(i, int) and i < 2
            nc.gpsimd.memset(zeros[:, :], 0.0).then_inc(filled, 1)
            nc.gpsimd.memset(lowest[:, :], -BIG).then_inc(filled, 1)
            pool.wait_ge(rows_in, 48)

            def finish_u(i, b):
                pool.wait_ge(step_done, i + 1)
                if not first(i):
                    pool.wait_ge(u_turned, i - 1)
                nc.gpsimd.tensor_tensor(u[b][:, :], rec[b][:, :], h[b][:, :], ALU.add).then_inc(u_done, 1)

            def add_beta(i, b):
                pool.wait_ge(x_in[b], landed(i, b))
                if not first(i):
                    pool.wait_ge(zz_done, i - 1)
                nc.gpsimd.tensor_tensor(xbeta[b][:, :], x[b][:, :], beta_row[:, :], ALU.add).then_inc(xbeta_done, 1)

            def scale_y(i, b):
                pool.wait_ge(mv_done, i + 1)
                if not first(i):
                    pool.wait_ge(yn_done, i - 1)
                row_scale(pool, k, mv[b][:, 0, 1:2], mv[b][:, 0, 0:1], small[b][:, 0, 0:1], small[b][:, 0, 1:2],
                          small[b][:, 0, 2:3], sc_done, 3 * i)

            def add_b4(i, b):
                pool.wait_ge(x_in[b], landed(i, b))
                if not first(i):
                    pool.wait_ge(y_done, i - 1)
                nc.gpsimd.tensor_tensor(xb[b][:, :], x[b][:, :], b4_row[:, :], ALU.add).then_inc(xb_done, 1)

            def times_gamma(i, b):
                pool.wait_ge(yn_done, i + 1)
                if not first(i):
                    pool.wait_ge(zz_done, i - 1)
                nc.gpsimd.tensor_tensor(yg[b][:, :], yn[b][:, :], gamma_row[:, :], ALU.mult).then_inc(yg_done, 1)

            def scale_x1(i, b):
                pool.wait_ge(mv2_done, i + 1)
                if not first(i):
                    pool.wait_ge(x1_done, i - 1)
                row_scale(pool, k, mv[b][:, 1, 1:2], mv[b][:, 1, 0:1], small[b][:, 1, 0:1], small[b][:, 1, 1:2],
                          small[b][:, 1, 2:3], sc2_done, 3 * i)

            run(pool, [(1, finish_u), (2, scale_y), (2, add_beta), (2, times_gamma), (1, add_b4), (2, scale_x1)])


def aggregate_phase(nc, k):
    with phase(nc, "a_") as (sb, ps, sem), ExitStack() as ctx:

        wl = sb("wl", [P, KB, D])
        old = sb("old", [P, EDGE_TILES, D])
        xT = [sb(f"xT{i}", [P, KB, P]) for i in range(2)]
        msg, tile_sum, both, share = ([sb(f"{n}{i}", [P, w]) for i in range(2)]
                                      for n, w in (("msg", D), ("tile_sum", D), ("both", D), ("share", P)))
        gamma, beta, bl, mean, var, tmp = (sb(n, [P, D]) for n in ("gamma", "beta", "bl", "mean", "var", "tmp"))
        compact, power, diag = sb("compact", [P, KB]), sb("power", [P, KB]), msg[0]
        p_T, p_A, p_S = ([ps(f"p_{n}{i}", [P, D]) for i in range(2)] for n in "TAS")
        p_sum, p_sq = ps("p_sum", [P, D]), ps("p_sq", [P, D])

        x_in, new_in = [sem(f"x_in{i}") for i in range(4)], [sem(f"new_in{i}") for i in range(4)]
        old_in, w_in, turned, turned_out, a_done, a_out, s_done, s_out, scattered = (
            sem(n) for n in ("old_in", "w_in", "turned", "turned_out", "done", "out", "s_done", "s_out", "scattered"))
        diff, both_done, share_done, summed, fin, power_done, diag_done, power_spread = (
            sem(n) for n in ("diff", "both_done", "share_done", "summed", "fin", "power", "diag", "power_spread"))

        block = ctx.enter_context(nc.Block())

        @block.sync
        def _(sp):
            sp.dma_start(wl[:, :, :], k.L1_Wl.rearrange("(c p) n -> p c n", p=P)).then_inc(w_in, 16)
            for out, r in ((gamma, k.L1_gamma), (beta, k.L1_beta), (bl, k.L1_bl)):
                sp.dma_start(out[:, :], r.rearrange("(a n) -> a n", a=1).to_broadcast([P, D])).then_inc(w_in, 16)

        @block.gpsimd
        def _(pool):
            for t in range(EDGE_TILES):
                if t >= 4:
                    pool.wait_ge(x_in[t % 4], 16 * (t // 4))
                pool.indirect_dma_start(k.src_rows_sb[:, t, :], None, k.x1[:, :], at_rows(k.index[:, 0, t:t + 1])
                                        ).then_inc(x_in[t % 4], 16)
                pool.indirect_dma_start(old[:, t, :], None, k.p[:, :], at_rows(k.index[:, 1, t:t + 1])
                                        ).then_inc(old_in, 16)
            pool.wait_ge(old_in, 16 * EDGE_TILES)
            for t in range(EDGE_TILES):
                pool.wait_ge(s_out, t + 1)
                if t:
                    pool.wait_ge(scattered, 16 * t)
                pool.indirect_dma_start(k.p[:, :], at_rows(k.unique[:, 1, t:t + 1]), tile_sum[t % 2][:, :], None,
                                        compute_op=ALU.add).then_inc(scattered, 16)
            pool.wait_ge(scattered, 16 * EDGE_TILES)
            for t in range(EDGE_TILES):
                if t >= 4:
                    pool.wait_ge(new_in[t % 4], 16 * (t // 4))
                pool.indirect_dma_start(k.dst_rows_sb[:, t, :], None, k.p[:, :], at_rows(k.index[:, 1, t:t + 1])
                                        ).then_inc(new_in[t % 4], 16)
            pool.wait_ge(fin, 6)
            nc.gpsimd.tensor_tensor(power[:, :], compact[:, :], k.minus_half[:, :], ALU.pow).then_inc(power_done, 1)

        @block.tensor
        def _(pe):
            def turn(t):
                pe.wait_ge(x_in[t % 4], 16 * (t // 4 + 1))
                if t >= 2:
                    pe.wait_ge(turned_out, t - 1)
                for c in range(KB):
                    last = nc.tensor.transpose(p_T[t % 2][:, c * P:(c + 1) * P],
                                               k.src_rows_sb[:, t, c * P:(c + 1) * P], k.ident[:, :])
                last.then_inc(turned, 1)

            def tile_sums(t):
                pe.wait_ge(a_out, t + 1)
                if t >= 2:
                    pe.wait_ge(s_out, t - 1)
                nc.tensor.matmul(p_S[t % 2][:, :], k.same_dst[:, t, :], msg[t % 2][:, :], start=True, stop=True
                                 ).then_inc(s_done, 1)

            turn(0)
            pe.wait_ge(w_in, 64)
            for t in range(EDGE_TILES):
                if t + 1 < EDGE_TILES:
                    turn(t + 1)
                pe.wait_ge(turned_out, t + 1)
                if t >= 2:
                    pe.wait_ge(a_out, t - 1)
                for c in range(KB):
                    last = nc.tensor.matmul(p_A[t % 2][:, :], xT[t % 2][:, c, :], wl[:, c, :],
                                            start=(c == 0), stop=(c == KB - 1))
                last.then_inc(a_done, 1)
                if t:
                    tile_sums(t - 1)
            tile_sums(EDGE_TILES - 1)
            nc.tensor.matmul(p_sum[:, :], k.ones[:, :], k.column_acc[:, 0, :], start=True, stop=False)
            nc.tensor.matmul(p_sq[:, :], k.ones[:, :], k.column_acc[:, 1, :], start=True, stop=False)
            for t in range(EDGE_TILES):
                pe.wait_ge(share_done, t + 1)
                pe.wait_ge(both_done, 2 * t + 2)
                last = t == EDGE_TILES - 1
                nc.tensor.matmul(p_sum[:, :], share[t % 2][:, :], old[:, t, :], start=False, stop=last)
                nc.tensor.matmul(p_sq[:, :], share[t % 2][:, :], both[t % 2][:, :], start=False, stop=last
                                 ).then_inc(summed, 1)
            pe.wait_ge(diag_done, 1)
            nc.tensor.matmul(p_T[0][:, :], k.ones[:, :], diag[:, :], start=True, stop=True).then_inc(power_spread, 1)

        @block.scalar
        def _(act):
            def turn_out(t):
                act.wait_ge(turned, t + 1)
                if t >= 2:
                    act.wait_ge(a_done, t - 1)
                nc.scalar.activation(xT[t % 2][:, :, :], p_T[t % 2][:, :].rearrange("p (c n) -> p c n", c=KB),
                                     ACT.Copy).then_inc(turned_out, 1)

            def sum_out(t):
                act.wait_ge(s_done, t + 1)
                if t >= 2:
                    act.wait_ge(scattered, 16 * (t - 1))
                nc.scalar.activation(tile_sum[t % 2][:, :], p_S[t % 2][:, :], ACT.Copy).then_inc(s_out, 1)

            turn_out(0)
            for t in range(EDGE_TILES):
                if t + 1 < EDGE_TILES:
                    turn_out(t + 1)
                act.wait_ge(a_done, t + 1)
                if t >= 2:
                    act.wait_ge(s_done, t - 1)
                nc.scalar.activation(msg[t % 2][:, :], p_A[t % 2][:, :], ACT.Copy, scale=k.inv_degree[:, t:t + 1]
                                     ).then_inc(a_out, 1)
                if t:
                    sum_out(t - 1)
            sum_out(EDGE_TILES - 1)

        @block.vector
        def _(dve):
            for t in range(EDGE_TILES):
                dve.wait_ge(new_in[t % 4], 16 * (t // 4 + 1))
                if t == 0:
                    dve.wait_ge(old_in, 16 * EDGE_TILES)
                if t >= 2:
                    dve.wait_ge(summed, t - 1)
                nc.vector.tensor_scalar(share[t % 2][:, :], k.ones[:, :], k.share[:, t:t + 1], None, ALU.mult
                                        ).then_inc(share_done, 1)
                nc.vector.tensor_tensor(both[t % 2][:, :], k.dst_rows_sb[:, t, :], old[:, t, :], ALU.add
                                        ).then_inc(both_done, 1)
                dve.wait_ge(both_done, 2 * t + 1)
                nc.vector.tensor_tensor(old[:, t, :], k.dst_rows_sb[:, t, :], old[:, t, :], ALU.subtract
                                        ).then_inc(diff, 1)
                dve.wait_ge(diff, t + 1)
                nc.vector.tensor_tensor(both[t % 2][:, :], both[t % 2][:, :], old[:, t, :], ALU.mult
                                        ).then_inc(both_done, 1)
            dve.wait_ge(summed, EDGE_TILES)
            dve.wait_ge(w_in, 64)
            n = [0]

            def step(ins):
                n[0] += 1
                ins.then_inc(fin, 1)
                dve.wait_ge(fin, n[0])

            step(nc.vector.tensor_scalar(mean[:, :], p_sum[:, :], 1.0 / N, None, ALU.mult))
            step(nc.vector.tensor_tensor(tmp[:, :], mean[:, :], mean[:, :], ALU.mult))
            step(nc.vector.scalar_tensor_tensor(out=var[:, :], in0=p_sq[:, :], scalar=1.0 / N, in1=tmp[:, :],
                                                op0=ALU.mult, op1=ALU.subtract))
            step(nc.vector.tensor_scalar(var[:, :], var[:, :], 0.0, LN_EPS, ALU.max, ALU.add))
            ident = k.ident[:, :].rearrange("p (a f) -> p a f", a=1).to_broadcast([P, KB, P])
            tmp3 = tmp[:, :].rearrange("p (c f) -> p c f", c=KB)
            step(nc.vector.tensor_tensor(tmp3, var[:, :].rearrange("p (c f) -> p c f", c=KB), ident, ALU.mult))
            step(nc.vector.tensor_reduce(compact[:, :], tmp3, AX_X, ALU.add))
            dve.wait_ge(power_done, 1)
            nc.vector.tensor_tensor(diag[:, :].rearrange("p (c f) -> p c f", c=KB), ident,
                                    power[:, :].rearrange("p (c a) -> p c a", a=1).to_broadcast([P, KB, P]),
                                    ALU.mult).then_inc(diag_done, 1)
            dve.wait_ge(power_spread, 1)
            step(nc.vector.tensor_tensor(k.bn_scale[:, :], p_T[0][:, :], gamma[:, :], ALU.mult))
            step(nc.vector.tensor_tensor(mean[:, :], mean[:, :], bl[:, :], ALU.add))
            step(nc.vector.tensor_tensor(mean[:, :], bl[:, :], mean[:, :], ALU.subtract))
            step(nc.vector.tensor_tensor(mean[:, :], mean[:, :], k.bn_scale[:, :], ALU.mult))
            step(nc.vector.tensor_tensor(k.bn_shift[:, :], mean[:, :], beta[:, :], ALU.add))


def plain_load(nc, k, sp, i):
    b = i % 2
    if i >= 2:
        sp.wait_ge(k.plain_y, i - 1)
    sp.dma_start(k.plain_p_rows[b][:, :], k.p[i * P:(i + 1) * P, :]).then_inc(k.plain_p_in[b], 16)
    sp.dma_start(k.plain_x1_rows[b][:, :], k.x1[i * P:(i + 1) * P, :]).then_inc(k.plain_x1_in[b], 16)


def plain_store(nc, k, sp, i):
    b = i % 2
    sp.wait_ge(k.plain_out, i + 1)
    sp.dma_start(k.out[i * P:(i + 1) * P, :], k.plain_y_rows[b][:, :]).then_inc(k.plain_gone[b], 16)


def plain_scale(nc, k, pool, i):
    b = i % 2
    pool.wait_ge(k.plain_p_in[b], 16 * (i // 2 + 1))
    nc.gpsimd.tensor_tensor(k.plain_p_rows[b][:, :], k.plain_p_rows[b][:, :], k.bn_scale[:, :], ALU.mult
                            ).then_inc(k.plain_scaled, 1)


def plain_norm(nc, k, dve, i):
    b = i % 2
    a, y = k.plain_p_rows[b], k.plain_y_rows[b]
    dve.wait_ge(k.plain_scaled, i + 1)
    nc.vector.tensor_tensor(a[:, :], a[:, :], k.bn_shift[:, :], ALU.add).then_inc(k.plain_shifted, 1)
    dve.wait_ge(k.plain_shifted, i + 1)
    nc.vector.scalar_tensor_tensor(out=a[:, :], in0=a[:, :], scalar=0.01, in1=a[:, :], op0=ALU.mult, op1=ALU.max
                                   ).then_inc(k.plain_leaky, 1)
    dve.wait_ge(k.plain_leaky, i + 1)
    dve.wait_ge(k.plain_x1_in[b], 16 * (i // 2 + 1))
    if i >= 2:
        dve.wait_ge(k.plain_gone[b], 16 * (i // 2))
    nc.vector.scalar_tensor_tensor(out=y[:, :], in0=k.plain_x1_rows[b][:, :], scalar=2.0, in1=a[:, :],
                                   op0=ALU.mult, op1=ALU.add).then_inc(k.plain_y, 1)
    dve.wait_ge(k.plain_y, i + 1)
    nc.vector.bn_stats(k.plain_stats[b][:, :], y[:, :]).then_inc(k.plain_st, 1)
    dve.wait_ge(k.plain_st, i + 1)
    if i >= 2:
        dve.wait_ge(k.plain_sc, 3 * i - 3)
    nc.vector.bn_aggr(k.plain_mv[b][:, :], k.plain_stats[b][:, :]).then_inc(k.plain_mv_done, 1)


def plain_row_scale(nc, k, pool, i):
    b = i % 2
    mv, small = k.plain_mv[b], k.plain_small[b]
    pool.wait_ge(k.plain_mv_done, i + 1)
    if i >= 2:
        pool.wait_ge(k.plain_out, i - 1)
    row_scale(pool, k, mv[:, 1:2], mv[:, 0:1], small[:, 0:1], small[:, 1:2], small[:, 2:3], k.plain_sc, 3 * i,
              norms=3)


def plain_row(nc, k, act, i):
    b = i % 2
    y, small = k.plain_y_rows[b], k.plain_small[b]
    act.wait_ge(k.plain_sc, 3 * i + 3)
    nc.scalar.activation(y[:, :], y[:, :], ACT.Identity, bias=small[:, 2:3], scale=small[:, 1:2]
                         ).then_inc(k.plain_out, 1)


def edge_rows_phase(nc, k):
    with phase(nc, "e_") as (sb, ps, sem), ExitStack() as ctx:
        T = EDGE_TILES
        ws, wv = sb("ws", [P, F]), sb("wv", [P, F])
        other = [sb(f"other{i}", [P, D]) for i in range(4)]
        a, y, featT = ([sb(f"{n}{i}", [P, D]) for i in range(2)] for n in ("a", "y", "featT"))
        stats, mv, small = ([sb(f"{n}{i}", [P, w]) for i in range(2)] for n, w in (("stats", 6), ("mv", 2), ("small", 4)))
        edge, part, tile_sum = ([sb(f"{n}{i}", [P, w]) for i in range(2)]
                                for n, w in (("edge", 8 * F), ("part", 3 * F), ("tile_sum", 8 * F)))
        p_T, p_F, p_S = ([ps(f"p_{n}{i}", [P, D]) for i in range(2)] for n in "TFS")

        w_in = sem("w_in")
        other_in = [sem(f"other_in{i}") for i in range(4)]
        scaled, shifted, leaky, y_done, st, mv_done, sc, x2_done = (
            sem(n) for n in ("scaled", "shifted", "leaky", "y", "st", "mv", "sc", "x2"))
        turned, turned_out, feat, s_part, v_part, dot, edge_done, s_done, s_out, scattered = (
            sem(n) for n in ("turned", "turned_out", "feat", "s_part", "v_part", "dot", "edge", "s_done", "s_out", "scat"))

        def p_of(u):
            return k.dst_rows_sb[:, u, :] if u < T else other[u % 4][:, :]

        def x1_of(u):
            return other[u % 4][:, :] if u < T else k.src_rows_sb[:, u - T, :]

        def x2_of(u):
            return k.dst_rows_sb[:, u, :] if u < T else k.src_rows_sb[:, u - T, :]

        block = ctx.enter_context(nc.Block())

        @block.sync
        def _(sp):
            sp.dma_start(ws[:, :], k.L2_ws).then_inc(w_in, 16)
            sp.dma_start(wv[:, :], k.L2_wv).then_inc(w_in, 16)

        @block.gpsimd
        def _(pool):
            def gather(u):
                if u >= 4:
                    pool.wait_ge(y_done if u - 4 < T else scaled, u - 3)
                table, side = (k.x1, 1) if u < T else (k.p, 0)
                pool.indirect_dma_start(other[u % 4][:, :], None, table[:, :],
                                        at_rows(k.index[:, side, u % T:u % T + 1])).then_inc(other_in[u % 4], 16)

            def scale(u):
                if u >= T:
                    pool.wait_ge(other_in[u % 4], 16 * (u // 4 + 1))
                if u >= 2:
                    pool.wait_ge(y_done, u - 1)
                nc.gpsimd.tensor_tensor(a[u % 2][:, :], p_of(u), k.bn_scale[:, :], ALU.mult).then_inc(scaled, 1)

            def row(u):
                b = u % 2
                pool.wait_ge(mv_done, u + 1)
                if u >= 2:
                    pool.wait_ge(x2_done, u - 1)
                row_scale(pool, k, mv[b][:, 1:2], mv[b][:, 0:1], small[b][:, 0:1], small[b][:, 1:2],
                          small[b][:, 2:3], sc, 3 * u)

            def scatter(t):
                pool.wait_ge(s_out, t + 1)
                if t:
                    pool.wait_ge(scattered, 16 * t)
                pool.indirect_dma_start(k.sum2[:, :], at_rows(k.unique[:, 0, t:t + 1]), tile_sum[t % 2][:, :], None,
                                        compute_op=ALU.add).then_inc(scattered, 16)

            for u in range(3):
                gather(u)
            for u in range(2 * T + 6):
                if u < 2 * T:
                    scale(u)
                if u + 3 < 2 * T:
                    gather(u + 3)
                if 1 <= u <= 2 * T:
                    row(u - 1)
                if 0 <= u - 5 < T:
                    scatter(u - 5)
            pool.wait_ge(scattered, 16 * T)

        @block.vector
        def _(dve):
            def norm(u):
                b = u % 2
                dve.wait_ge(scaled, u + 1)
                nc.vector.tensor_tensor(a[b][:, :], a[b][:, :], k.bn_shift[:, :], ALU.add).then_inc(shifted, 1)
                dve.wait_ge(shifted, u + 1)
                nc.vector.scalar_tensor_tensor(out=a[b][:, :], in0=a[b][:, :], scalar=0.01, in1=a[b][:, :],
                                               op0=ALU.mult, op1=ALU.max).then_inc(leaky, 1)
                dve.wait_ge(leaky, u + 1)
                if u < T:
                    dve.wait_ge(other_in[u % 4], 16 * (u // 4 + 1))
                if u >= 2:
                    dve.wait_ge(x2_done, u - 1)
                nc.vector.scalar_tensor_tensor(out=y[b][:, :], in0=x1_of(u), scalar=2.0, in1=a[b][:, :],
                                               op0=ALU.mult, op1=ALU.add).then_inc(y_done, 1)
                dve.wait_ge(y_done, u + 1)
                nc.vector.bn_stats(stats[b][:, :], y[b][:, :]).then_inc(st, 1)
                dve.wait_ge(st, u + 1)
                if u >= 2:
                    dve.wait_ge(sc, 3 * u - 3)
                nc.vector.bn_aggr(mv[b][:, :], stats[b][:, :]).then_inc(mv_done, 1)

            def message(t):
                b = t % 2
                e4 = edge[b][:, :].rearrange("p (c h f) -> p c h f", c=4, h=2)
                a4 = k.filters[:, t, :, :]
                dve.wait_ge(feat, t + 1)
                if t >= 2:
                    dve.wait_ge(s_done, t - 1)
                s = p_F[b][:, 0:F].rearrange("p (a f) -> p a f", a=1)
                v = p_F[b][:, F:4 * F].rearrange("p (c f) -> p c f", c=3)
                nc.vector.tensor_tensor(e4[:, :, 0, :], s.to_broadcast([P, 4, F]), a4[:, 0:4, :], ALU.mult
                                        ).then_inc(s_part, 1)
                nc.vector.tensor_tensor(e4[:, 1:4, 1, :], v, a4[:, 7:8, :].to_broadcast([P, 3, F]), ALU.mult
                                        ).then_inc(v_part, 1)
                if t >= 2:
                    dve.wait_ge(edge_done, t - 1)
                nc.vector.tensor_tensor(part[b][:, :].rearrange("p (c f) -> p c f", c=3), v, a4[:, 4:7, :], ALU.mult
                                        ).then_inc(dot, 1)
                dve.wait_ge(dot, t + 1)
                nc.vector.tensor_reduce(e4[:, 0, 1, :], part[b][:, :].rearrange("p (c f) -> p f c", c=3), AX_X,
                                        ALU.add).then_inc(edge_done, 1)

            for u in range(2 * T + 4):
                if u < 2 * T:
                    norm(u)
                if 0 <= u - 3 < T:
                    message(u - 3)

        @block.scalar
        def _(act):
            def x2_row(u):
                b = u % 2
                act.wait_ge(sc, 3 * u + 3)
                nc.scalar.activation(x2_of(u), y[b][:, :], ACT.Identity, bias=small[b][:, 2:3],
                                     scale=small[b][:, 1:2]).then_inc(x2_done, 1)

            def turn_out(t):
                act.wait_ge(turned, t + 1)
                if t >= 2:
                    act.wait_ge(feat, t - 1)
                nc.scalar.activation(featT[t % 2][:, :], p_T[t % 2][:, :], ACT.Copy).then_inc(turned_out, 1)

            def sum_out(t):
                act.wait_ge(s_done, t + 1)
                if t >= 2:
                    act.wait_ge(scattered, 16 * (t - 1))
                nc.scalar.activation(tile_sum[t % 2][:, :], p_S[t % 2][:, 0:8 * F], ACT.Copy).then_inc(s_out, 1)

            for u in range(2 * T + 5):
                if 1 <= u <= 2 * T:
                    x2_row(u - 1)
                if 0 <= u - 2 < T:
                    turn_out(u - 2)
                if 0 <= u - 4 < T:
                    sum_out(u - 4)

        @block.tensor
        def _(pe):
            def turn(t):
                pe.wait_ge(x2_done, t + 1)
                if t >= 2:
                    pe.wait_ge(turned_out, t - 1)
                x2 = k.dst_rows_sb[:, t, :]
                vector = x2[:, B:].rearrange("p (b c) -> p c b", c=3)
                for c in range(4):
                    last = nc.tensor.transpose(p_T[t % 2][:, c * P:(c + 1) * P],
                                               x2[:, 0:B] if c == 0 else vector[:, c - 1, :], k.ident[:, :])
                last.then_inc(turned, 1)

            def features(t):
                pe.wait_ge(turned_out, t + 1)
                if t >= 2:
                    pe.wait_ge(edge_done, t - 1)
                for c in range(4):
                    last = nc.tensor.matmul(p_F[t % 2][:, c * F:(c + 1) * F], featT[t % 2][:, c * P:(c + 1) * P],
                                            (ws if c == 0 else wv)[:, :], start=True, stop=True)
                last.then_inc(feat, 1)

            def tile_sums(t):
                pe.wait_ge(s_part, t + 1)
                pe.wait_ge(v_part, t + 1)
                pe.wait_ge(edge_done, t + 1)
                if t >= 2:
                    pe.wait_ge(s_out, t - 1)
                nc.tensor.matmul(p_S[t % 2][:, 0:8 * F], k.same_src[:, t, :], edge[t % 2][:, :], start=True, stop=True
                                 ).then_inc(s_done, 1)

            pe.wait_ge(w_in, 32)
            for u in range(T + 3):
                if u < T:
                    turn(u)
                if 1 <= u <= T:
                    features(u - 1)
                if 0 <= u - 2 < T:
                    tile_sums(u - 2)


def equivariant_phase(nc, k):
    with phase(nc, "q_") as (sb, ps, sem), ExitStack() as ctx:
        U, BATCH, AHEAD = 2 * EDGE_TILES, 4, 8
        NB = U // BATCH
        LAG = 2 * BATCH
        w1s, w1v, w2s, w2v = sb("w1s", [2 * F, B]), sb("w1v", [2 * F, B]), sb("w2s", [B, B]), sb("w2v", [B, B])
        sums = [sb(f"sums{i}", [P, 8 * F]) for i in range(AHEAD)]
        sumT = [sb(f"sumT{i}", [2 * F, 4, P]) for i in range(2)]
        outT = [sb(f"outT{i}", [P, BATCH, D]) for i in range(3)]
        mag, low, logs, pos = (sb(n, [P, BATCH, B]) for n in ("mag", "low", "logs", "pos"))
        y = [sb(f"y{i}", [P, D]) for i in range(2)]
        stats, mv, small = ([sb(f"{n}{i}", [P, w]) for i in range(2)] for n, w in (("stats", 6), ("mv", 2), ("small", 4)))
        p_T = [ps(f"p_T{i}", [2 * F, 4, P]) for i in range(2)]
        p_O, p_R = ([ps(f"p_{n}{i}", [P, D]) for i in range(2)] for n in "OR")
        w_in = sem("w_in")
        sums_in = [sem(f"sums_in{i}") for i in range(AHEAD)]
        turned, turned_out, first_done, first_out, act_steps, pos_done, ssp_done, second_done = (
            sem(n) for n in ("turned", "turned_out", "first", "first_out", "act", "pos", "ssp", "second"))
        y_s, y_done, st, mv_done, sc, x3_done = (sem(n) for n in ("y_s", "y", "st", "mv", "sc", "x3"))

        def rows_of(u):
            return (k.src_rows_sb, k.dst_rows_sb)[u % 2][:, u // 2, :]

        block = ctx.enter_context(nc.Block())

        @block.sync
        def _(sp):
            for out, w in ((w1s, k.L2_o1s), (w1v, k.L2_o1v), (w2s, k.L2_o2s), (w2v, k.L2_o2v)):
                sp.dma_start(out[:, :], w).then_inc(w_in, 16)
            for u in range(U):
                plain_load(nc, k, sp, u)
                if u >= 2:
                    plain_store(nc, k, sp, u - 2)

        @block.gpsimd
        def _(pool):
            def gather(u):
                if u >= AHEAD:
                    pool.wait_ge(turned, u - AHEAD + 1)
                pool.indirect_dma_start(sums[u % AHEAD][:, :], None, k.sum2[:, :],
                                        at_rows(k.index[:, u % 2, u // 2:u // 2 + 1])).then_inc(sums_in[u % AHEAD], 16)

            def row(u):
                b = u % 2
                pool.wait_ge(mv_done, u + 1)
                if u >= 2:
                    pool.wait_ge(x3_done, u - 1)
                row_scale(pool, k, mv[b][:, 1:2], mv[b][:, 0:1], small[b][:, 0:1], small[b][:, 1:2],
                          small[b][:, 2:3], sc, 3 * u)

            for u in range(AHEAD):
                gather(u)
            for u in range(U + LAG):
                if u < U:
                    plain_scale(nc, k, pool, u)
                if u >= LAG:
                    row(u - LAG)
                if u + AHEAD < U:
                    gather(u + AHEAD)
                if 1 <= u <= U:
                    plain_row_scale(nc, k, pool, u - 1)

        @block.tensor
        def _(pe):
            pe.wait_ge(w_in, 64)

            def turn(u):
                pe.wait_ge(sums_in[u % AHEAD], 16 * (u // AHEAD + 1))
                if u >= 2:
                    pe.wait_ge(turned_out, u - 1)
                for c in range(4):
                    last = nc.tensor.transpose(p_T[u % 2][:, c, :], sums[u % AHEAD][:, c * 2 * F:(c + 1) * 2 * F],
                                               k.ident[:, :])
                last.then_inc(turned, 1)

            def first(u):
                pe.wait_ge(turned_out, u + 1)
                if u >= 2:
                    pe.wait_ge(first_out, u - 1)
                nc.tensor.matmul(p_O[u % 2][:, 0:P], w1s[:, :], sumT[u % 2][:, 0, :], start=True, stop=True)
                nc.tensor.matmul(p_O[u % 2][:, P:D], w1v[:, :], sumT[u % 2][:, 1:4, :].rearrange("k c n -> k (c n)"),
                                 start=True, stop=True).then_inc(first_done, 1)

            def second(u):
                n = u // BATCH
                pe.wait_ge(ssp_done, n + 1)
                if u >= 2:
                    pe.wait_ge(y_done, u - 1)
                for c in range(4):
                    last = nc.tensor.matmul(p_R[u % 2][:, c * P:(c + 1) * P],
                                            outT[n % 3][:, u % BATCH, c * P:(c + 1) * P],
                                            (w2s if c == 0 else w2v)[:, :], start=True, stop=True)
                last.then_inc(second_done, 1)

            turn(0)
            for u in range(U + LAG):
                if u + 1 < U:
                    turn(u + 1)
                if u < U:
                    first(u)
                if u >= LAG:
                    second(u - LAG)

        @block.scalar
        def _(act):
            def turn_out(u):
                act.wait_ge(turned, u + 1)
                if u >= 2:
                    act.wait_ge(first_done, u - 1)
                nc.scalar.activation(sumT[u % 2][:, :, :], p_T[u % 2][:, :, :], ACT.Copy).then_inc(turned_out, 1)

            def first_product_out(u):
                n = u // BATCH
                act.wait_ge(first_done, u + 1)
                if n >= 3:
                    act.wait_ge(second_done, BATCH * (n - 2))
                nc.scalar.activation(outT[n % 3][:, u % BATCH, :], p_O[u % 2][:, :], ACT.Copy,
                                     scale=(2 * F) ** -0.5).then_inc(first_out, 1)

            def logarithms(n):
                act.wait_ge(first_out, BATCH * (n + 1))
                if n:
                    act.wait_ge(ssp_done, n)
                for step, (out, in_, func, bias, scale) in enumerate((
                        (mag[:, :, :], outT[n % 3][:, :, 0:B], ACT.Abs, 0.0, 1.0),
                        (low[:, :, :], mag[:, :, :], ACT.Exp, 0.0, -1.0),
                        (logs[:, :, :], low[:, :, :], ACT.Ln, 1.0, 1.0))):
                    nc.scalar.activation(out, in_, func, bias=bias, scale=scale).then_inc(act_steps, 1)
                    act.wait_ge(act_steps, 3 * n + step + 1)

            def x3_row(u):
                b = u % 2
                act.wait_ge(sc, 3 * u + 3)
                nc.scalar.activation(rows_of(u), y[b][:, :], ACT.Identity, bias=small[b][:, 2:3],
                                     scale=small[b][:, 1:2]).then_inc(x3_done, 1)

            turn_out(0)
            for u in range(U + LAG):
                if u + 1 < U:
                    turn_out(u + 1)
                if u < U:
                    first_product_out(u)
                if u >= LAG:
                    x3_row(u - LAG)
                if 1 <= u <= U:
                    plain_row(nc, k, act, u - 1)
                if u < U and u % BATCH == BATCH - 1:
                    logarithms(u // BATCH)

        @block.vector
        def _(dve):
            def softplus(n):
                nc.vector.tensor_scalar(pos[:, :, :], outT[n % 3][:, :, 0:B], 0.0, None, ALU.max
                                        ).then_inc(pos_done, 1)
                dve.wait_ge(pos_done, n + 1)
                nc.vector.scalar_tensor_tensor(out=outT[n % 3][:, :, 0:B], in0=logs[:, :, :], scalar=-LOG2,
                                               in1=pos[:, :, :], op0=ALU.add, op1=ALU.add).then_inc(ssp_done, 1)
                dve.wait_ge(ssp_done, n + 1)

            def norm(u):
                b = u % 2
                x2, inv = rows_of(u), float(B) ** -0.5
                dve.wait_ge(second_done, u + 1)
                if u >= 2:
                    dve.wait_ge(x3_done, u - 1)
                nc.vector.scalar_tensor_tensor(out=y[b][:, 0:B], in0=p_R[b][:, 0:B], scalar=inv,
                                               in1=x2[:, 0:B], op0=ALU.mult, op1=ALU.add).then_inc(y_s, 1)
                nc.vector.scalar_tensor_tensor(
                    out=y[b][:, B:D].rearrange("p (d c) -> p c d", c=3),
                    in0=p_R[b][:, B:D].rearrange("p (c d) -> p c d", c=3), scalar=inv,
                    in1=x2[:, B:D].rearrange("p (d c) -> p c d", c=3), op0=ALU.mult, op1=ALU.add
                    ).then_inc(y_done, 1)
                dve.wait_ge(y_s, u + 1)
                dve.wait_ge(y_done, u + 1)
                nc.vector.bn_stats(stats[b][:, :], y[b][:, :]).then_inc(st, 1)
                dve.wait_ge(st, u + 1)
                if u >= 2:
                    dve.wait_ge(sc, 3 * u - 3)
                nc.vector.bn_aggr(mv[b][:, :], stats[b][:, :]).then_inc(mv_done, 1)

            for u in range(U + LAG):
                if u % BATCH == 1 and 1 <= u // BATCH <= NB:
                    n = u // BATCH - 1
                    dve.wait_ge(act_steps, 3 * n + 3)
                    softplus(n)
                if u >= LAG:
                    norm(u - LAG)
                if u < U:
                    plain_norm(nc, k, dve, u)


def scores_phase(nc, k):
    with phase(nc, "s_") as (sb, ps, sem), ExitStack() as ctx:
        T = EDGE_TILES
        PLAIN = 2 * T
        wqk = sb("wqk", [P, KB, 2 * D])
        srcT = [sb(f"srcT{i}", [P, KB, P]) for i in range(2)]
        q = [sb(f"q{i}", [P, D]) for i in range(2)]
        prod = sb("prod", [P, D])
        diag = sb("diag", [HEADS, HEADS, P])
        away = [sb(f"away{i}", [P, P]) for i in range(2)]
        cand = sb("cand", [P, HEADS, P])
        tile_max, known = ([sb(f"{n}{i}", [P, HEADS]) for i in range(2)] for n in ("tile_max", "known"))
        p_T = [ps(f"p_T{i}", [P, D]) for i in range(2)]
        p_q, p_k, p_w = ps("p_q", [P, D]), ps("p_k", [P, D]), ps("p_w", [HEADS, P])
        p_all = ps("p_all", [P, HEADS, P])
        w_in, known_in, max_gone = sem("w_in"), sem("known_in"), sem("max_gone")
        turned, turned_out, q_done, k_done, q_out, prod_done, aw_done, aw_turned, diag_done, spread = (
            sem(n) for n in ("turned", "turned_out", "q_done", "k_done", "q_out", "prod", "aw", "aw_turned", "diag", "spread"))
        away_done, cand_done, tile_max_done, merged = (sem(n) for n in ("away", "cand", "tile_max", "merged"))

        block = ctx.enter_context(nc.Block())

        @block.sync
        def _(sp):
            sp.dma_start(wqk[:, :, :], k.L3_W[:, 0:2 * D].rearrange("(c p) n -> p c n", p=P)).then_inc(w_in, 16)
            sp.dma_start(k.wv[:, :, :], k.L3_W[:, 2 * D:3 * D].rearrange("(c p) n -> p c n", p=P)).then_inc(w_in, 16)
            for i in range(PLAIN, PLAIN + T):
                plain_load(nc, k, sp, i)
                plain_store(nc, k, sp, i - 2)
            sp.wait_ge(w_in, 32)

        @block.tensor
        def _(pe):
            def turn(t):
                for s, rows in enumerate((k.src_rows_sb, k.dst_rows_sb)):
                    if t >= 1:
                        pe.wait_ge(turned_out, 2 * t - 1 + s)
                    for c in range(KB):
                        last = nc.tensor.transpose(p_T[s][:, c * P:(c + 1) * P], rows[:, t, c * P:(c + 1) * P],
                                                   k.ident[:, :])
                    last.then_inc(turned, 1)

            def scores(t):
                pe.wait_ge(aw_done, t + 1)
                if t:
                    pe.wait_ge(diag_done, t)
                nc.tensor.transpose(p_w[:, :], k.scores[:, t, :], k.ident[:, :]).then_inc(aw_turned, 1)

            def spread_scores(t):
                pe.wait_ge(diag_done, t + 1)
                if t:
                    pe.wait_ge(cand_done, t)
                for half in range(2):
                    hs = slice(half * HEADS // 2, (half + 1) * HEADS // 2)
                    last = nc.tensor.matmul(p_all[:, hs, :], k.ones[0:HEADS, :], diag[:, hs, :], start=True, stop=True)
                last.then_inc(spread, 1)

            turn(0)
            pe.wait_ge(w_in, 32)
            for t in range(T + 1):
                if t < T:
                    pe.wait_ge(turned_out, 2 * t + 2)
                    if t:
                        pe.wait_ge(q_out, t)
                    for c in range(KB):
                        last = nc.tensor.matmul(p_q[:, :], srcT[t % 2][:, c, :], wqk[:, c, 0:D],
                                                start=(c == 0), stop=(c == KB - 1))
                    last.then_inc(q_done, 1)
                if t:
                    scores(t - 1)
                if t < T:
                    if t + 1 < T:
                        turn(t + 1)
                    if t:
                        pe.wait_ge(prod_done, t)
                    for c in range(KB):
                        last = nc.tensor.matmul(p_k[:, :], k.dst_rows_sb[:, t, c * P:(c + 1) * P], wqk[:, c, D:2 * D],
                                                start=(c == 0), stop=(c == KB - 1))
                    last.then_inc(k_done, 1)
                if t:
                    spread_scores(t - 1)

        @block.scalar
        def _(act):
            def turn_out(t):
                act.wait_ge(turned, 2 * t + 1)
                if t >= 2:
                    act.wait_ge(q_done, t - 1)
                nc.scalar.activation(srcT[t % 2][:, :, :], p_T[0][:, :].rearrange("p (c n) -> p c n", c=KB), ACT.Copy
                                     ).then_inc(turned_out, 1)
                act.wait_ge(turned, 2 * t + 2)
                nc.scalar.activation(k.dst_rows_sb[:, t, :], p_T[1][:, :], ACT.Copy).then_inc(turned_out, 1)

            turn_out(0)
            for t in range(T):
                if t >= 2:
                    act.wait_ge(cand_done, t - 1)
                same = k.same_src[:, t, :] if t < T - 1 else k.same_src_last[:, :]
                nc.scalar.activation(away[t % 2][:, :], same, ACT.Copy, bias=-BIG, scale=BIG).then_inc(away_done, 1)
                act.wait_ge(q_done, t + 1)
                if t >= 2:
                    act.wait_ge(prod_done, t - 1)
                nc.scalar.activation(q[t % 2][:, :], p_q[:, :], ACT.Copy, scale=float(HD) ** -0.5).then_inc(q_out, 1)
                if t + 1 < T:
                    turn_out(t + 1)
                if t:
                    plain_row(nc, k, act, PLAIN + t - 1)

        @block.vector
        def _(dve):
            def merge(t):
                dve.wait_ge(known_in, 16 * (t + 1))
                nc.vector.tensor_tensor(known[t % 2][:, :], known[t % 2][:, :], tile_max[t % 2][:, :], ALU.max
                                        ).then_inc(merged, 1)

            def tile_maximum(t):
                dve.wait_ge(spread, t + 1)
                dve.wait_ge(away_done, t + 1)
                if t:
                    dve.wait_ge(tile_max_done, t)
                nc.vector.tensor_tensor(cand[:, :, :], p_all[:, :, :],
                                        away[t % 2][:, :].rearrange("p (a e) -> p a e", a=1)
                                        .to_broadcast([P, HEADS, P]), ALU.add).then_inc(cand_done, 1)
                dve.wait_ge(cand_done, t + 1)
                if t >= 2:
                    dve.wait_ge(merged, t - 1)
                nc.vector.tensor_reduce(tile_max[t % 2][:, :], cand[:, :, :], AX_X, ALU.max).then_inc(tile_max_done, 1)
                dve.wait_ge(tile_max_done, t + 1)

            for t in range(T + 1):
                if t < T:
                    dve.wait_ge(k_done, t + 1)
                    dve.wait_ge(q_out, t + 1)
                    if t:
                        dve.wait_ge(aw_done, t)
                    nc.vector.tensor_tensor(prod[:, :], p_k[:, :], q[t % 2][:, :], ALU.mult).then_inc(prod_done, 1)
                    dve.wait_ge(prod_done, t + 1)
                    nc.vector.tensor_reduce(k.scores[:, t, :], prod[:, :].rearrange("p (h f) -> p h f", h=HEADS), AX_X,
                                            ALU.add).then_inc(aw_done, 1)
                if t:
                    tile_maximum(t - 1)
                    merge(t - 1)
                if t < T:
                    dve.wait_ge(aw_turned, t + 1)
                    if t:
                        dve.wait_ge(spread, t)
                    nc.vector.tensor_tensor(
                        diag[:, :, :], p_w[:, :].rearrange("h (a e) -> h a e", a=1).to_broadcast([HEADS, HEADS, P]),
                        k.ident[0:HEADS, 0:HEADS].rearrange("h (g a) -> h g a", a=1).to_broadcast([HEADS, HEADS, P]),
                        ALU.mult).then_inc(diag_done, 1)
                    plain_norm(nc, k, dve, PLAIN + t)

        @block.gpsimd
        def _(pool):
            plain_scale(nc, k, pool, PLAIN)
            for t in range(T):
                if t:
                    pool.wait_ge(max_gone, 16 * t)
                pool.indirect_dma_start(known[t % 2][:, :], None, k.max3[:, :], at_rows(k.index[:, 0, t:t + 1])
                                        ).then_inc(known_in, 16)
                if t:
                    plain_row_scale(nc, k, pool, PLAIN + t - 1)
                if t + 1 < T:
                    plain_scale(nc, k, pool, PLAIN + t + 1)
                pool.wait_ge(merged, t + 1)
                pool.indirect_dma_start(k.max3[:, :], at_rows(k.unique[:, 0, t:t + 1]), known[t % 2][:, :], None
                                        ).then_inc(max_gone, 16)
            pool.wait_ge(max_gone, 16 * T)


def values_phase(nc, k):
    with phase(nc, "v_") as (sb, ps, sem), ExitStack() as ctx:
        T = EDGE_TILES
        top = sb("top", [P, T, HEADS])
        weight = sb("weight", [P, T, HEADS])
        both = [sb(f"both{i}", [P, ATT]) for i in range(2)]
        tile_sum = [sb(f"tile_sum{i}", [P, ATT]) for i in range(2)]
        PLAIN = 3 * T
        p_v, p_S, p_W = ([ps(f"p_{n}{i}", [P, D]) for i in range(2)] for n in "vSW")
        top_in = [sem(f"top_in{i}") for i in range(4)]
        v_done, less, weighed, weights_in, both_done, s_done, s_out, scattered = (
            sem(n) for n in ("done", "less", "weighed", "weights_in", "both", "s_done", "s_out", "scattered"))
        block = ctx.enter_context(nc.Block())

        @block.sync
        def _(sp):
            for i in range(PLAIN, PLAIN + T):
                plain_load(nc, k, sp, i)
                plain_store(nc, k, sp, i - 2)
            for i in range(PLAIN + T - 2, PLAIN + T):
                plain_store(nc, k, sp, i)
            for b in range(2):
                sp.wait_ge(k.plain_gone[b], 16 * (NODE_TILES // 2))

        @block.gpsimd
        def _(pool):
            for t in range(T):
                if t >= 4:
                    pool.wait_ge(top_in[t % 4], 16 * (t // 4))
                pool.indirect_dma_start(top[:, t, :], None, k.max3[:, :], at_rows(k.index[:, 0, t:t + 1])
                                        ).then_inc(top_in[t % 4], 16)
            for t in range(T):
                plain_scale(nc, k, pool, PLAIN + t)
                plain_row_scale(nc, k, pool, PLAIN + t - 1)
                pool.wait_ge(s_out, 2 * t + 2)
                if t:
                    pool.wait_ge(scattered, 16 * t)
                pool.indirect_dma_start(k.sum3[:, :], at_rows(k.unique[:, 0, t:t + 1]), tile_sum[t % 2][:, :], None,
                                        compute_op=ALU.add).then_inc(scattered, 16)
            plain_row_scale(nc, k, pool, PLAIN + T - 1)
            pool.wait_ge(scattered, 16 * T)

        @block.tensor
        def _(pe):
            def tile_sums(t):
                pe.wait_ge(both_done, t + 1)
                pe.wait_ge(weights_in, t + 1)
                if t >= 2:
                    pe.wait_ge(s_out, 2 * t - 2)
                nc.tensor.matmul(p_S[t % 2][:, :], k.same_src[:, t, :], both[t % 2][:, 0:D], start=True, stop=True)
                nc.tensor.matmul(p_W[t % 2][:, 0:HEADS], k.same_src[:, t, :], both[t % 2][:, D:ATT], start=True,
                                 stop=True).then_inc(s_done, 1)

            for t in range(T):
                if t >= 2:
                    pe.wait_ge(both_done, t - 1)
                for c in range(KB):
                    last = nc.tensor.matmul(p_v[t % 2][:, :], k.dst_rows_sb[:, t, c * P:(c + 1) * P], k.wv[:, c, :],
                                            start=(c == 0), stop=(c == KB - 1))
                last.then_inc(v_done, 1)
                if t:
                    tile_sums(t - 1)
            tile_sums(T - 1)

        @block.vector
        def _(dve):
            for t in range(T):
                dve.wait_ge(top_in[t % 4], 16 * (t // 4 + 1))
                nc.vector.tensor_tensor(top[:, t, :], k.scores[:, t, :], top[:, t, :], ALU.subtract).then_inc(less, 1)
            for t in range(T):
                dve.wait_ge(v_done, t + 1)
                dve.wait_ge(weighed, t + 1)
                if t >= 2:
                    dve.wait_ge(s_done, t - 1)
                nc.vector.tensor_copy(both[t % 2][:, D:ATT], weight[:, t, :]).then_inc(weights_in, 1)
                nc.vector.tensor_tensor(
                    both[t % 2][:, 0:D].rearrange("p (h f) -> p h f", h=HEADS),
                    p_v[t % 2][:, :].rearrange("p (h f) -> p h f", h=HEADS),
                    weight[:, t, :].rearrange("p (h a) -> p h a", a=1).to_broadcast([P, HEADS, HD]), ALU.mult
                    ).then_inc(both_done, 1)
                plain_norm(nc, k, dve, PLAIN + t)

        @block.scalar
        def _(act):
            for t in range(T):
                act.wait_ge(less, t + 1)
                nc.scalar.activation(weight[:, t, :], top[:, t, :], ACT.Exp).then_inc(weighed, 1)
            for t in range(T):
                act.wait_ge(s_done, t + 1)
                if t >= 2:
                    act.wait_ge(scattered, 16 * (t - 1))
                nc.scalar.activation(tile_sum[t % 2][:, 0:D], p_S[t % 2][:, :], ACT.Copy).then_inc(s_out, 1)
                nc.scalar.activation(tile_sum[t % 2][:, D:ATT], p_W[t % 2][:, 0:HEADS], ACT.Copy).then_inc(s_out, 1)
                plain_row(nc, k, act, PLAIN + t - 1)
            plain_row(nc, k, act, PLAIN + T - 1)


def attended_rows_phase(nc, k):
    with phase(nc, "o_") as (sb, ps, sem), ExitStack() as ctx:
        T = EDGE_TILES
        sums = [sb(f"sums{i}", [P, ATT]) for i in range(4)]
        inv = [sb(f"inv{i}", [P, HEADS]) for i in range(2)]
        y, out = ([sb(f"{n}{i}", [P, D]) for i in range(2)] for n in ("y", "out"))
        stats, mv, small = ([sb(f"{n}{i}", [P, w]) for i in range(2)] for n, w in (("stats", 6), ("mv", 2), ("small", 4)))
        sums_in = [sem(f"sums_in{i}") for i in range(4)]
        inv_done, att, y_done, st, mv_done, sc, out_done, gone = (
            sem(n) for n in ("inv", "att", "y", "st", "mv", "sc", "out", "gone"))
        block = ctx.enter_context(nc.Block())

        @block.gpsimd
        def _(pool):
            def gather(t):
                if t >= 4:
                    pool.wait_ge(att, t - 3)
                pool.indirect_dma_start(sums[t % 4][:, :], None, k.sum3[:, :], at_rows(k.index[:, 0, t:t + 1])
                                        ).then_inc(sums_in[t % 4], 16)

            for t in range(3):
                gather(t)
            for t in range(T + 2):
                if t + 3 < T:
                    gather(t + 3)
                if t < T:
                    b = t % 2
                    pool.wait_ge(mv_done, t + 1)
                    if t >= 2:
                        pool.wait_ge(out_done, t - 1)
                    row_scale(pool, k, mv[b][:, 1:2], mv[b][:, 0:1], small[b][:, 0:1], small[b][:, 1:2],
                              small[b][:, 2:3], sc, 3 * t)
                if 0 <= t - 1 < T:
                    pool.wait_ge(out_done, t)
                    if t >= 2:
                        pool.wait_ge(gone, 16 * (t - 1))
                    pool.indirect_dma_start(k.out[:, :], at_rows(k.unique[:, 0, t - 1:t]), out[(t - 1) % 2][:, :], None
                                            ).then_inc(gone, 16)
            pool.wait_ge(gone, 16 * T)

        @block.vector
        def _(dve):
            for t in range(T):
                b = t % 2
                dve.wait_ge(sums_in[t % 4], 16 * (t // 4 + 1))
                if t >= 2:
                    dve.wait_ge(att, t - 1)
                nc.vector.reciprocal(inv[b][:, :], sums[t % 4][:, D:ATT]).then_inc(inv_done, 1)
                dve.wait_ge(inv_done, t + 1)
                if t >= 2:
                    dve.wait_ge(out_done, t - 1)
                nc.vector.tensor_tensor(
                    y[b][:, :].rearrange("p (h f) -> p h f", h=HEADS),
                    sums[t % 4][:, 0:D].rearrange("p (h f) -> p h f", h=HEADS),
                    inv[b][:, :].rearrange("p (h a) -> p h a", a=1).to_broadcast([P, HEADS, HD]), ALU.mult
                    ).then_inc(att, 1)
                dve.wait_ge(att, t + 1)
                nc.vector.tensor_tensor(y[b][:, :], y[b][:, :], k.src_rows_sb[:, t, :], ALU.add).then_inc(y_done, 1)
                dve.wait_ge(y_done, t + 1)
                nc.vector.bn_stats(stats[b][:, :], y[b][:, :]).then_inc(st, 1)
                dve.wait_ge(st, t + 1)
                if t >= 2:
                    dve.wait_ge(sc, 3 * t - 3)
                nc.vector.bn_aggr(mv[b][:, :], stats[b][:, :]).then_inc(mv_done, 1)

        @block.scalar
        def _(act):
            for t in range(T):
                b = t % 2
                act.wait_ge(sc, 3 * t + 3)
                if t >= 2:
                    act.wait_ge(gone, 16 * (t - 1))
                nc.scalar.activation(out[b][:, :], y[b][:, :], ACT.Identity, bias=small[b][:, 2:3],
                                     scale=small[b][:, 1:2]).then_inc(out_done, 1)


TABLES = [("sum0", D), ("x1", D), ("p", D), ("sum2", 8 * F), ("sum3", ATT), ("max3", HEADS)]
PASSED = ["L0_gnn_W1", "L0_gnn_b1", "L0_gnn_W2", "L0_gnn_b2", "L0_gnn_W3", "L0_gnn_b3", "L0_gnn_W4", "L0_gnn_b4",
          "L0_gnn_gamma", "L0_gnn_beta", "L1_gnn_W_l", "L1_gnn_b_l", "L1_gnn_W_r", "L1_gnn_gamma", "L1_gnn_beta",
          "L2_gnn_w_in2f_s", "L2_gnn_w_in2f_v", "L2_gnn_W1", "L2_gnn_b1", "L2_gnn_W2", "L2_gnn_b2",
          "L2_gnn_w_f2o1_s", "L2_gnn_w_f2o1_v", "L2_gnn_w_f2o2_s", "L2_gnn_w_f2o2_v", "L3_gnn_W"]
DEBUG = 0


def build(nc, args, out, debug=None):
    k = Shared()
    k.nc, k.out = nc, out
    k.x = args["x"]
    k.xT = args["xT"]
    k.src_cols = args["src_cols"]
    k.dst_cols = args["dst_cols"]
    k.src_rows = args["src_rows"]
    k.dst_rows = args["dst_rows"]
    k.f64T = args["edge_attr_64T"]
    k.f20T = args["edge_attr_20T"]
    k.y4 = args["edge_attr_4t"]
    k.cut = args["edge_weight_t"]
    k.L0_W1 = args["L0_gnn_W1"]
    k.L0_b1 = args["L0_gnn_b1"]
    k.L0_W2 = args["L0_gnn_W2"]
    k.L0_b2 = args["L0_gnn_b2"]
    k.L0_W3 = args["L0_gnn_W3"]
    k.L0_b3 = args["L0_gnn_b3"]
    k.L0_W4 = args["L0_gnn_W4"]
    k.L0_b4 = args["L0_gnn_b4"]
    k.L0_gamma = args["L0_gnn_gamma"]
    k.L0_beta = args["L0_gnn_beta"]
    k.L1_Wl = args["L1_gnn_W_l"]
    k.L1_bl = args["L1_gnn_b_l"]
    k.L1_Wr = args["L1_gnn_W_r"]
    k.L1_gamma = args["L1_gnn_gamma"]
    k.L1_beta = args["L1_gnn_beta"]
    k.L2_ws = args["L2_gnn_w_in2f_s"]
    k.L2_wv = args["L2_gnn_w_in2f_v"]
    k.L2_W1 = args["L2_gnn_W1"]
    k.L2_b1 = args["L2_gnn_b1"]
    k.L2_W2 = args["L2_gnn_W2"]
    k.L2_b2 = args["L2_gnn_b2"]
    k.L2_o1s = args["L2_gnn_w_f2o1_s"]
    k.L2_o1v = args["L2_gnn_w_f2o1_v"]
    k.L2_o2s = args["L2_gnn_w_f2o2_s"]
    k.L2_o2v = args["L2_gnn_w_f2o2_v"]
    k.L3_W = args["L3_gnn_W"]
    kinds = debug or {}
    k.sum0, k.x1, k.p, k.sum2, k.sum3, k.max3 = (
        kinds.get(name) if name in kinds else nc.dram_tensor(name, [ROWS, width], F32).ap() for name, width in TABLES)
    with ExitStack() as ctx:
        ctx.enter_context(nc.allow_non_contiguous_dma(reason="bias columns and strided weights"))
        sb = lambda name, shape, dt=F32: ctx.enter_context(nc.sbuf_tensor(name, shape, dt))
        sem = lambda name: ctx.enter_context(nc.semaphore(name))
        k.ident, k.ones, k.minus_half = sb("ident", [P, P]), sb("ones", [P, P]), sb("minus_half", [P, 4])
        k.index, k.unique = sb("index", [P, 2, EDGE_TILES], I32), sb("unique", [P, 2, EDGE_TILES], I32)
        k.inv_degree, k.share = sb("inv_degree", [P, EDGE_TILES]), sb("share", [P, EDGE_TILES])
        k.same_src, k.same_dst = sb("same_src", [P, EDGE_TILES, P]), sb("same_dst", [P, EDGE_TILES, P])
        k.same_src_last = sb("same_src_last", [P, P])
        k.filters = sb("filters", [P, EDGE_TILES, 8, F])
        k.filters_done, k.w3a_in, k.acc_zero, k.half_set, k.passed_dve, k.passed_pool = (
            sem(n) for n in ("filters_done", "w3a_in", "acc_zero", "half_set", "passed_dve", "passed_pool"))
        k.column_acc = sb("column_acc", [P, 2, D])
        with nc.sbuf_tensor("w3a", [P, KB, D], F32) as w3a:
            k.w3a = w3a
            message_phase(nc, k)
            dense_phase(nc, k)
        k.bn_scale, k.bn_shift = sb("bn_scale", [P, D]), sb("bn_shift", [P, D])
        k.src_rows_sb, k.dst_rows_sb = sb("src_rows_sb", [P, EDGE_TILES, D]), sb("dst_rows_sb", [P, EDGE_TILES, D])
        k.scores = sb("scores", [P, EDGE_TILES, HEADS])
        aggregate_phase(nc, k)
        edge_rows_phase(nc, k)
        k.plain_p_rows, k.plain_x1_rows, k.plain_y_rows = (
            [sb(f"plain_{n}{i}", [P, D]) for i in range(2)] for n in ("p", "x1", "y"))
        k.plain_stats, k.plain_mv, k.plain_small = (
            [sb(f"plain_{n}{i}", [P, w]) for i in range(2)] for n, w in (("stats", 6), ("mv", 2), ("small", 4)))
        k.plain_p_in, k.plain_x1_in, k.plain_gone = (
            [sem(f"plain_{n}{i}") for i in range(2)] for n in ("p_in", "x1_in", "gone"))
        k.plain_scaled, k.plain_shifted, k.plain_leaky, k.plain_y, k.plain_st, k.plain_mv_done, k.plain_sc, k.plain_out = (
            sem("plain_" + n) for n in ("scaled", "shifted", "leaky", "y_done", "st", "mv_done", "sc", "out"))
        equivariant_phase(nc, k)
        k.wv = sb("wv", [P, KB, D])
        scores_phase(nc, k)
        values_phase(nc, k)
        attended_rows_phase(nc, k)


def kernel(**inputs):
    import concourse.bacc as _bacc
    from concourse.bass_utils import run_bass_kernel_spmd as _run

    a = {n: np.asarray(v) for n, v in inputs.items()}

    def edges(v):
        return np.concatenate([v[:(EDGE_TILES - 1) * P], v[LAST_START:]])

    x = np.zeros((ROWS, D), a["x"].dtype)
    x[:N] = a["x"]
    arrays = {
        "x": x,
        "xT": np.ascontiguousarray(x.reshape(NODE_TILES, P, KB, P).transpose(0, 3, 2, 1)).reshape(ROWS, D),
        "edge_attr_64T": np.ascontiguousarray(edges(a["edge_attr_64"]).T),
        "edge_attr_20T": np.ascontiguousarray(edges(a["edge_attr_20"]).T),
        "edge_attr_4t": np.ascontiguousarray(edges(a["edge_attr_4"]).reshape(EDGE_TILES, P, 4).transpose(1, 0, 2)),
        "edge_weight_t": np.ascontiguousarray(edges(a["edge_weight"]).reshape(EDGE_TILES, P).T),
    }
    for n in ("src", "dst"):
        arrays[f"{n}_rows"] = a[n].reshape(1, -1)
        arrays[f"{n}_cols"] = np.ascontiguousarray(edges(a[n]).reshape(EDGE_TILES, P).T)
    for n in PASSED:
        arrays[n] = np.ascontiguousarray(a[n])

    nc = _bacc.Bacc("TRN2", target_bir_lowering=False, num_devices=1)
    args = {n: nc.dram_tensor(f"in_{n}", v.shape, mybir.dt.from_np(v.dtype), kind="ExternalInput").ap()
            for n, v in arrays.items()}
    out = nc.dram_tensor("out_rows", [ROWS, D], F32, kind="ExternalOutput").ap()
    debug = {n: nc.dram_tensor(n, [ROWS, w], F32, kind="ExternalOutput").ap() for n, w in TABLES} if DEBUG else None
    build(nc, args, out, debug)
    r = _run(nc, [{f"in_{n}": v for n, v in arrays.items()}], core_ids=[0])
    return r.results[0]["out_rows"][:N]
```

```python
from contextlib import ExitStack, contextmanager

import numpy as np

import concourse.bass as bass
from concourse import mybir

F32 = mybir.dt.float32
I32 = mybir.dt.int32
ALU = mybir.AluOpType
ACT = mybir.ActivationFunctionType
AX_X = mybir.AxisListType.X

P = 128
N = 10000
D = 512
KB = D // P
E = 2500
EDGE_TILES = -(-E // P)
LAST_START = E - P
OVERLAP = (EDGE_TILES - 1) * P - LAST_START
ROWS = 10240
NODE_TILES = ROWS // P
LAST_VALID_TILE = N // P
GROUP = 4
GROUPS = EDGE_TILES // GROUP
EDGE64, EDGE20 = 64, 20
F = 32
B = 128
HEADS = 8
HD = D // HEADS
ATT = D + HEADS
LN_EPS = 1e-5
PLAIN_BUFS = 4
LOG2 = 0.6931471805599453
BIG = 3.0e38


class Shared:
    pass


def at_rows(index_column):
    return bass.IndirectOffsetOnAxis(ap=index_column, axis=0)


def message_phase(nc, k):
    with phase(nc, "m_") as (sb, ps, sem), ExitStack() as ctx:

        w1 = sb("w1", [P, 2 * KB, D])
        w1a = sb("w1a", [EDGE64, D])
        w2 = sb("w2", [P, KB, D])
        w3b = sb("w3b", [P, KB, D])
        bias = sb("bias", [P, 2, KB])
        attrT = [sb(f"attrT{i}", [EDGE64, D]) for i in range(2)]
        x_in = sb("x_in", [P, 2, 2, D])
        xT = sb("xT", [P, 2, 2, KB, D])
        hidT = [sb("hid1T", [P, 2, KB, D]), sb("hid2T", [P, 2, KB, D])]
        h = sb("h", [P, 2, D])
        den = sb("den", [P, 2, D])
        rec = sb("rec", [P, 2, D])
        msg = sb("msg", [P, 2, D])
        tile_sum = sb("tile_sum", [P, 2, D])
        p_T = [ps(f"p_T{i}", [P, D]) for i in range(2)]
        p_H = [ps(f"p_H{i}", [P, D]) for i in range(3)]
        p_F = ps("p_F", [P, D])
        p_C = ps("p_C", [P, D])
        p_S = ps("p_S", [P, D])

        PARTS, FILLS = 4, 10
        COUNTS = (3, 3, 2, 2, 3, 3, 0, 0)
        row_i = sb("row_i", [P, E], I32)
        col_f = sb("col_f", [P, 2, EDGE_TILES])
        repeated, unique_f = sb("repeated", [P, 2, EDGE_TILES]), sb("unique_f", [P, 2, EDGE_TILES])
        counted = sb("counted", [P, E // PARTS])
        masked = counted[:, 0:GROUP * P].rearrange("p (t e) -> p t e", t=GROUP)
        degree = sb("degree", [P, PARTS, EDGE_TILES])
        earlier = sb("earlier", [P, P])
        dummy_i, dummy_f = sb("dummy_i", [P, 1], I32), sb("dummy_f", [P, 1])
        b3_row = tile_sum[:, 0, :]
        f20T = [sb(f"f20T{i}", [EDGE20, D]) for i in range(2)]
        w1e, b1e, w2e = sb("w1e", [EDGE20, F]), sb("b1e", [F, 1]), sb("w2e", [F + 1, 6 * F])
        y4, cut = sb("y4", [P, EDGE_TILES, 4]), sb("cut", [P, EDGE_TILES])
        mag = sb("mag", [F, D])
        hT = sb("hT", [F + 1, D])
        wf = sb("wf", [P, 4, F])

        rows_in, cols_in, b3_in, filt_in, sum0_set = (
            sem("rows_in"), sem("cols_in"), sem("b3_in"), sem("filt_in"), sem("sum0_set"))
        attr_in, f20_in = [sem(f"attr_in{i}") for i in range(2)], [sem(f"f20_in{i}") for i in range(2)]
        const_done, v, src_rows_used, unique_done = sem("const"), sem("setup_v"), sem("src_rows_used"), sem("unique")
        pre_h, act_h, pos_done, h20_done, pre_w = sem("pre_h"), sem("act_h"), sem("pos"), sem("h20"), sem("pre_w")
        w_in, w2_in, w3_in, small_in = sem("w1_in"), sem("w2_in"), sem("w3_in"), sem("small_in")
        gathered = [sem(f"gathered{i}") for i in range(2)]
        turned, turned_out = sem("turned"), sem("turned_out")
        pre, h_done, exp_done, den_done, rec_done, step_done, hid_done = (
            sem("pre"), sem("h"), sem("exp"), sem("den"), sem("rec"), sem("step"), sem("hid"))
        c_done, c_out, s_done, s_out, scattered = (
            sem("c_done"), sem("c_out"), sem("s_done"), sem("s_out"), sem("scattered0"))

        slots = []
        for it in range(GROUPS + 2):
            slots += [(0, it, q) for q in range(GROUP) if it < GROUPS]
            slots += [(1, it - 1, q) for q in range(GROUP) if it >= 1]
        chunk = {}
        for layer, g, q in slots:
            if g < GROUPS:
                chunk[layer, g, q] = len(chunk)
        CHUNKS = len(chunk)
        STEPS = CHUNKS // GROUPS

        def hid_buf(layer, g):
            return hidT[layer][:, g % hidT[layer].shape[1], :, :]

        block = ctx.enter_context(nc.Block())

        @block.sync
        def _(sp):
            sp.dma_start(k.index[:, 0, :], k.src_cols).then_inc(cols_in, 16)
            sp.dma_start(k.index[:, 1, :], k.dst_cols).then_inc(cols_in, 16)
            sp.dma_start(w1[:, :, :], k.L0_W1[0:2 * D, :].rearrange("(c p) n -> p c n", p=P)).then_inc(w_in, 16)
            sp.dma_start(w1a[:, :], k.L0_W1[2 * D:2 * D + EDGE64, :]).then_inc(w_in, 16)

            def load_group(g):
                if g >= 2:
                    sp.wait_ge(pre, chunk[0, g - 2, GROUP - 1] + 1)
                sp.dma_start(attrT[g % 2][:, :], k.f64T[:, g * D:(g + 1) * D]).then_inc(attr_in[g % 2], 16)
                if g >= 2:
                    sp.wait_ge(pre_h, g - 1)
                sp.dma_start(f20T[g % 2][:, :], k.f20T[:, g * D:(g + 1) * D]).then_inc(f20_in[g % 2], 16)

            load_group(0)
            load_group(1)
            sp.wait_ge(src_rows_used, 1)
            sp.dma_start(row_i[:, :], k.dst_rows.to_broadcast([P, E])).then_inc(rows_in, 16)
            sp.wait_ge(turned, 2 * GROUP - 2)
            sp.dma_start(w2[:, :, :], k.L0_W2.rearrange("(c p) n -> p c n", p=P)).then_inc(w2_in, 16)
            sp.dma_start(w3b[:, :, :], k.L0_W3[D:2 * D, :].rearrange("(c p) n -> p c n", p=P)).then_inc(w3_in, 16)
            sp.wait_ge(b3_in, 16)
            some = NODE_TILES // FILLS
            for part in range(FILLS):
                sp.wait_ge(pre, part + 1)
                sp.dma_start(k.sum0.rearrange("(p n) d -> p n d", p=P)[:, part * some:(part + 1) * some, :],
                             b3_row.rearrange("p (a d) -> p a d", a=1).to_broadcast([P, some, D])
                             ).then_inc(sum0_set, 16)
            for g in range(2, GROUPS):
                load_group(g)
            sp.dma_start(k.w3a[:, :, :], k.L0_W3[0:D, :].rearrange("(c p) n -> p c n", p=P)).then_inc(k.w3a_in, 16)

        @block.gpsimd
        def _(pool):
            pool.memset(k.ones[:, :], 1.0).then_inc(const_done, 1)
            pool.memset(k.ident[:, :], 0.0).then_inc(const_done, 1)
            pool.memset(k.minus_half[:, :], -0.5).then_inc(k.half_set, 1)
            pool.iota(dummy_i[:, :], [[0, 1]], base=N, channel_multiplier=1).then_inc(const_done, 1)
            pool.wait_ge(const_done, 3)
            pool.affine_select(out=k.ident[:, :], in_=k.ident[:, :], compare_op=ALU.not_equal, fill=1.0,
                               base=0, pattern=[[-1, P]], channel_multiplier=1).then_inc(const_done, 1)
            pool.affine_select(out=earlier[:, :], in_=k.ones[:, :], compare_op=ALU.is_gt, fill=0.0,
                               base=0, pattern=[[-1, P]], channel_multiplier=1).then_inc(const_done, 1)

            def gather(t):
                if t >= 2:
                    pool.wait_ge(turned, 2 * (t - 1))
                for s in range(2):
                    pool.indirect_dma_start(
                        x_in[:, t % 2, s, :], None, k.x[:, :],
                        at_rows(k.index[:, s, t:t + 1])).then_inc(gathered[t % 2], 16)

            def finish_chunk(c, layer, g, q):
                pool.wait_ge(step_done, c + 1)
                if layer == 0 and g >= 2:
                    pool.wait_ge(pre, chunk[1, g - 2, GROUP - 1] + 1)
                if layer == 1 and g >= 2:
                    pool.wait_ge(c_done, GROUP * (g - 1))
                nc.gpsimd.tensor_tensor(hid_buf(layer, g)[:, q, :], rec[:, c % 2, :], h[:, c % 2, :],
                                        ALU.add).then_inc(hid_done, 1)

            def scatter(n):
                pool.wait_ge(s_out, n + 1)
                if n >= 1:
                    pool.wait_ge(scattered, 16 * n)
                else:
                    pool.wait_ge(sum0_set, 16 * FILLS)
                    pool.wait_ge(unique_done, 1)
                pool.indirect_dma_start(
                    k.sum0[:, :], at_rows(k.unique[:, 1, n:n + 1]),
                    tile_sum[:, n % 2, :], None, compute_op=ALU.add).then_inc(scattered, 16)

            pool.wait_ge(cols_in, 32)
            for t in range(GROUP + 1):
                gather(t)
            for i, (layer, g, q) in enumerate(slots):
                if i and slots[i - 1] in chunk:
                    finish_chunk(chunk[slots[i - 1]], *slots[i - 1])
                if layer == 0:
                    t = GROUP * (g + 1) + q + 1
                    if t < EDGE_TILES:
                        gather(t)
                elif g >= 1:
                    n = GROUP * (g - 1) + q - 1
                    if n >= 0:
                        scatter(n)
            scatter(EDGE_TILES - 1)
            pool.wait_ge(scattered, 16 * EDGE_TILES)

        @block.tensor
        def _(pe):
            def turn(t):
                pe.wait_ge(gathered[t % 2], 32 * (t // 2 + 1))
                for s in range(2):
                    if 2 * t + s >= 2:
                        pe.wait_ge(turned_out, 2 * t + s - 1)
                    for c in range(KB):
                        last = pe.transpose(p_T[s][:, c * P:(c + 1) * P], x_in[:, t % 2, s, c * P:(c + 1) * P],
                                            k.ident[:, :])
                    last.then_inc(turned, 1)

            def tile_sums(n):
                pe.wait_ge(c_out, n + 1)
                if n >= 1:
                    pe.wait_ge(s_out, n)
                pe.matmul(p_S[:, :], k.same_dst[:, n, :], msg[:, n % 2, :], start=True, stop=True
                          ).then_inc(s_done, 1)

            def filter_hidden(g):
                pe.wait_ge(f20_in[g % 2], 16 * (g // 2 + 1))
                if g:
                    pe.wait_ge(k.filters_done, GROUP * g)
                else:
                    pe.wait_ge(filt_in, 16 * 6)
                pe.matmul(p_F[0:F, :], w1e[:, :], f20T[g % 2][:, :], start=True, stop=True).then_inc(pre_h, 1)

            def filter_output(g):
                pe.wait_ge(act_h, 3 * g + 1)
                pe.wait_ge(h20_done, g + 1)
                pe.wait_ge(v, 1)
                for j in range(GROUP):
                    last = pe.matmul(p_F[:, j * P:(j + 1) * P].rearrange("p (c f) -> p c f", c=4),
                                     hT[:, j * P:(j + 1) * P],
                                     w2e[:, :].rearrange("k (f c) -> k c f", c=6)[:, 0:4, :], start=True, stop=True)
                last.then_inc(pre_w, 1)

            pe.wait_ge(const_done, 5)
            for t in range(GROUP):
                turn(t)
            pe.wait_ge(w_in, 32)
            for layer, g, q in slots:
                if g < GROUPS:
                    c = chunk[layer, g, q]
                    if c >= 3:
                        pe.wait_ge(h_done, c - 2)
                    out = p_H[c % 3][:, :]
                    cols = slice(q * P, (q + 1) * P)
                    if layer == 0:
                        pe.wait_ge(turned_out, 2 * GROUP * (g + 1))
                        for s in range(2):
                            for b in range(KB):
                                pe.matmul(out, w1[:, s * KB + b, cols], xT[:, g % 2, s, b, :],
                                          start=(s == 0 and b == 0), stop=False)
                        pe.wait_ge(attr_in[g % 2], 16 * (g // 2 + 1))
                        pe.matmul(out, w1a[:, cols], attrT[g % 2][:, :], start=False, stop=True).then_inc(pre, 1)
                        if g + 1 < GROUPS:
                            turn(GROUP * (g + 1) + q)
                    else:
                        pe.wait_ge(w2_in, 16)
                        pe.wait_ge(hid_done, chunk[0, g, GROUP - 1] + 1)
                        for b in range(KB):
                            last = pe.matmul(out, w2[:, b, cols], hid_buf(0, g)[:, b, :],
                                             start=(b == 0), stop=(b == KB - 1))
                        last.then_inc(pre, 1)
                    if c % STEPS == 1:
                        filter_hidden(c // STEPS)
                    if c % STEPS == 5:
                        filter_output(c // STEPS)
                if layer == 1 and g >= 1:
                    n = GROUP * (g - 1) + q
                    if n == 0:
                        pe.wait_ge(unique_done, 1)
                    pe.wait_ge(w3_in, 16)
                    pe.wait_ge(hid_done, chunk[1, g - 1, GROUP - 1] + 1)
                    if n >= 1:
                        pe.wait_ge(c_out, n)
                    for b in range(KB):
                        last = pe.matmul(p_C[:, :], hid_buf(1, g - 1)[:, b, q * P:(q + 1) * P], w3b[:, b, :],
                                         start=(b == 0), stop=(b == KB - 1))
                    last.then_inc(c_done, 1)
                    if n >= 1:
                        tile_sums(n - 1)
            tile_sums(EDGE_TILES - 1)

        @block.scalar
        def _(act):
            def turn_out(t):
                for s in range(2):
                    g = t // GROUP
                    act.wait_ge(turned, 2 * t + s + 1)
                    if g >= 2:
                        act.wait_ge(pre, chunk[0, g - 2, GROUP - 1] + 1)
                    nc.scalar.activation(xT[:, g % 2, s, :, (t % GROUP) * P:(t % GROUP + 1) * P],
                                         p_T[s][:, :].rearrange("p (c e) -> p c e", c=KB), ACT.Copy
                                         ).then_inc(turned_out, 1)

            def message_out(n):
                act.wait_ge(c_done, n + 1)
                if n >= 2:
                    act.wait_ge(s_done, n - 1)
                nc.scalar.activation(msg[:, n % 2, :], p_C[:, :], ACT.Copy).then_inc(c_out, 1)

            def sum_out(n):
                act.wait_ge(s_done, n + 1)
                if n == 0:
                    act.wait_ge(sum0_set, 16 * FILLS)
                if n >= 2:
                    act.wait_ge(scattered, 16 * (n - 1))
                nc.scalar.activation(tile_sum[:, n % 2, :], p_S[:, :], ACT.Copy).then_inc(s_out, 1)

            def filter_logarithms(g):
                act.wait_ge(pos_done, g + 1)
                for i, (out, in_, func, bias, scale) in enumerate((
                        (mag, p_F[0:F, :], ACT.Abs, b1e[:, 0:1], 1.0),
                        (mag, mag[:, :], ACT.Exp, 0.0, -1.0),
                        (mag, mag[:, :], ACT.Ln, 1.0, 1.0))):
                    if i == 0 and g:
                        act.wait_ge(h20_done, g)
                    nc.scalar.activation(out[:, :], in_, func, bias=bias, scale=scale).then_inc(act_h, 1)
                    act.wait_ge(act_h, 3 * g + i + 1)

            act.dma_start(row_i[:, :], k.src_rows.to_broadcast([P, E])).then_inc(rows_in, 16)
            act.dma_start(b3_row, k.L0_b3.rearrange("(a n) -> a n", a=1).to_broadcast([P, D])).then_inc(b3_in, 16)
            for i, b in enumerate((k.L0_b1, k.L0_b2)):
                for q in range(KB):
                    act.dma_start(bias[:, i, q:q + 1], b[q * P:(q + 1) * P].rearrange("(p a) -> p a", a=1)
                                  ).then_inc(small_in, 16)
            act.dma_start(w1e[:, :], k.L2_W1).then_inc(filt_in, 16)
            act.dma_start(b1e[:, :], k.L2_b1.rearrange("(f a) -> f a", a=1)).then_inc(filt_in, 16)
            act.dma_start(w2e[0:F, :], k.L2_W2).then_inc(filt_in, 16)
            act.dma_start(w2e[F:F + 1, :], k.L2_b2.rearrange("(a f) -> a f", a=1)).then_inc(filt_in, 16)
            act.dma_start(y4[:, :, :], k.y4).then_inc(filt_in, 16)
            act.dma_start(cut[:, :], k.cut).then_inc(filt_in, 16)
            for t in range(GROUP):
                turn_out(t)
            for layer, g, q in slots:
                if g < GROUPS:
                    c = chunk[layer, g, q]
                    act.wait_ge(h_done, c + 1)
                    if c >= 2:
                        act.wait_ge(rec_done, c - 1)
                    nc.scalar.activation(den[:, c % 2, :], h[:, c % 2, :], ACT.Exp).then_inc(exp_done, 1)
                    act.wait_ge(exp_done, c + 1)
                    nc.scalar.activation(den[:, c % 2, :], den[:, c % 2, :], ACT.Square, bias=1.0
                                         ).then_inc(den_done, 1)
                    act.wait_ge(den_done, 2 * c + 1)
                    nc.scalar.activation(den[:, c % 2, :], den[:, c % 2, :], ACT.Copy, bias=1.0
                                         ).then_inc(den_done, 1)
                if layer == 0 and g + 1 < GROUPS:
                    turn_out(GROUP * (g + 1) + q)
                if layer == 1 and g >= 1:
                    n = GROUP * (g - 1) + q
                    message_out(n)
                    if n >= 1:
                        sum_out(n - 1)
                if g < GROUPS and chunk[layer, g, q] % STEPS == 2:
                    filter_logarithms(chunk[layer, g, q] // STEPS)
            sum_out(EDGE_TILES - 1)

        @block.vector
        def _(dve):
            def divide(c):
                dve.wait_ge(den_done, 2 * c + 2)
                if c >= 2:
                    dve.wait_ge(hid_done, c - 1)
                nc.vector.reciprocal(rec[:, c % 2, :], den[:, c % 2, :]).then_inc(rec_done, 1)
                dve.wait_ge(rec_done, c + 1)
                nc.vector.scalar_tensor_tensor(out=rec[:, c % 2, :], in0=h[:, c % 2, :], scalar=-2.0,
                                               in1=rec[:, c % 2, :], op0=ALU.mult, op1=ALU.mult
                                               ).then_inc(step_done, 1)

            n = [0]

            def step(ins):
                n[0] += 1
                ins.then_inc(v, 1)
                dve.wait_ge(v, n[0])

            def compare(s, same):
                for t in range(EDGE_TILES):
                    start = t * P if t < EDGE_TILES - 1 else LAST_START
                    last = nc.vector.tensor_scalar(same[:, t, :], row_i[:, start:start + P],
                                                   col_f[:, s, t:t + 1], None, ALU.is_equal)
                step(last)
                for g in range(GROUPS):
                    tiles = slice(g * GROUP, (g + 1) * GROUP)
                    step(nc.vector.tensor_tensor(
                        masked, same[:, tiles, :],
                        earlier[:, :].rearrange("p (a e) -> p a e", a=1).to_broadcast([P, GROUP, P]), ALU.mult))
                    step(nc.vector.tensor_reduce(repeated[:, s, tiles], masked, AX_X, ALU.max))
                step(nc.vector.tensor_scalar(unique_f[:, s, :], col_f[:, s, :], dummy_f[:, 0:1], -1.0,
                                             ALU.subtract, ALU.mult))
                step(nc.vector.tensor_tensor(unique_f[:, s, :], unique_f[:, s, :], repeated[:, s, :], ALU.mult))
                step(nc.vector.tensor_tensor(unique_f[:, s, :], unique_f[:, s, :], col_f[:, s, :], ALU.add))
                step(nc.vector.tensor_copy(k.unique[:, s, :], unique_f[:, s, :]))
                if s == 0:
                    step(nc.vector.tensor_copy(k.same_src_last[:, :], same[:, EDGE_TILES - 1, :]))
                step(nc.vector.memset(same[0:OVERLAP, EDGE_TILES - 1, :], 0.0))

            def count(n):
                t, part = n // PARTS, n % PARTS
                step(nc.vector.tensor_scalar(counted[:, :], row_i[:, part * (E // PARTS):(part + 1) * (E // PARTS)],
                                             col_f[:, 1, t:t + 1], None, ALU.is_equal, ALU.add,
                                             accum_out=degree[:, part, t:t + 1]))

            def filter_positive(g):
                dve.wait_ge(pre_h, g + 1)
                if g:
                    dve.wait_ge(pre_w, g)
                nc.vector.tensor_scalar(hT[0:F, :], p_F[0:F, :], b1e[:, 0:1], 0.0, ALU.add, ALU.max
                                        ).then_inc(pos_done, 1)

            def filter_softplus(g):
                dve.wait_ge(pos_done, g + 1)
                dve.wait_ge(act_h, 3 * g + 3)
                nc.vector.scalar_tensor_tensor(out=hT[0:F, :], in0=mag[:, :], scalar=-LOG2,
                                               in1=hT[0:F, :], op0=ALU.add, op1=ALU.add).then_inc(h20_done, 1)
                dve.wait_ge(h20_done, g + 1)

            def filter_tile(t):
                j = t % GROUP
                dve.wait_ge(pre_w, t // GROUP + 1)
                step(nc.vector.tensor_scalar(wf[:, :, :], p_F[:, j * P:(j + 1) * P].rearrange("p (c f) -> p c f", c=4),
                                             cut[:, t:t + 1], float(B) ** -0.5, ALU.mult, ALU.mult))
                a = k.filters[:, t, :, :]
                for c in range(4):
                    nc.vector.tensor_scalar(a[:, c, :], wf[:, 0 if c == 0 else 2, :], y4[:, t, c:c + 1], None, ALU.mult)
                for c in range(1, 4):
                    nc.vector.tensor_scalar(a[:, 3 + c, :], wf[:, 1, :], y4[:, t, c:c + 1], 3.0 ** -0.5,
                                            ALU.mult, ALU.mult)
                nc.vector.tensor_scalar(a[:, 7, :], wf[:, 3, :], y4[:, t, 0:1], None, ALU.mult
                                        ).then_inc(k.filters_done, 1)
                dve.wait_ge(k.filters_done, t + 1)

            step(nc.vector.memset(hT[F:F + 1, :], 1.0))
            dve.wait_ge(cols_in, 32)
            dve.wait_ge(const_done, 5)
            step(nc.vector.tensor_copy(col_f[:, :, :], k.index[:, :, :]))
            step(nc.vector.tensor_copy(dummy_f[:, :], dummy_i[:, :]))
            dve.wait_ge(rows_in, 16)
            compare(0, k.same_src)
            dve.sem_inc(src_rows_used, 1)
            dve.wait_ge(rows_in, 32)
            compare(1, k.same_dst)
            dve.sem_inc(unique_done, 1)
            counts = 0
            dve.wait_ge(filt_in, 16 * 6)
            dve.wait_ge(small_in, 16 * 8)
            for layer, g, q in slots:
                if g < GROUPS:
                    c = chunk[layer, g, q]
                    dve.wait_ge(pre, c + 1)
                    if c >= 2:
                        dve.wait_ge(hid_done, c - 1)
                    nc.vector.tensor_scalar(h[:, c % 2, :], p_H[c % 3][:, :], bias[:, layer, q:q + 1], None,
                                            ALU.add).then_inc(h_done, 1)
                    dve.wait_ge(h_done, c + 1)
                    if c >= 1:
                        divide(c - 1)
                    if c + 1 == CHUNKS:
                        divide(c)
                    for _ in range(COUNTS[c % STEPS]):
                        count(counts)
                        counts += 1
                    if c % STEPS == 2:
                        filter_positive(c // STEPS)
                    if c % STEPS == 3:
                        filter_softplus(c // STEPS)
                    if c % STEPS >= 6:
                        first = GROUP * (c // STEPS) + 2 * (c % STEPS - 6)
                        filter_tile(first)
                        filter_tile(first + 1)
            for part in range(1, PARTS):
                step(nc.vector.tensor_tensor(degree[:, 0, :], degree[:, 0, :], degree[:, part, :], ALU.add))
            step(nc.vector.reciprocal(k.inv_degree[:, :], degree[:, 0, :]))
            step(nc.vector.tensor_copy(k.share[:, :], k.inv_degree[:, :]))
            step(nc.vector.memset(k.share[0:OVERLAP, EDGE_TILES - 1:EDGE_TILES], 0.0))
            step(nc.vector.tensor_scalar(k.minus_share[:, :], k.share[:, :], -1.0, None, ALU.mult))


@contextmanager
def phase(nc, prefix):
    sems = []
    with ExitStack() as ctx:
        def sem(name):
            sems.append(nc.alloc_semaphore(prefix + name))
            return sems[-1]
        yield (lambda name, shape, dt=F32: ctx.enter_context(nc.sbuf_tensor(prefix + name, shape, dt)),
               lambda name, shape: ctx.enter_context(nc.psum_tensor(prefix + name, shape, F32)), sem)
    nc.clear_and_free_semaphores(sems)
    nc.all_engine_barrier()


def row_scale(pool, k, var, mean, tmp, rstd, shift, done, base, norms=1):
    factor, add = (1.0, LN_EPS) if norms == 1 else (1.0 + LN_EPS + LN_EPS ** 2, LN_EPS ** 3)
    nc = k.nc
    pool.sem_inc(k.passed_pool, 1)
    nc.gpsimd.tensor_scalar(tmp, var, factor, add, ALU.mult, ALU.add).then_inc(done, 1)
    pool.wait_ge(done, base + 1)
    nc.gpsimd.tensor_tensor(rstd, tmp, k.minus_half[:, 0:1], ALU.pow).then_inc(done, 1)
    pool.wait_ge(done, base + 2)
    pool.sem_inc(k.passed_pool, 1)
    nc.gpsimd.tensor_scalar(shift, mean, rstd, -1.0, ALU.mult, ALU.mult).then_inc(done, 1)


def dense_phase(nc, k):
    with phase(nc, "d_") as (sb, ps, sem), ExitStack() as ctx:
        two = lambda name, shape=(P, D): [sb(f"{name}{i}", list(shape)) for i in range(2)]

        xT, x, z, h, den, rec, u, uT = (two("xT", (P, KB, P)), two("x"), two("z"), two("h"),
                                        two("den"), two("rec"), two("u"), two("uT", (P, KB, P)))
        xb, y, yn, yg, xbeta, zz, x1, x1T, p_row, p_sq = (
            two("xb"), two("y"), two("yn"), two("yg"), two("xbeta"), two("zz"), two("x1"),
            two("x1T", (P, KB, P)), two("p"), two("psq"))
        stats, mv, small = two("stats", (P, 2, 6)), two("mv", (P, 2, 2)), two("small", (P, 2, 4))
        wr, w4 = sb("wr", [P, KB, D]), sb("w4", [P, KB, D])
        b4_row, gamma_row, beta_row = sb("b4_row", [P, D]), sb("gamma_row", [P, D]), sb("beta_row", [P, D])
        zeros, lowest = sb("zeros", [P, ATT]), sb("lowest", [P, HEADS])
        p_h, p_o, p_p = ([ps(f"p_{n}{i}", [P, D]) for i in range(2)] for n in "hop")
        p_uT, p_xT = ps("p_uT", [P, D]), ps("p_xT", [P, D])

        xT_in, x_in, z_in, x1_out, p_out = ([sem(f"{n}{i}") for i in range(2)]
                                            for n in ("xT_in", "x_in", "z_in", "x1_out", "p_out"))
        h_pre, h_done, exp_done, den_done, rec_done, step_done, u_done, u_turned, uT_done = (
            sem(n) for n in ("h_pre", "h_done", "exp", "den", "rec", "step", "u", "u_turned", "uT"))
        o_done, xb_done, y_done, st_done, mv_done, sc_done, yn_done, xbeta_done, yg_done, zz_done = (
            sem(n) for n in ("o", "xb", "y", "st", "mv", "sc", "yn", "xbeta", "yg", "zz"))
        st2_done, mv2_done, sc2_done, x1_done, x1_turned, x1T_done, p_done, row_done, sq_done, acc_done = (
            sem(n) for n in ("st2", "mv2", "sc2", "x1", "x1_turned", "x1T", "pp", "row", "sq", "acc"))

        wr_in, w4_in, rows_in, filled, tables_set = (
            sem("wr_in"), sem("w4_in"), sem("rows_in"), sem("filled"), sem("tables_set"))
        DEPTH, PEELED = 5, 8

        def run(eng, stages):
            def turn(i, par):
                for lag, f in stages:
                    if not isinstance(i, int) or 0 <= i - lag < NODE_TILES:
                        f(i - lag, (par - lag) % 2)
            for i in range(PEELED):
                turn(i, i % 2)
            with eng.Fori(PEELED, NODE_TILES - 2, 2) as i:
                turn(i, 0)
                turn(i + 1, 1)
            for i in range(NODE_TILES - 2, NODE_TILES + DEPTH):
                turn(i, i % 2)

        def landed(i, par):
            return 16 * (i // 2 + 1) if isinstance(i, int) else (i + (2 - par)) * 8

        def rows(table, i):
            return table[bass.ds(i * P, P), :]

        block = ctx.enter_context(nc.Block())

        @block.sync
        def _(sp):
            def load(i, b):
                if not isinstance(i, int) or i >= 2:
                    sp.wait_ge(h_pre, i - 1)
                sp.dma_start(xT[b][:, :, :], k.xT[bass.ds(i * P, P), :].rearrange("p (c n) -> p c n", c=KB)
                             ).then_inc(xT_in[b], 16)
                if not isinstance(i, int) or i >= 2:
                    sp.wait_ge(h_done, i - 1)
                sp.dma_start(z[b][:, :], rows(k.sum0, i)).then_inc(z_in[b], 16)

            def load_x(i, b):
                if not isinstance(i, int) or i >= 2:
                    sp.wait_ge(xbeta_done, i - 1)
                    sp.wait_ge(xb_done, i - 1)
                sp.dma_start(x[b][:, :], rows(k.x, i)).then_inc(x_in[b], 16)

            sp.wait_ge(filled, 2)

            def store_x1(i, b):
                sp.wait_ge(x1_done, i + 1)
                sp.dma_start(rows(k.x1, i), x1[b][:, :]).then_inc(x1_out[b], 16)

            def store_p(i, b):
                sp.wait_ge(row_done, i + 1)
                sp.dma_start(rows(k.p, i), p_row[b][:, :]).then_inc(p_out[b], 16)

            def fill(i, b):
                sp.dma_start(rows(k.sum2, i), zeros[:, 0:8 * F]).then_inc(tables_set, 16)
                sp.dma_start(rows(k.sum3, i), zeros[:, :]).then_inc(tables_set, 16)
                sp.dma_start(rows(k.max3, i), lowest[:, :]).then_inc(tables_set, 16)

            run(sp, [(0, load), (1, load_x), (3, store_x1), (5, store_p), (2, fill)])
            sp.wait_ge(tables_set, 16 * 3 * NODE_TILES)
            for b in range(2):
                sp.wait_ge(x1_out[b], 16 * (NODE_TILES // 2))
                sp.wait_ge(p_out[b], 16 * (NODE_TILES // 2))

        @block.tensor
        def _(pe):
            pe.wait_ge(k.w3a_in, 16)

            def product(out, lhsT, w, done):
                for c in range(KB):
                    last = nc.tensor.matmul(out[:, :], lhsT[:, c, :], w[:, c, :], start=(c == 0), stop=(c == KB - 1))
                last.then_inc(done, 1)

            def transposes(out, row, done):
                for c in range(KB):
                    last = nc.tensor.transpose(out[:, c * P:(c + 1) * P], row[:, c * P:(c + 1) * P], k.ident[:, :])
                last.then_inc(done, 1)

            def first(i):
                return isinstance(i, int) and i < 2

            def turn_x1(i, b):
                pe.wait_ge(x1_done, i + 1)
                if not isinstance(i, int) or i >= 1:
                    pe.wait_ge(x1T_done, i)
                transposes(p_xT, x1[b], x1_turned)

            def hidden(i, b):
                pe.wait_ge(xT_in[b], landed(i, b))
                if not first(i):
                    pe.wait_ge(h_done, i - 1)
                product(p_h[b], xT[b], k.w3a, h_pre)

            def turn_u(i, b):
                pe.wait_ge(u_done, i + 1)
                if not isinstance(i, int) or i >= 1:
                    pe.wait_ge(uT_done, i)
                transposes(p_uT, u[b], u_turned)

            def root(i, b):
                pe.wait_ge(x1T_done, i + 1)
                if isinstance(i, int) and i == 0:
                    pe.wait_ge(wr_in, 16)
                if not first(i):
                    pe.wait_ge(row_done, i - 1)
                    pe.wait_ge(sq_done, i - 1)
                product(p_p[b], x1T[b], wr, p_done)

            def output(i, b):
                pe.wait_ge(uT_done, i + 1)
                if isinstance(i, int) and i == 0:
                    pe.wait_ge(w4_in, 16)
                if not first(i):
                    pe.wait_ge(y_done, i - 1)
                product(p_o[b], uT[b], w4, o_done)

            run(pe, [(0, hidden), (1, turn_u), (3, turn_x1), (4, root), (1, output)])

        @block.scalar
        def _(act):
            first = lambda i: isinstance(i, int) and i < 2
            for out, row in ((b4_row, k.L0_b4), (gamma_row, k.L0_gamma), (beta_row, k.L0_beta)):
                act.dma_start(out[:, :], row.rearrange("(a n) -> a n", a=1).to_broadcast([P, D])).then_inc(rows_in, 16)
            act.dma_start(w4[:, :, :], k.L0_W4.rearrange("(c p) n -> p c n", p=P)).then_inc(w4_in, 16)
            act.dma_start(wr[:, :, :], k.L1_Wr.rearrange("(c p) n -> p c n", p=P)).then_inc(wr_in, 16)

            def x1_turned_out(i, b):
                act.wait_ge(x1_turned, i + 1)
                if not first(i):
                    act.wait_ge(p_done, i - 1)
                nc.scalar.activation(x1T[b][:, :, :], p_xT[:, :].rearrange("p (c n) -> p c n", c=KB), ACT.Copy
                                     ).then_inc(x1T_done, 1)

            def normalise_y(i, b):
                act.wait_ge(sc_done, 3 * i + 3)
                if not first(i):
                    act.wait_ge(yg_done, i - 1)
                nc.scalar.activation(yn[b][:, :], y[b][:, :], ACT.Identity, bias=small[b][:, 0, 2:3],
                                     scale=small[b][:, 0, 1:2]).then_inc(yn_done, 1)

            def u_turned_out(i, b):
                act.wait_ge(u_turned, i + 1)
                if not first(i):
                    act.wait_ge(o_done, i - 1)
                nc.scalar.activation(uT[b][:, :, :], p_uT[:, :].rearrange("p (c n) -> p c n", c=KB), ACT.Copy
                                     ).then_inc(uT_done, 1)

            def denominator(i, b):
                act.wait_ge(h_done, i + 1)
                if not first(i):
                    act.wait_ge(rec_done, i - 1)
                nc.scalar.activation(den[b][:, :], h[b][:, :], ACT.Exp).then_inc(exp_done, 1)
                act.wait_ge(exp_done, i + 1)
                nc.scalar.activation(den[b][:, :], den[b][:, :], ACT.Square, bias=1.0).then_inc(den_done, 1)
                act.wait_ge(den_done, 2 * i + 1)
                nc.scalar.activation(den[b][:, :], den[b][:, :], ACT.Copy, bias=1.0).then_inc(den_done, 1)

            def normalise_x1(i, b):
                act.wait_ge(sc2_done, 3 * i + 3)
                if not first(i):
                    act.wait_ge(x1_turned, i - 1)
                    act.wait_ge(x1_out[b], landed(i - 2, b))
                nc.scalar.activation(x1[b][:, :], zz[b][:, :], ACT.Identity, bias=small[b][:, 1, 2:3],
                                     scale=small[b][:, 1, 1:2]).then_inc(x1_done, 1)

            def root_out(i, b):
                act.wait_ge(p_done, i + 1)
                if not first(i):
                    act.wait_ge(p_out[b], landed(i - 2, b))
                    act.wait_ge(acc_done, 2 * i - 2)
                nc.scalar.activation(p_row[b][:, :], p_p[b][:, :], ACT.Copy).then_inc(row_done, 1)
                nc.scalar.activation(p_sq[b][:, :], p_p[b][:, :], ACT.Square).then_inc(sq_done, 1)

            run(act, [(3, normalise_x1), (2, normalise_y), (1, u_turned_out), (3, x1_turned_out),
                      (0, denominator), (4, root_out)])

        @block.vector
        def _(dve):
            first = lambda i: isinstance(i, int) and i < 2

            def residual(i, b):
                dve.wait_ge(o_done, i + 1)
                dve.wait_ge(xb_done, i + 1)
                if not first(i):
                    dve.wait_ge(yn_done, i - 1)
                nc.vector.tensor_tensor(y[b][:, :], p_o[b][:, :], xb[b][:, :], ALU.add).then_inc(y_done, 1)
                dve.wait_ge(y_done, i + 1)
                nc.vector.bn_stats(stats[b][:, 0, :], y[b][:, :]).then_inc(st_done, 1)
                dve.wait_ge(st_done, i + 1)
                if not first(i):
                    dve.wait_ge(sc_done, 3 * i - 3)
                dve.sem_inc(k.passed_dve, 1)
                nc.vector.bn_aggr(mv[b][:, 0, :], stats[b][:, 0, :]).then_inc(mv_done, 1)

            def accumulate(i, b):
                valid = P
                if isinstance(i, int) and i >= LAST_VALID_TILE:
                    valid = N % P if i == LAST_VALID_TILE else 0
                dve.wait_ge(row_done, i + 1)
                dve.wait_ge(sq_done, i + 1)
                if not isinstance(i, int) or i >= 1:
                    dve.wait_ge(acc_done, 2 * i)
                for s, part in enumerate((p_row, p_sq)):
                    if valid:
                        nc.vector.tensor_tensor(k.column_acc[0:valid, s, :], k.column_acc[0:valid, s, :],
                                                part[b][0:valid, :], ALU.add).then_inc(acc_done, 1)

            def hidden(i, b):
                dve.wait_ge(h_pre, i + 1)
                dve.wait_ge(z_in[b], landed(i, b))
                if not first(i):
                    dve.wait_ge(step_done, i - 1)
                    dve.wait_ge(u_done, i - 1)
                nc.vector.tensor_tensor(h[b][:, :], p_h[b][:, :], z[b][:, :], ALU.add).then_inc(h_done, 1)

            def second_norm(i, b):
                dve.wait_ge(yg_done, i + 1)
                dve.wait_ge(xbeta_done, i + 1)
                if not first(i):
                    dve.wait_ge(x1_done, i - 1)
                nc.vector.tensor_tensor(zz[b][:, :], yg[b][:, :], xbeta[b][:, :], ALU.add).then_inc(zz_done, 1)
                dve.wait_ge(zz_done, i + 1)
                nc.vector.bn_stats(stats[b][:, 1, :], zz[b][:, :]).then_inc(st2_done, 1)
                dve.wait_ge(st2_done, i + 1)
                if not first(i):
                    dve.wait_ge(sc2_done, 3 * i - 3)
                dve.sem_inc(k.passed_dve, 1)
                nc.vector.bn_aggr(mv[b][:, 1, :], stats[b][:, 1, :]).then_inc(mv2_done, 1)

            def divide(i, b):
                dve.wait_ge(den_done, 2 * i + 2)
                if not first(i):
                    dve.wait_ge(u_done, i - 1)
                nc.vector.reciprocal(rec[b][:, :], den[b][:, :]).then_inc(rec_done, 1)
                dve.wait_ge(rec_done, i + 1)
                nc.vector.scalar_tensor_tensor(out=rec[b][:, :], in0=h[b][:, :], scalar=-2.0, in1=rec[b][:, :],
                                               op0=ALU.mult, op1=ALU.mult).then_inc(step_done, 1)

            nc.vector.memset(k.column_acc[:, :, :], 0.0).then_inc(k.acc_zero, 1)
            dve.wait_ge(k.acc_zero, 1)
            run(dve, [(2, residual), (5, accumulate), (0, hidden), (2, second_norm), (0, divide)])

        @block.gpsimd
        def _(pool):
            first = lambda i: isinstance(i, int) and i < 2
            nc.gpsimd.memset(zeros[:, :], 0.0).then_inc(filled, 1)
            nc.gpsimd.memset(lowest[:, :], -BIG).then_inc(filled, 1)
            pool.wait_ge(rows_in, 48)

            def finish_u(i, b):
                pool.wait_ge(step_done, i + 1)
                if not first(i):
                    pool.wait_ge(u_turned, i - 1)
                nc.gpsimd.tensor_tensor(u[b][:, :], rec[b][:, :], h[b][:, :], ALU.add).then_inc(u_done, 1)

            def add_beta(i, b):
                pool.wait_ge(x_in[b], landed(i, b))
                if not first(i):
                    pool.wait_ge(zz_done, i - 1)
                nc.gpsimd.tensor_tensor(xbeta[b][:, :], x[b][:, :], beta_row[:, :], ALU.add).then_inc(xbeta_done, 1)

            def scale_y(i, b):
                pool.wait_ge(mv_done, i + 1)
                if not first(i):
                    pool.wait_ge(yn_done, i - 1)
                row_scale(pool, k, mv[b][:, 0, 1:2], mv[b][:, 0, 0:1], small[b][:, 0, 0:1], small[b][:, 0, 1:2],
                          small[b][:, 0, 2:3], sc_done, 3 * i)

            def add_b4(i, b):
                pool.wait_ge(x_in[b], landed(i, b))
                if not first(i):
                    pool.wait_ge(y_done, i - 1)
                nc.gpsimd.tensor_tensor(xb[b][:, :], x[b][:, :], b4_row[:, :], ALU.add).then_inc(xb_done, 1)

            def times_gamma(i, b):
                pool.wait_ge(yn_done, i + 1)
                if not first(i):
                    pool.wait_ge(zz_done, i - 1)
                nc.gpsimd.tensor_tensor(yg[b][:, :], yn[b][:, :], gamma_row[:, :], ALU.mult).then_inc(yg_done, 1)

            def scale_x1(i, b):
                pool.wait_ge(mv2_done, i + 1)
                if not first(i):
                    pool.wait_ge(x1_done, i - 1)
                row_scale(pool, k, mv[b][:, 1, 1:2], mv[b][:, 1, 0:1], small[b][:, 1, 0:1], small[b][:, 1, 1:2],
                          small[b][:, 1, 2:3], sc2_done, 3 * i)

            run(pool, [(1, finish_u), (2, scale_y), (2, add_beta), (2, times_gamma), (1, add_b4), (2, scale_x1)])


def aggregate_phase(nc, k):
    with phase(nc, "a_") as (sb, ps, sem), ExitStack() as ctx:

        wl = sb("wl", [P, KB, D])
        old = sb("old", [P, EDGE_TILES, D])
        xT = [sb(f"xT{i}", [P, KB, P]) for i in range(2)]
        msg, square = ([sb(f"{n}{i}", [P, D]) for i in range(2)] for n in ("msg", "square"))
        tile_sum = k.dst_rows_sb
        gamma, beta, bl, mean, var, tmp = (sb(n, [P, D]) for n in ("gamma", "beta", "bl", "mean", "var", "tmp"))
        compact, power, diag = sb("compact", [P, KB]), sb("power", [P, KB]), msg[0]
        p_T, p_A, p_S = ([ps(f"p_{n}{i}", [P, D]) for i in range(2)] for n in "TAS")
        p_sum, p_sq = ps("p_sum", [P, D]), ps("p_sq", [P, D])

        x_in, new_in = [sem(f"x_in{i}") for i in range(4)], [sem(f"new_in{i}") for i in range(4)]
        old_in, w_in, turned, turned_out, a_done, a_out, s_done, s_out, scattered = (
            sem(n) for n in ("old_in", "w_in", "turned", "turned_out", "done", "out", "s_done", "s_out", "scattered"))
        old_sq, new_sq, corrected, summed, fin, power_done, diag_done, power_spread = (
            sem(n) for n in ("old_sq", "new_sq", "corrected", "summed", "fin", "power", "diag", "power_spread"))

        block = ctx.enter_context(nc.Block())

        @block.sync
        def _(sp):
            sp.dma_start(wl[:, :, :], k.L1_Wl.rearrange("(c p) n -> p c n", p=P)).then_inc(w_in, 16)
            for out, r in ((gamma, k.L1_gamma), (beta, k.L1_beta), (bl, k.L1_bl)):
                sp.dma_start(out[:, :], r.rearrange("(a n) -> a n", a=1).to_broadcast([P, D])).then_inc(w_in, 16)

        @block.gpsimd
        def _(pool):
            for t in range(EDGE_TILES):
                if t >= 4:
                    pool.wait_ge(x_in[t % 4], 16 * (t // 4))
                pool.indirect_dma_start(k.src_rows_sb[:, t, :], None, k.x1[:, :], at_rows(k.index[:, 0, t:t + 1])
                                        ).then_inc(x_in[t % 4], 16)
                pool.indirect_dma_start(old[:, t, :], None, k.p[:, :], at_rows(k.index[:, 1, t:t + 1])
                                        ).then_inc(old_in, 16)
            pool.wait_ge(old_in, 16 * EDGE_TILES)
            for t in range(EDGE_TILES):
                pool.wait_ge(s_out, t + 1)
                if t:
                    pool.wait_ge(scattered, 16 * t)
                pool.indirect_dma_start(k.p[:, :], at_rows(k.unique[:, 1, t:t + 1]), tile_sum[:, t, :], None,
                                        compute_op=ALU.add).then_inc(scattered, 16)
            pool.wait_ge(scattered, 16 * EDGE_TILES)
            for t in range(EDGE_TILES):
                if t >= 4:
                    pool.wait_ge(new_in[t % 4], 16 * (t // 4))
                pool.indirect_dma_start(k.dst_rows_sb[:, t, :], None, k.p[:, :], at_rows(k.index[:, 1, t:t + 1])
                                        ).then_inc(new_in[t % 4], 16)
            pool.wait_ge(fin, 6)
            nc.gpsimd.tensor_tensor(power[:, :], compact[:, :], k.minus_half[:, :], ALU.pow).then_inc(power_done, 1)

        @block.tensor
        def _(pe):
            def turn(t):
                pe.wait_ge(x_in[t % 4], 16 * (t // 4 + 1))
                if t >= 2:
                    pe.wait_ge(turned_out, t - 1)
                for c in range(KB):
                    last = nc.tensor.transpose(p_T[t % 2][:, c * P:(c + 1) * P],
                                               k.src_rows_sb[:, t, c * P:(c + 1) * P], k.ident[:, :])
                last.then_inc(turned, 1)

            def tile_sums(t):
                pe.wait_ge(a_out, t + 1)
                if t >= 2:
                    pe.wait_ge(s_out, t - 1)
                nc.tensor.matmul(p_S[t % 2][:, :], k.same_dst[:, t, :], msg[t % 2][:, :], start=True, stop=True
                                 ).then_inc(s_done, 1)

            turn(0)
            pe.wait_ge(w_in, 64)
            for t in range(EDGE_TILES):
                if t + 1 < EDGE_TILES:
                    turn(t + 1)
                pe.wait_ge(turned_out, t + 1)
                if t >= 2:
                    pe.wait_ge(a_out, t - 1)
                for c in range(KB):
                    last = nc.tensor.matmul(p_A[t % 2][:, :], xT[t % 2][:, c, :], wl[:, c, :],
                                            start=(c == 0), stop=(c == KB - 1))
                last.then_inc(a_done, 1)
                if t:
                    tile_sums(t - 1)
            tile_sums(EDGE_TILES - 1)
            pe.wait_ge(corrected, 4 * EDGE_TILES)
            nc.tensor.matmul(p_sum[:, :], k.ones[:, :], k.column_acc[:, 0, :], start=True, stop=True)
            nc.tensor.matmul(p_sq[:, :], k.ones[:, :], k.column_acc[:, 1, :], start=True, stop=True
                             ).then_inc(summed, 1)
            pe.wait_ge(diag_done, 1)
            nc.tensor.matmul(p_T[0][:, :], k.ones[:, :], diag[:, :], start=True, stop=True).then_inc(power_spread, 1)

        @block.scalar
        def _(act):
            def turn_out(t):
                act.wait_ge(turned, t + 1)
                if t >= 2:
                    act.wait_ge(a_done, t - 1)
                nc.scalar.activation(xT[t % 2][:, :, :], p_T[t % 2][:, :].rearrange("p (c n) -> p c n", c=KB),
                                     ACT.Copy).then_inc(turned_out, 1)

            def sum_out(t):
                act.wait_ge(s_done, t + 1)
                nc.scalar.activation(tile_sum[:, t, :], p_S[t % 2][:, :], ACT.Copy).then_inc(s_out, 1)

            turn_out(0)
            for t in range(EDGE_TILES):
                if t + 1 < EDGE_TILES:
                    turn_out(t + 1)
                act.wait_ge(a_done, t + 1)
                if t >= 2:
                    act.wait_ge(s_done, t - 1)
                nc.scalar.activation(msg[t % 2][:, :], p_A[t % 2][:, :], ACT.Copy, scale=k.inv_degree[:, t:t + 1]
                                     ).then_inc(a_out, 1)
                if t:
                    sum_out(t - 1)
            sum_out(EDGE_TILES - 1)
            for t in range(EDGE_TILES):
                act.wait_ge(new_in[t % 4], 16 * (t // 4 + 1))
                act.wait_ge(corrected, 2 * EDGE_TILES + 2 * max(t - 1, 0))
                nc.scalar.activation(square[t % 2][:, :], k.dst_rows_sb[:, t, :], ACT.Square).then_inc(new_sq, 1)

        @block.vector
        def _(dve):
            count = [0]

            def correct(part, rows, factor):
                if count[0] >= 2:
                    dve.wait_ge(corrected, count[0] - 1)
                nc.vector.scalar_tensor_tensor(out=k.column_acc[:, part, :], in0=rows, scalar=factor,
                                               in1=k.column_acc[:, part, :], op0=ALU.mult, op1=ALU.add
                                               ).then_inc(corrected, 1)
                count[0] += 1

            dve.wait_ge(old_in, 16 * EDGE_TILES)
            for t in range(EDGE_TILES):
                if t >= 2:
                    dve.wait_ge(corrected, 2 * t - 2)
                nc.vector.tensor_tensor(square[t % 2][:, :], old[:, t, :], old[:, t, :], ALU.mult).then_inc(old_sq, 1)
                correct(0, old[:, t, :], k.minus_share[:, t:t + 1])
                dve.wait_ge(old_sq, t + 1)
                correct(1, square[t % 2][:, :], k.minus_share[:, t:t + 1])
            for t in range(EDGE_TILES):
                dve.wait_ge(new_in[t % 4], 16 * (t // 4 + 1))
                correct(0, k.dst_rows_sb[:, t, :], k.share[:, t:t + 1])
                dve.wait_ge(new_sq, t + 1)
                correct(1, square[t % 2][:, :], k.share[:, t:t + 1])
            dve.wait_ge(summed, 1)
            dve.wait_ge(w_in, 64)
            n = [0]

            def step(ins):
                n[0] += 1
                ins.then_inc(fin, 1)
                dve.wait_ge(fin, n[0])

            step(nc.vector.tensor_scalar(mean[:, :], p_sum[:, :], 1.0 / N, None, ALU.mult))
            step(nc.vector.tensor_tensor(tmp[:, :], mean[:, :], mean[:, :], ALU.mult))
            step(nc.vector.scalar_tensor_tensor(out=var[:, :], in0=p_sq[:, :], scalar=1.0 / N, in1=tmp[:, :],
                                                op0=ALU.mult, op1=ALU.subtract))
            step(nc.vector.tensor_scalar(var[:, :], var[:, :], 0.0, LN_EPS, ALU.max, ALU.add))
            ident = k.ident[:, :].rearrange("p (a f) -> p a f", a=1).to_broadcast([P, KB, P])
            tmp3 = tmp[:, :].rearrange("p (c f) -> p c f", c=KB)
            step(nc.vector.tensor_tensor(tmp3, var[:, :].rearrange("p (c f) -> p c f", c=KB), ident, ALU.mult))
            step(nc.vector.tensor_reduce(compact[:, :], tmp3, AX_X, ALU.add))
            dve.wait_ge(power_done, 1)
            nc.vector.tensor_tensor(diag[:, :].rearrange("p (c f) -> p c f", c=KB), ident,
                                    power[:, :].rearrange("p (c a) -> p c a", a=1).to_broadcast([P, KB, P]),
                                    ALU.mult).then_inc(diag_done, 1)
            dve.wait_ge(power_spread, 1)
            step(nc.vector.tensor_tensor(k.bn_scale[:, :], p_T[0][:, :], gamma[:, :], ALU.mult))
            step(nc.vector.tensor_tensor(mean[:, :], mean[:, :], bl[:, :], ALU.add))
            step(nc.vector.tensor_tensor(mean[:, :], bl[:, :], mean[:, :], ALU.subtract))
            step(nc.vector.tensor_tensor(mean[:, :], mean[:, :], k.bn_scale[:, :], ALU.mult))
            step(nc.vector.tensor_tensor(k.bn_shift[:, :], mean[:, :], beta[:, :], ALU.add))


def plain_load(nc, k, sp, i):
    b = i % PLAIN_BUFS
    if i >= PLAIN_BUFS:
        sp.wait_ge(k.plain_y, i - PLAIN_BUFS + 1)
    sp.dma_start(k.plain_p_rows[b][:, :], k.p[i * P:(i + 1) * P, :]).then_inc(k.plain_p_in[b], 16)
    sp.dma_start(k.plain_x1_rows[b][:, :], k.x1[i * P:(i + 1) * P, :]).then_inc(k.plain_x1_in[b], 16)


def plain_store(nc, k, sp, i):
    b = i % PLAIN_BUFS
    sp.wait_ge(k.plain_out, i + 1)
    sp.dma_start(k.out[i * P:(i + 1) * P, :], k.plain_y_rows[b][:, :]).then_inc(k.plain_gone[b], 16)


def plain_transfers(nc, k, sp, first, end):
    for i in range(first, end):
        plain_load(nc, k, sp, i)
        if i > max(first, PLAIN_BUFS):
            plain_store(nc, k, sp, i - 1 - PLAIN_BUFS)
    plain_store(nc, k, sp, end - 1 - PLAIN_BUFS)


def plain_scale(nc, k, pool, i):
    b = i % PLAIN_BUFS
    pool.wait_ge(k.plain_p_in[b], 16 * (i // PLAIN_BUFS + 1))
    nc.gpsimd.tensor_tensor(k.plain_p_rows[b][:, :], k.plain_p_rows[b][:, :], k.bn_scale[:, :], ALU.mult
                            ).then_inc(k.plain_scaled, 1)


def plain_shift(nc, k, engine, i):
    a = k.plain_p_rows[i % PLAIN_BUFS]
    engine.wait_ge(k.plain_scaled, i + 1)
    engine.tensor_tensor(a[:, :], a[:, :], k.bn_shift[:, :], ALU.add).then_inc(k.plain_shifted, 1)


def plain_leaky(nc, k, dve, i):
    a = k.plain_p_rows[i % PLAIN_BUFS]
    dve.wait_ge(k.plain_shifted, i + 1)
    nc.vector.scalar_tensor_tensor(out=a[:, :], in0=a[:, :], scalar=0.01, in1=a[:, :], op0=ALU.mult, op1=ALU.max
                                   ).then_inc(k.plain_leaky, 1)


def plain_residual(nc, k, dve, i):
    b = i % PLAIN_BUFS
    dve.wait_ge(k.plain_leaky, i + 1)
    dve.wait_ge(k.plain_x1_in[b], 16 * (i // PLAIN_BUFS + 1))
    if i >= PLAIN_BUFS:
        dve.wait_ge(k.plain_gone[b], 16 * (i // PLAIN_BUFS))
    nc.vector.scalar_tensor_tensor(out=k.plain_y_rows[b][:, :], in0=k.plain_x1_rows[b][:, :], scalar=2.0,
                                   in1=k.plain_p_rows[b][:, :], op0=ALU.mult, op1=ALU.add).then_inc(k.plain_y, 1)


def plain_statistics(nc, k, dve, i):
    dve.wait_ge(k.plain_y, i + 1)
    nc.vector.bn_stats(k.plain_stats[i % 2][:, :], k.plain_y_rows[i % PLAIN_BUFS][:, :]).then_inc(k.plain_st, 1)


def plain_moments(nc, k, dve, i):
    dve.wait_ge(k.plain_st, i + 1)
    if i >= 2:
        dve.wait_ge(k.plain_sc, 3 * i - 3)
    nc.vector.bn_aggr(k.plain_mv[i % 2][:, :], k.plain_stats[i % 2][:, :]).then_inc(k.plain_mv_done, 1)


def plain_norm(nc, k, dve, *tiles):
    for step in (plain_leaky, plain_residual, plain_statistics, plain_moments):
        for i in tiles:
            step(nc, k, dve, i)


def plain_row_scale(nc, k, pool, i):
    mv, small = k.plain_mv[i % 2], k.plain_small[i % PLAIN_BUFS]
    pool.wait_ge(k.plain_mv_done, i + 1)
    if i >= PLAIN_BUFS:
        pool.wait_ge(k.plain_out, i - PLAIN_BUFS + 1)
    row_scale(pool, k, mv[:, 1:2], mv[:, 0:1], small[:, 0:1], small[:, 1:2], small[:, 2:3], k.plain_sc, 3 * i,
              norms=3)


def plain_row(nc, k, act, i):
    y, small = k.plain_y_rows[i % PLAIN_BUFS], k.plain_small[i % PLAIN_BUFS]
    act.wait_ge(k.plain_sc, 3 * i + 3)
    nc.scalar.activation(y[:, :], y[:, :], ACT.Identity, bias=small[:, 2:3], scale=small[:, 1:2]
                         ).then_inc(k.plain_out, 1)


def edge_rows_phase(nc, k):
    with phase(nc, "e_") as (sb, ps, sem), ExitStack() as ctx:
        T = EDGE_TILES
        ws, wv = sb("ws", [P, F]), sb("wv", [P, F])
        other = [sb(f"other{i}", [P, D]) for i in range(4)]
        a, y = ([sb(f"{n}{i}", [P, D]) for i in range(4)] for n in ("a", "y"))
        featT = [sb(f"featT{i}", [P, D]) for i in range(2)]
        stats, mv, small = ([sb(f"{n}{i}", [P, w]) for i in range(4)] for n, w in (("stats", 6), ("mv", 2), ("small", 4)))
        edge, part, tile_sum = ([sb(f"{n}{i}", [P, w]) for i in range(2)]
                                for n, w in (("edge", 8 * F), ("part", 3 * F), ("tile_sum", 8 * F)))
        p_T, p_F, p_S = ([ps(f"p_{n}{i}", [P, D]) for i in range(2)] for n in "TFS")

        w_in = sem("w_in")
        other_in = [sem(f"other_in{i}") for i in range(4)]
        dst_scaled, src_scaled, shifted, leaky, y_done, st, mv_done, sc, x2_done = (
            sem(n) for n in ("dst_scaled", "src_scaled", "shifted", "leaky", "y", "st", "mv", "sc", "x2"))
        turned, turned_out, feat, s_part, v_part, dot, edge_done, s_done, s_out, scattered = (
            sem(n) for n in ("turned", "turned_out", "feat", "s_part", "v_part", "dot", "edge", "s_done", "s_out", "scat"))

        def rows_of(u):
            return (k.dst_rows_sb, k.src_rows_sb)[u % 2][:, u // 2, :]

        def p_of(u):
            return rows_of(u) if u % 2 == 0 else other[u % 4][:, :]

        def x1_of(u):
            return other[u % 4][:, :] if u % 2 == 0 else rows_of(u)

        block = ctx.enter_context(nc.Block())

        @block.sync
        def _(sp):
            sp.dma_start(ws[:, :], k.L2_ws).then_inc(w_in, 16)
            sp.dma_start(wv[:, :], k.L2_wv).then_inc(w_in, 16)

        @block.gpsimd
        def _(pool):
            def gather(u):
                if u >= 4:
                    if u % 2 == 0:
                        pool.wait_ge(y_done, u - 3)
                    else:
                        pool.wait_ge(src_scaled, u // 2 - 1)
                table, side = (k.x1, 1) if u % 2 == 0 else (k.p, 0)
                pool.indirect_dma_start(other[u % 4][:, :], None, table[:, :],
                                        at_rows(k.index[:, side, u // 2:u // 2 + 1])).then_inc(other_in[u % 4], 16)

            def scale(u):
                if u >= 4:
                    pool.wait_ge(y_done, u - 3)
                nc.gpsimd.tensor_tensor(a[u % 4][:, :], p_of(u), k.bn_scale[:, :], ALU.mult).then_inc(dst_scaled, 1)

            def row(u):
                b = u % 4
                pool.wait_ge(mv_done, u + 1)
                if u >= 4:
                    pool.wait_ge(x2_done, u - 3)
                row_scale(pool, k, mv[b][:, 1:2], mv[b][:, 0:1], small[b][:, 0:1], small[b][:, 1:2],
                          small[b][:, 2:3], sc, 3 * u)

            def scatter(t):
                pool.wait_ge(s_out, t + 1)
                if t:
                    pool.wait_ge(scattered, 16 * t)
                pool.indirect_dma_start(k.sum2[:, :], at_rows(k.unique[:, 0, t:t + 1]), tile_sum[t % 2][:, :], None,
                                        compute_op=ALU.add).then_inc(scattered, 16)

            for u in range(4):
                gather(u)
            scale(0)
            for t in range(T + 6):
                if 1 <= t <= T:
                    row(2 * t - 2)
                    row(2 * t - 1)
                if t + 1 < T:
                    scale(2 * t + 2)
                if 0 <= t - 5 < T:
                    scatter(t - 5)
                if t + 2 < T:
                    gather(2 * t + 4)
                    gather(2 * t + 5)
            pool.wait_ge(scattered, 16 * T)

        @block.vector
        def _(dve):
            def norm(t):
                pair = (2 * t, 2 * t + 1)
                u = 2 * t + 1
                dve.wait_ge(other_in[u % 4], 16 * (u // 4 + 1))
                if u >= 4:
                    dve.wait_ge(y_done, u - 3)
                nc.vector.tensor_tensor(a[u % 4][:, :], p_of(u), k.bn_scale[:, :], ALU.mult).then_inc(src_scaled, 1)
                for u in pair:
                    dve.wait_ge(src_scaled if u % 2 else dst_scaled, t + 1)
                    nc.vector.tensor_tensor(a[u % 4][:, :], a[u % 4][:, :], k.bn_shift[:, :], ALU.add
                                            ).then_inc(shifted, 1)
                for u in pair:
                    dve.wait_ge(shifted, u + 1)
                    nc.vector.scalar_tensor_tensor(out=a[u % 4][:, :], in0=a[u % 4][:, :], scalar=0.01,
                                                   in1=a[u % 4][:, :], op0=ALU.mult, op1=ALU.max).then_inc(leaky, 1)
                for u in pair:
                    dve.wait_ge(leaky, u + 1)
                    if u % 2 == 0:
                        dve.wait_ge(other_in[u % 4], 16 * (u // 4 + 1))
                    if u >= 4:
                        dve.wait_ge(x2_done, u - 3)
                    nc.vector.scalar_tensor_tensor(out=y[u % 4][:, :], in0=x1_of(u), scalar=2.0, in1=a[u % 4][:, :],
                                                   op0=ALU.mult, op1=ALU.add).then_inc(y_done, 1)
                for u in pair:
                    dve.wait_ge(y_done, u + 1)
                    nc.vector.bn_stats(stats[u % 4][:, :], y[u % 4][:, :]).then_inc(st, 1)
                for u in pair:
                    dve.wait_ge(st, u + 1)
                    if u >= 4:
                        dve.wait_ge(sc, 3 * u - 9)
                    nc.vector.bn_aggr(mv[u % 4][:, :], stats[u % 4][:, :]).then_inc(mv_done, 1)

            def message(t):
                b = t % 2
                e4 = edge[b][:, :].rearrange("p (c h f) -> p c h f", c=4, h=2)
                a4 = k.filters[:, t, :, :]
                dve.wait_ge(feat, t + 1)
                if t >= 2:
                    dve.wait_ge(s_done, t - 1)
                s = p_F[b][:, 0:F].rearrange("p (a f) -> p a f", a=1)
                v = p_F[b][:, F:4 * F].rearrange("p (c f) -> p c f", c=3)
                nc.vector.tensor_tensor(e4[:, :, 0, :], s.to_broadcast([P, 4, F]), a4[:, 0:4, :], ALU.mult
                                        ).then_inc(s_part, 1)
                nc.vector.tensor_tensor(e4[:, 1:4, 1, :], v, a4[:, 7:8, :].to_broadcast([P, 3, F]), ALU.mult
                                        ).then_inc(v_part, 1)
                if t >= 2:
                    dve.wait_ge(edge_done, t - 1)
                nc.vector.tensor_tensor(part[b][:, :].rearrange("p (c f) -> p c f", c=3), v, a4[:, 4:7, :], ALU.mult
                                        ).then_inc(dot, 1)
                dve.wait_ge(dot, t + 1)
                nc.vector.tensor_reduce(e4[:, 0, 1, :], part[b][:, :].rearrange("p (c f) -> p f c", c=3), AX_X,
                                        ALU.add).then_inc(edge_done, 1)

            for t in range(T + 3):
                if t < T:
                    norm(t)
                if 0 <= t - 3 < T:
                    message(t - 3)

        @block.scalar
        def _(act):
            def x2_row(u):
                b = u % 4
                act.wait_ge(sc, 3 * u + 3)
                nc.scalar.activation(rows_of(u), y[b][:, :], ACT.Identity, bias=small[b][:, 2:3],
                                     scale=small[b][:, 1:2]).then_inc(x2_done, 1)

            def turn_out(t):
                act.wait_ge(turned, t + 1)
                if t >= 2:
                    act.wait_ge(feat, t - 1)
                nc.scalar.activation(featT[t % 2][:, :], p_T[t % 2][:, :], ACT.Copy).then_inc(turned_out, 1)

            def sum_out(t):
                act.wait_ge(s_done, t + 1)
                if t >= 2:
                    act.wait_ge(scattered, 16 * (t - 1))
                nc.scalar.activation(tile_sum[t % 2][:, :], p_S[t % 2][:, 0:8 * F], ACT.Copy).then_inc(s_out, 1)

            for t in range(T + 4):
                if 1 <= t <= T:
                    x2_row(2 * t - 2)
                    x2_row(2 * t - 1)
                    turn_out(t - 1)
                if 0 <= t - 4 < T:
                    sum_out(t - 4)

        @block.tensor
        def _(pe):
            def turn(t):
                pe.wait_ge(x2_done, 2 * t + 1)
                if t >= 2:
                    pe.wait_ge(turned_out, t - 1)
                x2 = k.dst_rows_sb[:, t, :]
                vector = x2[:, B:].rearrange("p (b c) -> p c b", c=3)
                for c in range(4):
                    last = nc.tensor.transpose(p_T[t % 2][:, c * P:(c + 1) * P],
                                               x2[:, 0:B] if c == 0 else vector[:, c - 1, :], k.ident[:, :])
                last.then_inc(turned, 1)

            def features(t):
                pe.wait_ge(turned_out, t + 1)
                if t >= 2:
                    pe.wait_ge(edge_done, t - 1)
                for c in range(4):
                    last = nc.tensor.matmul(p_F[t % 2][:, c * F:(c + 1) * F], featT[t % 2][:, c * P:(c + 1) * P],
                                            (ws if c == 0 else wv)[:, :], start=True, stop=True)
                last.then_inc(feat, 1)

            def tile_sums(t):
                pe.wait_ge(s_part, t + 1)
                pe.wait_ge(v_part, t + 1)
                pe.wait_ge(edge_done, t + 1)
                if t >= 2:
                    pe.wait_ge(s_out, t - 1)
                nc.tensor.matmul(p_S[t % 2][:, 0:8 * F], k.same_src[:, t, :], edge[t % 2][:, :], start=True, stop=True
                                 ).then_inc(s_done, 1)

            pe.wait_ge(w_in, 32)
            for u in range(T + 3):
                if u < T:
                    turn(u)
                if 1 <= u <= T:
                    features(u - 1)
                if 0 <= u - 2 < T:
                    tile_sums(u - 2)


def equivariant_phase(nc, k):
    with phase(nc, "q_") as (sb, ps, sem), ExitStack() as ctx:
        U, BATCH, AHEAD = 2 * EDGE_TILES, 4, 8
        NB = U // BATCH
        LAG = 2 * BATCH
        w1s, w1v, w2s, w2v = sb("w1s", [2 * F, B]), sb("w1v", [2 * F, B]), sb("w2s", [B, B]), sb("w2v", [B, B])
        sums = [sb(f"sums{i}", [P, 8 * F]) for i in range(AHEAD)]
        sumT = [sb(f"sumT{i}", [2 * F, 4, P]) for i in range(2)]
        outT = [sb(f"outT{i}", [P, BATCH, D]) for i in range(3)]
        mag, low, logs, pos = (sb(n, [P, BATCH, B]) for n in ("mag", "low", "logs", "pos"))
        y = [sb(f"y{i}", [P, D]) for i in range(2)]
        stats, mv, small = ([sb(f"{n}{i}", [P, w]) for i in range(2)] for n, w in (("stats", 6), ("mv", 2), ("small", 4)))
        p_T = [ps(f"p_T{i}", [2 * F, 4, P]) for i in range(2)]
        p_O, p_R = ([ps(f"p_{n}{i}", [P, D]) for i in range(2)] for n in "OR")
        w_in = sem("w_in")
        sums_in = [sem(f"sums_in{i}") for i in range(AHEAD)]
        turned, turned_out, first_done, first_out, act_steps, pos_done, ssp_done, second_done = (
            sem(n) for n in ("turned", "turned_out", "first", "first_out", "act", "pos", "ssp", "second"))
        y_s, y_done, st, mv_done, sc, x3_done = (sem(n) for n in ("y_s", "y", "st", "mv", "sc", "x3"))

        def rows_of(u):
            return (k.src_rows_sb, k.dst_rows_sb)[u % 2][:, u // 2, :]

        block = ctx.enter_context(nc.Block())

        @block.sync
        def _(sp):
            for out, w in ((w1s, k.L2_o1s), (w1v, k.L2_o1v), (w2s, k.L2_o2s), (w2v, k.L2_o2v)):
                sp.dma_start(out[:, :], w).then_inc(w_in, 16)
            plain_transfers(nc, k, sp, 0, U // 2)
            sp.dma_start(k.wqk, k.L3_W[:, 0:2 * D].rearrange("(c p) n -> p c n", p=P)).then_inc(k.wqk_in, 16)

        @block.gpsimd
        def _(pool):
            def gather(u):
                if u >= AHEAD:
                    pool.wait_ge(turned, u - AHEAD + 1)
                pool.indirect_dma_start(sums[u % AHEAD][:, :], None, k.sum2[:, :],
                                        at_rows(k.index[:, u % 2, u // 2:u // 2 + 1])).then_inc(sums_in[u % AHEAD], 16)

            def row(u):
                b = u % 2
                pool.wait_ge(mv_done, u + 1)
                if u >= 2:
                    pool.wait_ge(x3_done, u - 1)
                row_scale(pool, k, mv[b][:, 1:2], mv[b][:, 0:1], small[b][:, 0:1], small[b][:, 1:2],
                          small[b][:, 2:3], sc, 3 * u)

            for u in range(AHEAD):
                gather(u)
            for u in range(U + LAG):
                if u < U and u % 2 == 0:
                    plain_scale(nc, k, pool, u // 2)
                if u > LAG:
                    row(u - LAG - 1)
                if u + AHEAD < U:
                    gather(u + AHEAD)
                if u < U and u % 2 == 1:
                    plain_row_scale(nc, k, pool, u // 2)
            row(U - 1)

        @block.tensor
        def _(pe):
            pe.wait_ge(w_in, 64)

            def turn(u):
                pe.wait_ge(sums_in[u % AHEAD], 16 * (u // AHEAD + 1))
                if u >= 2:
                    pe.wait_ge(turned_out, u - 1)
                for c in range(4):
                    last = nc.tensor.transpose(p_T[u % 2][:, c, :], sums[u % AHEAD][:, c * 2 * F:(c + 1) * 2 * F],
                                               k.ident[:, :])
                last.then_inc(turned, 1)

            def first(u):
                pe.wait_ge(turned_out, u + 1)
                if u >= 2:
                    pe.wait_ge(first_out, u - 1)
                nc.tensor.matmul(p_O[u % 2][:, 0:P], w1s[:, :], sumT[u % 2][:, 0, :], start=True, stop=True)
                nc.tensor.matmul(p_O[u % 2][:, P:D], w1v[:, :], sumT[u % 2][:, 1:4, :].rearrange("k c n -> k (c n)"),
                                 start=True, stop=True).then_inc(first_done, 1)

            def second(u):
                n = u // BATCH
                pe.wait_ge(ssp_done, n + 1)
                if u >= 2:
                    pe.wait_ge(y_done, u - 1)
                for c in range(4):
                    last = nc.tensor.matmul(p_R[u % 2][:, c * P:(c + 1) * P],
                                            outT[n % 3][:, u % BATCH, c * P:(c + 1) * P],
                                            (w2s if c == 0 else w2v)[:, :], start=True, stop=True)
                last.then_inc(second_done, 1)

            turn(0)
            for u in range(U + LAG):
                if u + 1 < U:
                    turn(u + 1)
                if u < U:
                    first(u)
                if u >= LAG:
                    second(u - LAG)

        @block.scalar
        def _(act):
            def turn_out(u):
                act.wait_ge(turned, u + 1)
                if u >= 2:
                    act.wait_ge(first_done, u - 1)
                nc.scalar.activation(sumT[u % 2][:, :, :], p_T[u % 2][:, :, :], ACT.Copy).then_inc(turned_out, 1)

            def first_product_out(u):
                n = u // BATCH
                act.wait_ge(first_done, u + 1)
                if n >= 3:
                    act.wait_ge(second_done, BATCH * (n - 2))
                nc.scalar.activation(outT[n % 3][:, u % BATCH, :], p_O[u % 2][:, :], ACT.Copy,
                                     scale=(2 * F) ** -0.5).then_inc(first_out, 1)

            def logarithms(n):
                act.wait_ge(first_out, BATCH * (n + 1))
                if n:
                    act.wait_ge(ssp_done, n)
                for step, (out, in_, func, bias, scale) in enumerate((
                        (mag[:, :, :], outT[n % 3][:, :, 0:B], ACT.Abs, 0.0, 1.0),
                        (low[:, :, :], mag[:, :, :], ACT.Exp, 0.0, -1.0),
                        (logs[:, :, :], low[:, :, :], ACT.Ln, 1.0, 1.0))):
                    nc.scalar.activation(out, in_, func, bias=bias, scale=scale).then_inc(act_steps, 1)
                    act.wait_ge(act_steps, 3 * n + step + 1)

            def x3_row(u):
                b = u % 2
                act.wait_ge(sc, 3 * u + 3)
                nc.scalar.activation(rows_of(u), y[b][:, :], ACT.Identity, bias=small[b][:, 2:3],
                                     scale=small[b][:, 1:2]).then_inc(x3_done, 1)

            turn_out(0)
            for u in range(U + LAG):
                if u + 1 < U:
                    turn_out(u + 1)
                if u < U:
                    first_product_out(u)
                if u > LAG:
                    x3_row(u - LAG - 1)
                if 2 <= u <= U and u % 2 == 0:
                    plain_row(nc, k, act, u // 2 - 1)
                if u < U and u % BATCH == BATCH - 1:
                    logarithms(u // BATCH)
            x3_row(U - 1)

        @block.vector
        def _(dve):
            def softplus(n):
                nc.vector.tensor_scalar(pos[:, :, :], outT[n % 3][:, :, 0:B], 0.0, None, ALU.max
                                        ).then_inc(pos_done, 1)
                dve.wait_ge(pos_done, n + 1)
                nc.vector.scalar_tensor_tensor(out=outT[n % 3][:, :, 0:B], in0=logs[:, :, :], scalar=-LOG2,
                                               in1=pos[:, :, :], op0=ALU.add, op1=ALU.add).then_inc(ssp_done, 1)
                dve.wait_ge(ssp_done, n + 1)

            def add(u):
                b = u % 2
                x2, inv = rows_of(u), float(B) ** -0.5
                dve.wait_ge(second_done, u + 1)
                if u >= 2:
                    dve.wait_ge(x3_done, u - 1)
                nc.vector.scalar_tensor_tensor(out=y[b][:, 0:B], in0=p_R[b][:, 0:B], scalar=inv,
                                               in1=x2[:, 0:B], op0=ALU.mult, op1=ALU.add).then_inc(y_s, 1)
                nc.vector.scalar_tensor_tensor(
                    out=y[b][:, B:D].rearrange("p (d c) -> p c d", c=3),
                    in0=p_R[b][:, B:D].rearrange("p (c d) -> p c d", c=3), scalar=inv,
                    in1=x2[:, B:D].rearrange("p (d c) -> p c d", c=3), op0=ALU.mult, op1=ALU.add
                    ).then_inc(y_done, 1)

            def statistics(u):
                dve.wait_ge(y_s, u + 1)
                dve.wait_ge(y_done, u + 1)
                nc.vector.bn_stats(stats[u % 2][:, :], y[u % 2][:, :]).then_inc(st, 1)

            def moments(u):
                dve.wait_ge(st, u + 1)
                if u >= 2:
                    dve.wait_ge(sc, 3 * u - 3)
                nc.vector.bn_aggr(mv[u % 2][:, :], stats[u % 2][:, :]).then_inc(mv_done, 1)

            for u in range(U + LAG):
                if u % BATCH == 1 and 1 <= u // BATCH <= NB:
                    n = u // BATCH - 1
                    dve.wait_ge(act_steps, 3 * n + 3)
                    softplus(n)
                if u >= LAG:
                    add(u - LAG)
                    statistics(u - LAG)
                    moments(u - LAG)
                if u < U and u % 2 == 0:
                    plain_shift(nc, k, nc.vector, u // 2)
                    plain_norm(nc, k, dve, u // 2)



def scores_phase(nc, k):
    with phase(nc, "s_") as (sb, ps, sem), ExitStack() as ctx:
        T = EDGE_TILES
        PLAIN = T
        srcT = [sb(f"srcT{i}", [P, KB, P]) for i in range(2)]
        q = [sb(f"q{i}", [P, D]) for i in range(2)]
        prod = sb("prod", [P, D])
        diag = sb("diag", [HEADS, HEADS, P])
        away = [sb(f"away{i}", [P, P]) for i in range(2)]
        cand = sb("cand", [P, HEADS, P])
        tile_max, known = ([sb(f"{n}{i}", [P, HEADS]) for i in range(2)] for n in ("tile_max", "known"))
        p_T = [ps(f"p_T{i}", [P, D]) for i in range(2)]
        p_q, p_k, p_w = ps("p_q", [P, D]), ps("p_k", [P, D]), ps("p_w", [HEADS, P])
        p_all = ps("p_all", [P, HEADS, P])
        w_in, known_in, max_gone = sem("w_in"), sem("known_in"), sem("max_gone")
        turned, turned_out, q_done, k_done, q_out, prod_done, aw_done, aw_turned, diag_done, spread = (
            sem(n) for n in ("turned", "turned_out", "q_done", "k_done", "q_out", "prod", "aw", "aw_turned", "diag", "spread"))
        away_done, cand_done, tile_max_done, merged = (sem(n) for n in ("away", "cand", "tile_max", "merged"))

        block = ctx.enter_context(nc.Block())

        @block.sync
        def _(sp):
            sp.dma_start(k.wv[:, :, :], k.L3_W[:, 2 * D:3 * D].rearrange("(c p) n -> p c n", p=P)).then_inc(w_in, 16)
            plain_transfers(nc, k, sp, PLAIN, PLAIN + 2 * T)
            sp.wait_ge(w_in, 16)

        @block.tensor
        def _(pe):
            def turn(t):
                for s, rows in enumerate((k.src_rows_sb, k.dst_rows_sb)):
                    if t >= 1:
                        pe.wait_ge(turned_out, 2 * t - 1 + s)
                    for c in range(KB):
                        last = nc.tensor.transpose(p_T[s][:, c * P:(c + 1) * P], rows[:, t, c * P:(c + 1) * P],
                                                   k.ident[:, :])
                    last.then_inc(turned, 1)

            def scores(t):
                pe.wait_ge(aw_done, t + 1)
                if t:
                    pe.wait_ge(diag_done, t)
                nc.tensor.transpose(p_w[:, :], k.scores[:, t, :], k.ident[:, :]).then_inc(aw_turned, 1)

            def spread_scores(t):
                pe.wait_ge(diag_done, t + 1)
                if t:
                    pe.wait_ge(cand_done, t)
                for half in range(2):
                    hs = slice(half * HEADS // 2, (half + 1) * HEADS // 2)
                    last = nc.tensor.matmul(p_all[:, hs, :], k.ones[0:HEADS, :], diag[:, hs, :], start=True, stop=True)
                last.then_inc(spread, 1)

            turn(0)
            pe.wait_ge(k.wqk_in, 16)
            for t in range(T + 1):
                if t < T:
                    pe.wait_ge(turned_out, 2 * t + 2)
                    if t:
                        pe.wait_ge(q_out, t)
                    for c in range(KB):
                        last = nc.tensor.matmul(p_q[:, :], srcT[t % 2][:, c, :], k.wqk[:, c, 0:D],
                                                start=(c == 0), stop=(c == KB - 1))
                    last.then_inc(q_done, 1)
                if t:
                    scores(t - 1)
                if t < T:
                    if t + 1 < T:
                        turn(t + 1)
                    if t:
                        pe.wait_ge(prod_done, t)
                    for c in range(KB):
                        last = nc.tensor.matmul(p_k[:, :], k.dst_rows_sb[:, t, c * P:(c + 1) * P], k.wqk[:, c, D:2 * D],
                                                start=(c == 0), stop=(c == KB - 1))
                    last.then_inc(k_done, 1)
                if t:
                    spread_scores(t - 1)

        @block.scalar
        def _(act):
            def turn_out(t):
                act.wait_ge(turned, 2 * t + 1)
                if t >= 2:
                    act.wait_ge(q_done, t - 1)
                nc.scalar.activation(srcT[t % 2][:, :, :], p_T[0][:, :].rearrange("p (c n) -> p c n", c=KB), ACT.Copy
                                     ).then_inc(turned_out, 1)
                act.wait_ge(turned, 2 * t + 2)
                nc.scalar.activation(k.dst_rows_sb[:, t, :], p_T[1][:, :], ACT.Copy).then_inc(turned_out, 1)

            turn_out(0)
            for t in range(T):
                if t >= 2:
                    act.wait_ge(cand_done, t - 1)
                same = k.same_src[:, t, :] if t < T - 1 else k.same_src_last[:, :]
                nc.scalar.activation(away[t % 2][:, :], same, ACT.Copy, bias=-BIG, scale=BIG).then_inc(away_done, 1)
                act.wait_ge(q_done, t + 1)
                if t >= 2:
                    act.wait_ge(prod_done, t - 1)
                nc.scalar.activation(q[t % 2][:, :], p_q[:, :], ACT.Copy, scale=float(HD) ** -0.5).then_inc(q_out, 1)
                if t + 1 < T:
                    turn_out(t + 1)
                if t >= 2:
                    plain_row(nc, k, act, PLAIN + 2 * t - 4)
                    plain_row(nc, k, act, PLAIN + 2 * t - 3)
            for i in range(PLAIN + 2 * T - 4, PLAIN + 2 * T):
                plain_row(nc, k, act, i)

        @block.vector
        def _(dve):
            def merge(t):
                dve.wait_ge(known_in, 16 * (t + 1))
                nc.vector.tensor_tensor(known[t % 2][:, :], known[t % 2][:, :], tile_max[t % 2][:, :], ALU.max
                                        ).then_inc(merged, 1)

            def tile_maximum(t):
                dve.wait_ge(spread, t + 1)
                dve.wait_ge(away_done, t + 1)
                if t:
                    dve.wait_ge(tile_max_done, t)
                nc.vector.tensor_tensor(cand[:, :, :], p_all[:, :, :],
                                        away[t % 2][:, :].rearrange("p (a e) -> p a e", a=1)
                                        .to_broadcast([P, HEADS, P]), ALU.add).then_inc(cand_done, 1)
                dve.wait_ge(cand_done, t + 1)
                if t >= 2:
                    dve.wait_ge(merged, t - 1)
                nc.vector.tensor_reduce(tile_max[t % 2][:, :], cand[:, :, :], AX_X, ALU.max).then_inc(tile_max_done, 1)
                dve.wait_ge(tile_max_done, t + 1)

            for t in range(T + 1):
                if t < T:
                    dve.wait_ge(k_done, t + 1)
                    dve.wait_ge(q_out, t + 1)
                    if t:
                        dve.wait_ge(aw_done, t)
                    nc.vector.tensor_tensor(prod[:, :], p_k[:, :], q[t % 2][:, :], ALU.mult).then_inc(prod_done, 1)
                    dve.wait_ge(prod_done, t + 1)
                    nc.vector.tensor_reduce(k.scores[:, t, :], prod[:, :].rearrange("p (h f) -> p h f", h=HEADS), AX_X,
                                            ALU.add).then_inc(aw_done, 1)
                if t:
                    tile_maximum(t - 1)
                    merge(t - 1)
                if t < T:
                    dve.wait_ge(aw_turned, t + 1)
                    if t:
                        dve.wait_ge(spread, t)
                    nc.vector.tensor_tensor(
                        diag[:, :, :], p_w[:, :].rearrange("h (a e) -> h a e", a=1).to_broadcast([HEADS, HEADS, P]),
                        k.ident[0:HEADS, 0:HEADS].rearrange("h (g a) -> h g a", a=1).to_broadcast([HEADS, HEADS, P]),
                        ALU.mult).then_inc(diag_done, 1)
                    plain_norm(nc, k, dve, PLAIN + 2 * t, PLAIN + 2 * t + 1)

        @block.gpsimd
        def _(pool):
            def scale_and_shift(t):
                for i in (PLAIN + 2 * t, PLAIN + 2 * t + 1):
                    plain_scale(nc, k, pool, i)
                    plain_shift(nc, k, nc.gpsimd, i)

            scale_and_shift(0)
            for t in range(T):
                if t:
                    plain_row_scale(nc, k, pool, PLAIN + 2 * t - 2)
                    plain_row_scale(nc, k, pool, PLAIN + 2 * t - 1)
                    pool.wait_ge(max_gone, 16 * t)
                pool.indirect_dma_start(known[t % 2][:, :], None, k.max3[:, :], at_rows(k.index[:, 0, t:t + 1])
                                        ).then_inc(known_in, 16)
                if t + 1 < T:
                    scale_and_shift(t + 1)
                pool.wait_ge(merged, t + 1)
                pool.indirect_dma_start(k.max3[:, :], at_rows(k.unique[:, 0, t:t + 1]), known[t % 2][:, :], None
                                        ).then_inc(max_gone, 16)
            plain_row_scale(nc, k, pool, PLAIN + 2 * T - 2)
            plain_row_scale(nc, k, pool, PLAIN + 2 * T - 1)
            pool.wait_ge(max_gone, 16 * T)


def values_phase(nc, k):
    with phase(nc, "v_") as (sb, ps, sem), ExitStack() as ctx:
        T = EDGE_TILES
        top = sb("top", [P, T, HEADS])
        weight = sb("weight", [P, T, HEADS])
        both = [sb(f"both{i}", [P, ATT]) for i in range(2)]
        tile_sum = [sb(f"tile_sum{i}", [P, ATT]) for i in range(2)]
        PLAIN = 3 * T
        AHEAD = 4
        p_v, p_S, p_W = ([ps(f"p_{n}{i}", [P, D]) for i in range(2)] for n in "vSW")
        top_in = [sem(f"top_in{i}") for i in range(4)]
        v_done, less, weighed, weights_in, both_done, s_done, s_out, scattered = (
            sem(n) for n in ("done", "less", "weighed", "weights_in", "both", "s_done", "s_out", "scattered"))
        block = ctx.enter_context(nc.Block())

        @block.sync
        def _(sp):
            plain_transfers(nc, k, sp, PLAIN, PLAIN + T)
            for i in range(PLAIN + T - PLAIN_BUFS, PLAIN + T):
                plain_store(nc, k, sp, i)
            for b in range(PLAIN_BUFS):
                sp.wait_ge(k.plain_gone[b], 16 * len(range(b, NODE_TILES, PLAIN_BUFS)))

        @block.gpsimd
        def _(pool):
            def gather(t):
                if t >= 4:
                    pool.wait_ge(top_in[t % 4], 16 * (t // 4))
                pool.indirect_dma_start(top[:, t, :], None, k.max3[:, :], at_rows(k.index[:, 0, t:t + 1])
                                        ).then_inc(top_in[t % 4], 16)

            for t in range(AHEAD + 2):
                gather(t)
            for t in range(T):
                plain_scale(nc, k, pool, PLAIN + t)
                if t:
                    plain_row_scale(nc, k, pool, PLAIN + t - 1)
                pool.wait_ge(s_out, 2 * t + 2)
                if t:
                    pool.wait_ge(scattered, 16 * t)
                pool.indirect_dma_start(k.sum3[:, :], at_rows(k.unique[:, 0, t:t + 1]), tile_sum[t % 2][:, :], None,
                                        compute_op=ALU.add).then_inc(scattered, 16)
                if t + AHEAD + 2 < T:
                    gather(t + AHEAD + 2)
            plain_row_scale(nc, k, pool, PLAIN + T - 1)
            pool.wait_ge(scattered, 16 * T)

        @block.tensor
        def _(pe):
            def tile_sums(t):
                pe.wait_ge(both_done, t + 1)
                pe.wait_ge(weights_in, t + 1)
                if t >= 2:
                    pe.wait_ge(s_out, 2 * t - 2)
                nc.tensor.matmul(p_S[t % 2][:, :], k.same_src[:, t, :], both[t % 2][:, 0:D], start=True, stop=True)
                nc.tensor.matmul(p_W[t % 2][:, 0:HEADS], k.same_src[:, t, :], both[t % 2][:, D:ATT], start=True,
                                 stop=True).then_inc(s_done, 1)

            for t in range(T):
                if t >= 2:
                    pe.wait_ge(both_done, t - 1)
                for c in range(KB):
                    last = nc.tensor.matmul(p_v[t % 2][:, :], k.dst_rows_sb[:, t, c * P:(c + 1) * P], k.wv[:, c, :],
                                            start=(c == 0), stop=(c == KB - 1))
                last.then_inc(v_done, 1)
                if t:
                    tile_sums(t - 1)
            tile_sums(T - 1)

        @block.vector
        def _(dve):
            def subtract_top(t):
                dve.wait_ge(top_in[t % 4], 16 * (t // 4 + 1))
                nc.vector.tensor_tensor(top[:, t, :], k.scores[:, t, :], top[:, t, :], ALU.subtract).then_inc(less, 1)

            for t in range(AHEAD):
                subtract_top(t)
            for t in range(T):
                if t + AHEAD < T:
                    subtract_top(t + AHEAD)
                dve.wait_ge(v_done, t + 1)
                dve.wait_ge(weighed, t + 1)
                if t >= 2:
                    dve.wait_ge(s_done, t - 1)
                nc.vector.tensor_copy(both[t % 2][:, D:ATT], weight[:, t, :]).then_inc(weights_in, 1)
                nc.vector.tensor_tensor(
                    both[t % 2][:, 0:D].rearrange("p (h f) -> p h f", h=HEADS),
                    p_v[t % 2][:, :].rearrange("p (h f) -> p h f", h=HEADS),
                    weight[:, t, :].rearrange("p (h a) -> p h a", a=1).to_broadcast([P, HEADS, HD]), ALU.mult
                    ).then_inc(both_done, 1)
                plain_shift(nc, k, nc.vector, PLAIN + t)
                plain_norm(nc, k, dve, PLAIN + t)

        @block.scalar
        def _(act):
            def weigh(t):
                act.wait_ge(less, t + 1)
                nc.scalar.activation(weight[:, t, :], top[:, t, :], ACT.Exp).then_inc(weighed, 1)

            for t in range(AHEAD):
                weigh(t)
            for t in range(T):
                if t + AHEAD < T:
                    weigh(t + AHEAD)
                act.wait_ge(s_done, t + 1)
                if t >= 2:
                    act.wait_ge(scattered, 16 * (t - 1))
                nc.scalar.activation(tile_sum[t % 2][:, 0:D], p_S[t % 2][:, :], ACT.Copy).then_inc(s_out, 1)
                nc.scalar.activation(tile_sum[t % 2][:, D:ATT], p_W[t % 2][:, 0:HEADS], ACT.Copy).then_inc(s_out, 1)
                if t:
                    plain_row(nc, k, act, PLAIN + t - 1)
            plain_row(nc, k, act, PLAIN + T - 1)


def attended_rows_phase(nc, k):
    with phase(nc, "o_") as (sb, ps, sem), ExitStack() as ctx:
        T = EDGE_TILES
        sums = [sb(f"sums{i}", [P, ATT]) for i in range(4)]
        inv = [sb(f"inv{i}", [P, HEADS]) for i in range(2)]
        y, out = ([sb(f"{n}{i}", [P, D]) for i in range(2)] for n in ("y", "out"))
        stats, mv, small = ([sb(f"{n}{i}", [P, w]) for i in range(2)] for n, w in (("stats", 6), ("mv", 2), ("small", 4)))
        sums_in = [sem(f"sums_in{i}") for i in range(4)]
        inv_done, att, y_done, st, mv_done, sc, out_done, gone = (
            sem(n) for n in ("inv", "att", "y", "st", "mv", "sc", "out", "gone"))
        block = ctx.enter_context(nc.Block())

        @block.gpsimd
        def _(pool):
            def gather(t):
                if t >= 4:
                    pool.wait_ge(att, t - 3)
                pool.indirect_dma_start(sums[t % 4][:, :], None, k.sum3[:, :], at_rows(k.index[:, 0, t:t + 1])
                                        ).then_inc(sums_in[t % 4], 16)

            for t in range(3):
                gather(t)
            for t in range(T + 2):
                if t + 3 < T:
                    gather(t + 3)
                if t < T:
                    b = t % 2
                    pool.wait_ge(mv_done, t + 1)
                    if t >= 2:
                        pool.wait_ge(out_done, t - 1)
                    row_scale(pool, k, mv[b][:, 1:2], mv[b][:, 0:1], small[b][:, 0:1], small[b][:, 1:2],
                              small[b][:, 2:3], sc, 3 * t)
                if 0 <= t - 1 < T:
                    pool.wait_ge(out_done, t)
                    if t >= 2:
                        pool.wait_ge(gone, 16 * (t - 1))
                    pool.indirect_dma_start(k.out[:, :], at_rows(k.unique[:, 0, t - 1:t]), out[(t - 1) % 2][:, :], None
                                            ).then_inc(gone, 16)
            pool.wait_ge(gone, 16 * T)

        @block.vector
        def _(dve):
            for t in range(T):
                b = t % 2
                dve.wait_ge(sums_in[t % 4], 16 * (t // 4 + 1))
                if t >= 2:
                    dve.wait_ge(att, t - 1)
                nc.vector.reciprocal(inv[b][:, :], sums[t % 4][:, D:ATT]).then_inc(inv_done, 1)
                dve.wait_ge(inv_done, t + 1)
                if t >= 2:
                    dve.wait_ge(out_done, t - 1)
                nc.vector.tensor_tensor(
                    y[b][:, :].rearrange("p (h f) -> p h f", h=HEADS),
                    sums[t % 4][:, 0:D].rearrange("p (h f) -> p h f", h=HEADS),
                    inv[b][:, :].rearrange("p (h a) -> p h a", a=1).to_broadcast([P, HEADS, HD]), ALU.mult
                    ).then_inc(att, 1)
                dve.wait_ge(att, t + 1)
                nc.vector.tensor_tensor(y[b][:, :], y[b][:, :], k.src_rows_sb[:, t, :], ALU.add).then_inc(y_done, 1)
                dve.wait_ge(y_done, t + 1)
                nc.vector.bn_stats(stats[b][:, :], y[b][:, :]).then_inc(st, 1)
                dve.wait_ge(st, t + 1)
                if t >= 2:
                    dve.wait_ge(sc, 3 * t - 3)
                nc.vector.bn_aggr(mv[b][:, :], stats[b][:, :]).then_inc(mv_done, 1)

        @block.scalar
        def _(act):
            for t in range(T):
                b = t % 2
                act.wait_ge(sc, 3 * t + 3)
                if t >= 2:
                    act.wait_ge(gone, 16 * (t - 1))
                nc.scalar.activation(out[b][:, :], y[b][:, :], ACT.Identity, bias=small[b][:, 2:3],
                                     scale=small[b][:, 1:2]).then_inc(out_done, 1)


TABLES = [("sum0", D), ("x1", D), ("p", D), ("sum2", 8 * F), ("sum3", ATT), ("max3", HEADS)]
PASSED = ["L0_gnn_W1", "L0_gnn_b1", "L0_gnn_W2", "L0_gnn_b2", "L0_gnn_W3", "L0_gnn_b3", "L0_gnn_W4", "L0_gnn_b4",
          "L0_gnn_gamma", "L0_gnn_beta", "L1_gnn_W_l", "L1_gnn_b_l", "L1_gnn_W_r", "L1_gnn_gamma", "L1_gnn_beta",
          "L2_gnn_w_in2f_s", "L2_gnn_w_in2f_v", "L2_gnn_W1", "L2_gnn_b1", "L2_gnn_W2", "L2_gnn_b2",
          "L2_gnn_w_f2o1_s", "L2_gnn_w_f2o1_v", "L2_gnn_w_f2o2_s", "L2_gnn_w_f2o2_v", "L3_gnn_W"]
DEBUG = 0


def build(nc, args, out, debug=None):
    k = Shared()
    k.nc, k.out = nc, out
    k.x = args["x"]
    k.xT = args["xT"]
    k.src_cols = args["src_cols"]
    k.dst_cols = args["dst_cols"]
    k.src_rows = args["src_rows"]
    k.dst_rows = args["dst_rows"]
    k.f64T = args["edge_attr_64T"]
    k.f20T = args["edge_attr_20T"]
    k.y4 = args["edge_attr_4t"]
    k.cut = args["edge_weight_t"]
    k.L0_W1 = args["L0_gnn_W1"]
    k.L0_b1 = args["L0_gnn_b1"]
    k.L0_W2 = args["L0_gnn_W2"]
    k.L0_b2 = args["L0_gnn_b2"]
    k.L0_W3 = args["L0_gnn_W3"]
    k.L0_b3 = args["L0_gnn_b3"]
    k.L0_W4 = args["L0_gnn_W4"]
    k.L0_b4 = args["L0_gnn_b4"]
    k.L0_gamma = args["L0_gnn_gamma"]
    k.L0_beta = args["L0_gnn_beta"]
    k.L1_Wl = args["L1_gnn_W_l"]
    k.L1_bl = args["L1_gnn_b_l"]
    k.L1_Wr = args["L1_gnn_W_r"]
    k.L1_gamma = args["L1_gnn_gamma"]
    k.L1_beta = args["L1_gnn_beta"]
    k.L2_ws = args["L2_gnn_w_in2f_s"]
    k.L2_wv = args["L2_gnn_w_in2f_v"]
    k.L2_W1 = args["L2_gnn_W1"]
    k.L2_b1 = args["L2_gnn_b1"]
    k.L2_W2 = args["L2_gnn_W2"]
    k.L2_b2 = args["L2_gnn_b2"]
    k.L2_o1s = args["L2_gnn_w_f2o1_s"]
    k.L2_o1v = args["L2_gnn_w_f2o1_v"]
    k.L2_o2s = args["L2_gnn_w_f2o2_s"]
    k.L2_o2v = args["L2_gnn_w_f2o2_v"]
    k.L3_W = args["L3_gnn_W"]
    kinds = debug or {}
    k.sum0, k.x1, k.p, k.sum2, k.sum3, k.max3 = (
        kinds.get(name) if name in kinds else nc.dram_tensor(name, [ROWS, width], F32).ap() for name, width in TABLES)
    with ExitStack() as ctx:
        ctx.enter_context(nc.allow_non_contiguous_dma(reason="bias columns and strided weights"))
        sb = lambda name, shape, dt=F32: ctx.enter_context(nc.sbuf_tensor(name, shape, dt))
        sem = lambda name: ctx.enter_context(nc.semaphore(name))
        k.ident, k.ones, k.minus_half = sb("ident", [P, P]), sb("ones", [P, P]), sb("minus_half", [P, 4])
        k.index, k.unique = sb("index", [P, 2, EDGE_TILES], I32), sb("unique", [P, 2, EDGE_TILES], I32)
        k.inv_degree, k.share, k.minus_share = (
            sb(n, [P, EDGE_TILES]) for n in ("inv_degree", "share", "minus_share"))
        k.same_src, k.same_dst = sb("same_src", [P, EDGE_TILES, P]), sb("same_dst", [P, EDGE_TILES, P])
        k.same_src_last = sb("same_src_last", [P, P])
        k.filters = sb("filters", [P, EDGE_TILES, 8, F])
        k.filters_done, k.w3a_in, k.acc_zero, k.half_set, k.passed_dve, k.passed_pool = (
            sem(n) for n in ("filters_done", "w3a_in", "acc_zero", "half_set", "passed_dve", "passed_pool"))
        k.column_acc = sb("column_acc", [P, 2, D])
        with nc.sbuf_tensor("w3a", [P, KB, D], F32) as w3a:
            k.w3a = w3a
            message_phase(nc, k)
            dense_phase(nc, k)
        k.bn_scale, k.bn_shift = sb("bn_scale", [P, D]), sb("bn_shift", [P, D])
        k.src_rows_sb, k.dst_rows_sb = sb("src_rows_sb", [P, EDGE_TILES, D]), sb("dst_rows_sb", [P, EDGE_TILES, D])
        k.scores = sb("scores", [P, EDGE_TILES, HEADS])
        aggregate_phase(nc, k)
        edge_rows_phase(nc, k)
        k.plain_stats, k.plain_mv = (
            [sb(f"plain_{n}{i}", [P, w]) for i in range(2)] for n, w in (("stats", 6), ("mv", 2)))
        k.plain_p_rows, k.plain_x1_rows, k.plain_y_rows, k.plain_small = (
            [sb(f"plain_{n}{i}", [P, w]) for i in range(PLAIN_BUFS)]
            for n, w in (("p", D), ("x1", D), ("y", D), ("small", 4)))
        k.plain_p_in, k.plain_x1_in, k.plain_gone = (
            [sem(f"plain_{n}{i}") for i in range(PLAIN_BUFS)] for n in ("p_in", "x1_in", "gone"))
        k.plain_scaled, k.plain_shifted, k.plain_leaky, k.plain_y, k.plain_st, k.plain_mv_done, k.plain_sc, k.plain_out = (
            sem("plain_" + n) for n in ("scaled", "shifted", "leaky", "y_done", "st", "mv_done", "sc", "out"))
        k.wqk = k.filters[:, :, :, :].rearrange("p t c f -> p (t c f)")[:, 0:KB * 2 * D].rearrange(
            "p (c n) -> p c n", c=KB)
        k.wqk_in = sem("wqk_in")
        equivariant_phase(nc, k)
        k.wv = sb("wv", [P, KB, D])
        scores_phase(nc, k)
        values_phase(nc, k)
        attended_rows_phase(nc, k)


def kernel(**inputs):
    import concourse.bacc as _bacc
    from concourse.bass_utils import run_bass_kernel_spmd as _run

    a = {n: np.asarray(v) for n, v in inputs.items()}

    def edges(v):
        return np.concatenate([v[:(EDGE_TILES - 1) * P], v[LAST_START:]])

    x = np.zeros((ROWS, D), a["x"].dtype)
    x[:N] = a["x"]
    arrays = {
        "x": x,
        "xT": np.ascontiguousarray(x.reshape(NODE_TILES, P, KB, P).transpose(0, 3, 2, 1)).reshape(ROWS, D),
        "edge_attr_64T": np.ascontiguousarray(edges(a["edge_attr_64"]).T),
        "edge_attr_20T": np.ascontiguousarray(edges(a["edge_attr_20"]).T),
        "edge_attr_4t": np.ascontiguousarray(edges(a["edge_attr_4"]).reshape(EDGE_TILES, P, 4).transpose(1, 0, 2)),
        "edge_weight_t": np.ascontiguousarray(edges(a["edge_weight"]).reshape(EDGE_TILES, P).T),
    }
    for n in ("src", "dst"):
        arrays[f"{n}_rows"] = a[n].reshape(1, -1)
        arrays[f"{n}_cols"] = np.ascontiguousarray(edges(a[n]).reshape(EDGE_TILES, P).T)
    for n in PASSED:
        arrays[n] = np.ascontiguousarray(a[n])

    nc = _bacc.Bacc("TRN2", target_bir_lowering=False, num_devices=1)
    args = {n: nc.dram_tensor(f"in_{n}", v.shape, mybir.dt.from_np(v.dtype), kind="ExternalInput").ap()
            for n, v in arrays.items()}
    out = nc.dram_tensor("out_rows", [ROWS, D], F32, kind="ExternalOutput").ap()
    debug = {n: nc.dram_tensor(n, [ROWS, w], F32, kind="ExternalOutput").ap() for n, w in TABLES} if DEBUG else None
    build(nc, args, out, debug)
    r = _run(nc, [{f"in_{n}": v for n, v in arrays.items()}], core_ids=[0])
    return r.results[0]["out_rows"][:N]
```
